# Optimizing a Trainium2 kernel written in Bass

```python
import numpy as np
import jax
import jax.numpy as jnp

def _softmax(x, axis=-1):
    return jax.nn.softmax(x, axis=axis)

def _gelu(x):
    return jax.nn.gelu(x, approximate=True)

def _silu(x):
    return jax.nn.silu(x)

def _sigmoid(x):
    return jax.nn.sigmoid(x)

def _layernorm(x, axis=-1, eps=1e-05):
    m = jnp.mean(x, axis=axis, keepdims=True)
    v = jnp.var(x, axis=axis, keepdims=True)
    return (x - m) / jnp.sqrt(v + eps)

def _scatter_add(tgt, idx, src, axis=0):
    return tgt.at[idx].add(src)

def _segment_sum(src, seg, n):
    return jax.ops.segment_sum(src, seg, n)
kernel_name = 'mk_sandwich_d2_jaxref_r4_948bbc'

def setup_inputs(seed: int=0):
    np.random.seed(seed)
    _w = jnp.asarray

    def _L0_attn_setup():
        import jax, jax.numpy as jnp
        import numpy as np
        B, S, D, H = (4, 512, 256, 16)
        DH = D // H
        key = jax.random.key(seed)
        ks = jax.random.split(key, 5)
        std = 1.0 / np.sqrt(D)
        return {'x': jax.random.normal(ks[0], (B, S, D), dtype=jnp.float32), 'mask': jnp.ones((S, S), dtype=bool), 'Wq': jax.random.normal(ks[1], (D, D), dtype=jnp.float32) * std, 'Wk': jax.random.normal(ks[2], (D, D), dtype=jnp.float32) * std, 'Wv': jax.random.normal(ks[3], (D, D), dtype=jnp.float32) * std, 'Wout': jax.random.normal(ks[4], (D, D), dtype=jnp.float32) * std}
    _L0_attn_in = _L0_attn_setup()

    def _L0_ffn_setup():
        import jax, jax.numpy as jnp
        import numpy as np
        NUM_TRUE = 8
        NUM_NULL = 2
        NUM_EXPERTS = NUM_TRUE + NUM_NULL
        TOP_K = 2
        key = jax.random.key(seed)
        k0, k1, k2 = jax.random.split(key, 3)
        B, S, D = (4, 512, 256)
        inputs = jax.random.normal(k0, (B, S, D), dtype=jnp.float32)
        gate_w = jax.random.normal(k1, (NUM_EXPERTS, D), dtype=jnp.float32) * 0.02
        gate_b = jnp.zeros((NUM_EXPERTS,), dtype=jnp.float32)
        expert_w = jax.random.normal(k2, (NUM_TRUE, D, D), dtype=jnp.float32) * 0.02
        expert_b = jnp.zeros((NUM_TRUE, D), dtype=jnp.float32)
        return {'inputs': inputs, 'gate_w': gate_w, 'gate_b': gate_b, 'expert_w': expert_w, 'expert_b': expert_b}
    _L0_ffn_in = _L0_ffn_setup()

    def _L1_attn_setup():
        import jax, jax.numpy as jnp
        import numpy as np
        DIM_IN, DIM_K, DIM_V, NH = (256, 256, 256, 16)
        DK, DV = (DIM_K // NH, DIM_V // NH)
        key = jax.random.key(seed)
        kx, kq, kk, kv = jax.random.split(key, 4)
        x = jax.random.normal(kx, (4, 512, DIM_IN), dtype=jnp.float32)
        Wq = jax.random.normal(kq, (DIM_K, DIM_IN), dtype=jnp.float32) / np.sqrt(DIM_IN)
        Wk = jax.random.normal(kk, (DK, DIM_IN), dtype=jnp.float32) / np.sqrt(DIM_IN)
        Wv = jax.random.normal(kv, (DV, DIM_IN), dtype=jnp.float32) / np.sqrt(DIM_IN)
        return {'x': x, 'Wq': Wq, 'Wk': Wk, 'Wv': Wv}
    _L1_attn_in = _L1_attn_setup()

    def _L1_ffn_setup():
        import jax, jax.numpy as jnp
        import numpy as np
        B, N, D = (4, 512, 256)
        SPARSITY = 0.01
        key = jax.random.key(seed)
        k1, k2, k3 = jax.random.split(key, 3)
        x = jax.random.normal(k1, (B, N, D), dtype=jnp.float32)
        spatial = jax.random.normal(k2, (D, D), dtype=jnp.float32) * 0.02
        freq = jnp.fft.fft(spatial, axis=-1)
        k = int(D * SPARSITY)
        mag = jnp.abs(freq)
        kth = jax.lax.top_k(mag, k)[0][:, -1:]
        w_sparse = jnp.where(mag >= kth, freq, 0.0 + 0j)
        bias = jax.random.normal(k3, (D,), dtype=jnp.float32) * 0.01
        return {'x': x, 'w_freq_real': jnp.real(w_sparse).astype(jnp.float32), 'w_freq_imag': jnp.imag(w_sparse).astype(jnp.float32), 'bias': bias}
    _L1_ffn_in = _L1_ffn_setup()
    _d = {'L0_attn_x': _L0_attn_in['x'], 'L0_attn_mask': _L0_attn_in['mask'], 'L0_attn_Wq': _L0_attn_in['Wq'], 'L0_attn_Wk': _L0_attn_in['Wk'], 'L0_attn_Wv': _L0_attn_in['Wv'], 'L0_attn_Wout': _L0_attn_in['Wout'], 'L0_ffn_gate_w': _L0_ffn_in['gate_w'], 'L0_ffn_gate_b': _L0_ffn_in['gate_b'], 'L0_ffn_expert_w': _L0_ffn_in['expert_w'], 'L0_ffn_expert_b': _L0_ffn_in['expert_b'], 'L1_attn_Wq': _L1_attn_in['Wq'], 'L1_attn_Wk': _L1_attn_in['Wk'], 'L1_attn_Wv': _L1_attn_in['Wv'], 'L1_ffn_w_freq_real': _L1_ffn_in['w_freq_real'], 'L1_ffn_w_freq_imag': _L1_ffn_in['w_freq_imag'], 'L1_ffn_bias': _L1_ffn_in['bias']}
    _x0 = _d['L0_attn_x']
    _d['L0_attn_x'] = jax.random.normal(jax.random.fold_in(jax.random.key(seed), 1), (4, 1024, 256), dtype=_x0.dtype)
    del _x0
    return _d

def reference(L0_attn_x, L0_attn_mask, L0_attn_Wq, L0_attn_Wk, L0_attn_Wv, L0_attn_Wout, L0_ffn_gate_w, L0_ffn_gate_b, L0_ffn_expert_w, L0_ffn_expert_b, L1_attn_Wq, L1_attn_Wk, L1_attn_Wv, L1_ffn_w_freq_real, L1_ffn_w_freq_imag, L1_ffn_bias):

    def _L0_attn_ref(x, mask, Wq, Wk, Wv, Wout):
        import jax, jax.numpy as jnp
        import numpy as np
        B, S, D, H = (4, 512, 256, 16)
        DH = D // H
        n, s, d = x.shape
        scale = 1.0 / np.sqrt(DH).astype(np.float32)
        q = (x @ Wq).reshape(n, s, H, DH)
        k = (x @ Wk).reshape(n, s, H, DH)
        v = (x @ Wv).reshape(n, s, H, DH)
        attn = jnp.einsum('nqhd,nkhd->nqkh', q, k) * scale
        attn = jax.nn.softmax(attn, axis=-2)
        z = jnp.einsum('nqkh,nkhd->nqhd', attn, v).reshape(n, s, d)
        z = jnp.einsum('nqd,de->nqe', z, Wout)
        return x + z

    def _L0_ffn_ref(inputs, gate_w, gate_b, expert_w, expert_b):
        import jax, jax.numpy as jnp
        import numpy as np
        NUM_TRUE = 8
        NUM_NULL = 2
        NUM_EXPERTS = NUM_TRUE + NUM_NULL
        TOP_K = 2
        D = inputs.shape[-1]
        x = inputs.reshape(-1, D)
        gate_logits = x @ gate_w.T + gate_b
        gate_probs = jax.nn.softmax(gate_logits, axis=-1)
        weights, selected = jax.lax.top_k(gate_probs, TOP_K)
        true_mask = selected < NUM_TRUE
        true_weights = weights * true_mask
        denom = true_weights.sum(axis=-1, keepdims=True)
        denom = jnp.where(denom > 0, denom, jnp.ones_like(denom))
        norm_w = (true_weights / denom).astype(x.dtype)
        one_hot = jax.nn.one_hot(selected, NUM_EXPERTS, dtype=norm_w.dtype)
        combine_w = jnp.einsum('tk,tke->te', norm_w, one_hot)[:, :NUM_TRUE]
        expert_out = jnp.einsum('td,edh->teh', x, expert_w) + expert_b[None, :, :]
        out = jnp.einsum('te,teh->th', combine_w, expert_out)
        return out.reshape(inputs.shape[:-1] + (out.shape[-1],))

    def _L1_attn_ref(x, Wq, Wk, Wv):
        import jax, jax.numpy as jnp
        import numpy as np
        DIM_IN, DIM_K, DIM_V, NH = (256, 256, 256, 16)
        DK, DV = (DIM_K // NH, DIM_V // NH)
        B, S, _ = x.shape
        scale = 1.0 / np.sqrt(DK)
        q = (x @ Wq.T).reshape(B, S, NH, DK).transpose(0, 2, 1, 3)
        k = x @ Wk.T
        v = x @ Wv.T
        dist = jnp.einsum('bhqd,bkd->bhqk', q, k) * scale
        dist = jax.nn.softmax(dist, axis=-1)
        att = jnp.einsum('bhqk,bkd->bhqd', dist, v)
        return att.transpose(0, 2, 1, 3).reshape(B, S, DIM_V)

    def _L1_ffn_ref(x, w_freq_real, w_freq_imag, bias):
        import jax, jax.numpy as jnp
        import numpy as np
        B, N, D = (4, 512, 256)
        SPARSITY = 0.01
        w = jax.lax.complex(w_freq_real, w_freq_imag)
        x_freq = jnp.fft.fft(x, axis=-1)
        y_freq = jnp.einsum('bnd,do->bno', x_freq, w)
        y = jnp.real(jnp.fft.ifft(y_freq, axis=-1))
        return y + bias
    x = L0_attn_x
    x = x + _layernorm(_L0_attn_ref(_layernorm(x, axis=-1), L0_attn_mask, L0_attn_Wq, L0_attn_Wk, L0_attn_Wv, L0_attn_Wout), axis=-1)
    x = x + _layernorm(_L0_ffn_ref(_layernorm(x, axis=-1), L0_ffn_gate_w, L0_ffn_gate_b, L0_ffn_expert_w, L0_ffn_expert_b), axis=-1)
    x = x + _layernorm(_L1_attn_ref(_layernorm(x, axis=-1), L1_attn_Wq, L1_attn_Wk, L1_attn_Wv), axis=-1)
    x = x + _layernorm(_L1_ffn_ref(_layernorm(x, axis=-1), L1_ffn_w_freq_real, L1_ffn_w_freq_imag, L1_ffn_bias), axis=-1)
    return x

_drawn_inputs = setup_inputs


def setup_inputs(seed=0):
    import zlib

    import numpy as np

    out = dict(_drawn_inputs(seed))
    spreads = {'L0_ffn_gate_b': (0.0, 0.1), 'L0_ffn_expert_b': (0.0, 0.1)}
    factors = {'L1_ffn_bias': 8.0}
    for name, (base, spread) in spreads.items():
        noise = np.random.default_rng([zlib.crc32(name.encode()), seed]).standard_normal(out[name].shape)
        drawn = base * np.exp(spread * noise) if base else spread * noise
        out[name] = jnp.asarray(drawn.astype(out[name].dtype))
    for name, factor in factors.items():
        out[name] = (out[name] * factor).astype(out[name].dtype)
    return out
```

```python
from contextlib import ExitStack

import numpy as np

import concourse.bass as bass
from concourse import mybir

F32 = mybir.dt.float32
BF16 = mybir.dt.bfloat16
U32 = mybir.dt.uint32
ALU = mybir.AluOpType
ACT = mybir.ActivationFunctionType
AX = mybir.AxisListType

P = 128
B, S, D, H = 4, 1024, 256, 16
DH = D // H
KC = D // P
TILES = B * S // P
CHUNK = 4
CHUNKS = TILES // CHUNK
CT = CHUNK * P
HG = 4
GROUPS = B * H // HG
GF = HG * DH
HALVES = 2 * GROUPS
HQ = S // 2
KT = S // P
QT = HQ // P
PARTS = 3
Q_PARTS = (0, 0, 0, 1, 1, 2)
K_PARTS = (0, 1, 2, 0, 1, 0)
ROWS = len(Q_PARTS) * DH
VW = 32
EXPERTS, NULLS = 8, 2
GATES = EXPERTS + NULLS
EPS = 1e-5
SCALE = DH ** -0.5

SCRATCH = 9216


def ge(engine, semaphore, value):
    if isinstance(value, int) and value <= 0:
        return
    engine.wait_ge(semaphore, value)


def ge_bare(engine, semaphore, value):
    if not isinstance(value, int):
        engine.lower_val(value)
        engine.wait_ge(semaphore, 1)
    engine.wait_ge(semaphore, value)


class Chain:

    def __init__(self, engine, semaphore):
        self.engine, self.semaphore, self.base, self.count = engine, semaphore, 0, 0

    def then(self, instruction, bare=False):
        instruction.then_inc(self.semaphore, 1)
        self.count += 1
        (ge_bare if bare else ge)(self.engine, self.semaphore, self.base + self.count)


class Memory:

    def __init__(self, nc, ctx):
        def sb(name, shape, dt=F32):
            return ctx.enter_context(nc.sbuf_tensor(name, shape, dt))

        self.x = sb("x_res", [P, TILES, D])
        self.z = sb("z_res", [P, GROUPS, KT, GF])
        self.v = sb("v_res", [P, GROUPS, KT, GF])
        self.mean = sb("mean_first", [P, TILES])
        self.rstd = sb("rstd_first", [P, TILES])
        self.q_stack = sb("q_stack", [P, 4, HG, HQ], BF16)
        self.k_stack = sb("k_stack", [P, 2, HG, S], BF16)
        self.v_group = sb("v_group", [P, 2, KT, HG, VW])
        self.scratch = sb("scratch", [P, SCRATCH])
        self.ident = sb("ident", [P, P])
        self.wq0 = sb("wq0", [P, KC, D])
        self.wk0 = sb("wk0", [P, KC, D])
        self.wv0 = sb("wv0", [P, KC, D])
        self.wout = sb("wout", [P, KC, D])
        self.wq1 = sb("wq1", [P, KC, D])
        self.wk1 = sb("wk1", [P, KC, DH])
        self.wv1 = sb("wv1", [P, KC, DH])
        self.gate_w = sb("gate_w_sb", [P, KC, GATES])
        self.gate_b = sb("gate_b_sb", [P, GATES])
        self.expert_w = sb("expert_w_sb", [P, KC, EXPERTS, D])
        self.expert_b = sb("expert_b_sb", [EXPERTS, D])
        self.bias = sb("bias_sb", [P, D])
        self.index = sb("index_row", [P, EXPERTS])
        self.fold = sb("fold", [P, KC, D])
        self.eps = sb("eps_col", [P, CHUNK])
        self.minus_half = sb("minus_half", [P, CHUNK])
        self.psum = ctx.enter_context(nc.psum_tensor("psum", [P, 8, 512], F32))


def setup(nc, m, io):
    with ExitStack() as ctx:
        def sem(name):
            return ctx.enter_context(nc.semaphore(name))

        x_loaded, w_loaded, dft_loaded = sem("x_loaded"), sem("w_loaded"), sem("dft_loaded")
        transforms, scaled, folded, fold_kept, presets = (
            sem("transforms"), sem("scaled"), sem("folded"), sem("fold_kept"), sem("presets"))
        W = KC * D
        dft = [m.scratch[:, i * W:(i + 1) * W].rearrange("p (c n) -> p c n", c=KC) for i in range(7)]
        cos, sin, minus_cos, w_real, w_imag, a_t, nb_t = dft

        def chunked(w):
            return w.rearrange("(c p) n -> p c n", p=P)

        block = ctx.enter_context(nc.Block())

        @block.sync
        def _(sp):
            for dst, name in ((cos, "dft_cos"), (sin, "dft_sin"), (minus_cos, "dft_minus_cos"),
                              (w_real, "w_real"), (w_imag, "w_imag")):
                sp.dma_start(dst, chunked(io[name])).then_inc(dft_loaded, 16)
            x_view = io["x"].rearrange("(t p) d -> p t d", p=P)
            for t in range(0, TILES, CHUNK):
                sp.dma_start(m.x[:, t:t + CHUNK, :], x_view[:, t:t + CHUNK, :]).then_inc(x_loaded, 16)
            sp.wait_ge(x_loaded, 16 * CHUNKS)

        @block.vector
        def _(dve):
            dve.memset(m.eps[:, :], EPS)
            dve.memset(m.minus_half[:, :], -0.5)
            dve.memset(m.v_group[:, :, :, :, :], 0.0).then_inc(presets, 1)
            dve.wait_ge(presets, 1)
            dve.memset(m.v_group[:, :, :, :, DH:DH + 1], 1.0)
            dve.memset(m.k_stack[ROWS:ROWS + PARTS, :, :, :], 1.0)

        @block.scalar
        def _(act):
            loads = [(m.ident[:, :], io["ident"]), (m.gate_b[:, :], io["gate_b"]), (m.bias[:, :], io["bias"]),
                     (m.index[:, :], io["index"]), (m.expert_b[:, :], io["expert_b"]),
                     (m.expert_w[:, :, :, :], io["expert_w"].rearrange("e (c p) n -> p c e n", p=P))]
            for dst, name in ((m.wq0, "wq0"), (m.wk0, "wk0"), (m.wv0, "wv0"), (m.wout, "wout"), (m.wq1, "wq1"),
                              (m.wk1, "wk1"), (m.wv1, "wv1"), (m.gate_w, "gate_w")):
                loads.append((dst[:, :, :], chunked(io[name])))
            n = 0
            for dst, src in loads:
                parts = [(dst[:, c], src[:, c]) for c in range(KC)] if len(src.shape) == 4 else [(dst, src)]
                for d, s in parts:
                    act.dma_start(d, s).then_inc(w_loaded, 16)
                    n += 1
            act.wait_ge(transforms, 1)
            act.activation(a_t, m.psum[:, 0, :].rearrange("p (c n) -> p c n", c=KC), ACT.Copy,
                           scale=1.0 / D).then_inc(scaled, 1)
            act.wait_ge(transforms, 2)
            act.activation(nb_t, m.psum[:, 1, :].rearrange("p (c n) -> p c n", c=KC), ACT.Copy,
                           scale=1.0 / D).then_inc(scaled, 1)
            act.wait_ge(folded, 1)
            act.copy(m.fold[:, :, :], m.psum[:, 2, :].rearrange("p (c n) -> p c n", c=KC)).then_inc(fold_kept, 1)
            act.wait_ge(fold_kept, 1)
            act.wait_ge(w_loaded, 16 * n)

        @block.tensor
        def _(pe):
            def product(bank, pairs):
                for j in range(KC):
                    for i, (left, right) in enumerate(pairs):
                        for k in range(KC):
                            last = pe.matmul(m.psum[:, bank, j * D:(j + 1) * D], left[:, k, j * P:(j + 1) * P],
                                             right[:, k, :], start=(i == 0 and k == 0),
                                             stop=(i == len(pairs) - 1 and k == KC - 1))
                return last

            pe.wait_ge(dft_loaded, 16 * 5)
            product(0, ((w_real, cos), (w_imag, sin))).then_inc(transforms, 1)
            product(1, ((w_real, sin), (w_imag, minus_cos))).then_inc(transforms, 1)
            pe.wait_ge(scaled, 2)
            product(2, ((a_t, cos), (nb_t, sin))).then_inc(folded, 1)


def projection(nc, m, layer, q_dram, k_dram):
    shared = layer == 1
    wq, wk, wv = (m.wq1, m.wk1, m.wv1) if shared else (m.wq0, m.wk0, m.wv0)
    KB = 1 if shared else KC
    KR = DH if shared else P
    VN = DH if shared else D
    XT_BANK, Q_BANK, K_BANK, V_BANK = 0, 2, 4, 6
    with ExitStack() as ctx:
        def sem(name):
            return ctx.enter_context(nc.semaphore(f"{name}_{layer}"))

        stats_ready, rstd_ready, xln_ready = sem("stats_ready"), sem("rstd_ready"), sem("xln_ready")
        xt_full, xt_ready = sem("xt_full"), sem("xt_ready")
        v_full, v_copied = sem("v_full"), sem("v_copied")
        full = [sem("q_full"), sem("k_full")]
        high = [sem("q_high"), sem("k_high")]
        rest = [sem("q_rest"), sem("k_rest")]
        middle = [sem("q_middle"), sem("k_middle")]
        low = [sem("q_low"), sem("k_low")]
        stored = [sem("q_stored"), sem("k_stored")]
        dve_steps, pool_steps = sem("dve_steps"), sem("pool_steps")

        def cut(start, words):
            return m.scratch[:, start:start + words]

        W = CHUNK * D
        xln = [cut(i * W, W).rearrange("p (t d) -> p t d", t=CHUNK) for i in range(2)]
        xt = [cut((2 + i) * W, W).rearrange("p (c t) -> p c t", c=KC) for i in range(2)]
        rests = [cut((4 + i) * W, W).rearrange("p (c t) -> p c t", c=KC) for i in range(2)]
        parts = [cut(6 * W + i * W * PARTS // 2, W * PARTS // 2).bitcast(BF16).rearrange(
            "p (s c t) -> p s c t", s=PARTS, c=KC) for i in range(2)]
        bn = ctx.enter_context(nc.sbuf_tensor(f"bn_{layer}", [P, CHUNK, 6], F32))
        mv = ctx.enter_context(nc.sbuf_tensor(f"mv_{layer}", [P, 2, CHUNK, 2], F32))
        var = ctx.enter_context(nc.sbuf_tensor(f"var_{layer}", [P, CHUNK], F32))
        rstd = ctx.enter_context(nc.sbuf_tensor(f"rstd_{layer}", [P, 2, CHUNK], F32))

        blocks, rows = (KC, KB), (P, KR)
        banks = (Q_BANK, K_BANK)

        def in_psum(i):
            return m.psum[0:rows[i], banks[i]:banks[i] + blocks[i], :]

        def loop(engine, chain, per_chunk, body):
            if chain:
                chain.base, chain.count = 0, 0
            start = chain.count if chain else 0
            body(0, -1)
            body(0, 0)
            after = chain.count if chain else 0
            with engine.Fori(0, CHUNKS // 2 - 1) as J:
                if chain:
                    chain.base, chain.count = J * (2 * per_chunk), after
                body(J, 1)
                body(J, 2)
                if chain:
                    assert chain.count == after + 2 * per_chunk, (chain.count, after, start)
            if chain:
                chain.base = (CHUNKS // 2 - 2) * 2 * per_chunk
            body(0, CHUNKS - 1)

        def at(J, u):
            return 2 * J + u, u % 2, J + u // 2, u % 2

        STORES = (16 * PARTS * KC * 2, 16 * PARTS * (1 if shared else KC * 2))

        block = ctx.enter_context(nc.Block())

        @block.sync
        def _(sp):
            def body(J, u):
                if u == -1:
                    return
                c, _, b, qh = at(J, u)
                for i, dram in enumerate((q_dram, k_dram)):
                    sp.wait_ge(low[i], c + 1)
                    for s in range(PARTS):
                        if i == 1 and shared:
                            sp.dma_start(dram[bass.ds(b, 1), s, :, qh * CT:(qh + 1) * CT].rearrange("o r t -> (o r) t"),
                                         parts[i][0:KR, s, 0, :]).then_inc(stored[i], 16)
                            continue
                        for blk in range(KC):
                            for hh in range(2):
                                g = b * (GROUPS // B) + blk * 2 + hh
                                sp.dma_start(
                                    dram[bass.ds(g, 1), s, :, qh * CT:(qh + 1) * CT].rearrange("o r t -> (o r) t"),
                                    parts[i][hh * GF:(hh + 1) * GF, s, blk, :]).then_inc(stored[i], 16)

            loop(sp, None, 0, body)
            sp.wait_ge(stored[0], STORES[0] * CHUNKS)
            sp.wait_ge(stored[1], STORES[1] * CHUNKS)

        @block.gpsimd
        def _(pool):
            chain = Chain(pool, pool_steps)

            def body(J, u):
                c, par, _, _ = at(J, u)
                if isinstance(J, int) and c + 1 >= CHUNKS:
                    return
                nxt = (u + 1) % 2
                pool.wait_ge(stats_ready, c + 2)
                chain.then(pool.tensor_tensor(var[:, :], mv[:, nxt, :, 1], m.eps[:, :], ALU.add))
                pool.tensor_tensor(rstd[:, nxt, :], var[:, :], m.minus_half[:, :], ALU.pow).then_inc(rstd_ready, 1)

            loop(pool, chain, 1, body)

        @block.vector
        def _(dve):
            chain = Chain(dve, dve_steps)

            def body(J, u):
                c, par, _, _ = at(J, u)
                nxt = (u + 1) % 2
                if not (isinstance(J, int) and c + 1 >= CHUNKS):
                    for t in range(CHUNK):
                        ins = dve.bn_stats(bn[:, t, :], m.x[:, bass.ds((c + 1) * CHUNK + t, 1), :])
                    chain.then(ins, bare=True)
                    for t in range(CHUNK):
                        ins = dve.bn_aggr(mv[:, nxt, t, :], bn[:, t, :])
                    ins.then_inc(stats_ready, 1)
                    dve.wait_ge(rstd_ready, c + 2)
                    ge(dve, xt_ready, c)
                    for t in range(CHUNK):
                        ins = dve.tensor_scalar(xln[nxt][:, t, :], m.x[:, bass.ds((c + 1) * CHUNK + t, 1), :],
                                                mv[:, nxt, t, 0:1], rstd[:, nxt, t:t + 1], ALU.subtract, ALU.mult)
                    ins.then_inc(xln_ready, 1)
                    if not shared:
                        dve.tensor_copy(m.mean[:, bass.ds((c + 1) * CHUNK, CHUNK)], mv[:, nxt, :, 0])
                        dve.tensor_copy(m.rstd[:, bass.ds((c + 1) * CHUNK, CHUNK)], rstd[:, nxt, :])
                if u == -1:
                    return
                for i in range(2):
                    r = slice(0, rows[i])
                    dve.wait_ge(high[i], c + 1)
                    dve.tensor_tensor(rests[i][r, 0:blocks[i], :], in_psum(i), parts[i][r, 0, 0:blocks[i], :],
                                      ALU.subtract).then_inc(rest[i], 1)
                    dve.wait_ge(middle[i], c + 1)
                    dve.tensor_tensor(parts[i][r, 2, 0:blocks[i], :], rests[i][r, 0:blocks[i], :],
                                      parts[i][r, 1, 0:blocks[i], :], ALU.subtract).then_inc(low[i], 1)

            loop(dve, chain, 1, body)

        @block.scalar
        def _(act):
            def take_high(i, c, r):
                act.wait_ge(full[i], c + 1)
                ge(act, stored[i], STORES[i] * c)
                act.copy(parts[i][r, 0, 0:blocks[i], :], in_psum(i)).then_inc(high[i], 1)

            def take_middle(i, c, r):
                act.wait_ge(rest[i], c + 1)
                act.copy(parts[i][r, 1, 0:blocks[i], :], rests[i][r, 0:blocks[i], :]).then_inc(middle[i], 1)

            def body(J, u):
                c, par, b, qh = at(J, u)
                nxt = (u + 1) % 2
                if u >= 0:
                    take_high(0, c, slice(0, rows[0]))
                    take_middle(0, c, slice(0, rows[0]))
                    take_high(1, c, slice(0, rows[1]))
                if not (isinstance(J, int) and c + 1 >= CHUNKS):
                    act.wait_ge(xt_full, c + 2)
                    ge(act, v_full, c)
                    act.copy(xt[nxt], m.psum[:, XT_BANK:XT_BANK + 2, :]).then_inc(xt_ready, 1)
                if u == -1:
                    return
                take_middle(1, c, slice(0, rows[1]))
                act.wait_ge(v_full, c + 1)
                v_new = m.psum[:, V_BANK:V_BANK + 2, :].rearrange("p b (t n) -> p (b t) n", n=D)
                for hg in range(GROUPS // B):
                    g = b * (GROUPS // B) + hg
                    dst = m.v[:, bass.ds(g, 1), qh * CHUNK:(qh + 1) * CHUNK, :].rearrange("p o t n -> p (o t) n")
                    if shared:
                        for t in range(CHUNK):
                            ins = act.copy(dst[:, t, :].rearrange("p (h d) -> p h d", h=HG),
                                           v_new[:, t, 0:DH].rearrange("p (o d) -> p o d", o=1).to_broadcast([P, HG, DH]))
                    else:
                        ins = act.copy(dst, v_new[:, :, hg * GF:(hg + 1) * GF])
                ins.then_inc(v_copied, 1)

            loop(act, None, 0, body)

        @block.tensor
        def _(pe):
            def body(J, u):
                c, par, _, _ = at(J, u)
                nxt = (u + 1) % 2
                if u >= 0:
                    pe.wait_ge(xt_ready, c + 1)
                    for i, w in enumerate((wq, wk)):
                        ge(pe, rest[i], c)
                        for blk in range(blocks[i]):
                            for k in range(KC):
                                ins = pe.matmul(m.psum[0:rows[i], banks[i] + blk, :],
                                                w[:, k, blk * P:blk * P + rows[i]], xt[par][:, k, :],
                                                start=(k == 0), stop=(k == KC - 1))
                        ins.then_inc(full[i], 1)
                if not (isinstance(J, int) and c + 1 >= CHUNKS):
                    pe.wait_ge(xln_ready, c + 2)
                    ge(pe, xt_ready, c + 1)
                    for t in range(CHUNK):
                        for k in range(KC):
                            ins = pe.transpose(m.psum[:, XT_BANK + k, t * P:(t + 1) * P],
                                               xln[nxt][:, t, k * P:(k + 1) * P], m.ident[:, :])
                    ins.then_inc(xt_full, 1)
                if u == -1:
                    return
                ge(pe, v_copied, c)
                for t in range(CHUNK):
                    for k in range(KC):
                        ins = pe.matmul(m.psum[:, V_BANK + t // 2, (t % 2) * D:(t % 2) * D + VN],
                                        xt[par][:, k, t * P:(t + 1) * P], wv[:, k, :],
                                        start=(k == 0), stop=(k == KC - 1))
                ins.then_inc(v_full, 1)

            loop(pe, None, 0, body)


def attention(nc, m, layer, q_dram, k_dram):
    shared = layer == 1
    S_BANK, ST_BANK, ST_BANKS, PV_BANK = 0, 4, 3, 7
    P_SLOTS = 4
    UNITS = HG * QT
    with ExitStack() as ctx:
        def sem(name):
            return ctx.enter_context(nc.semaphore(f"{name}_{layer}"))

        q_loaded = [sem(f"q_loaded{i}") for i in range(4)]
        k_loaded = [sem(f"k_loaded{i}") for i in range(2)]
        v_ready = sem("v_ready")
        item_full, item_done = sem("item_full"), sem("item_done")
        parts_ready = sem("max_parts_ready")
        max_loaded = [sem(f"max_loaded{i}") for i in range(2)]
        st_full, exp_done, pv_done = sem("st_full"), sem("exp_done"), sem("pv_done")
        zt_ready = sem("zt_ready")
        dve_steps = sem("dve_steps_att")

        probs = [m.scratch[:, i * HG * HQ:(i + 1) * HG * HQ].rearrange("p (h q) -> p h q", h=HG)
                 for i in range(P_SLOTS)]
        off = P_SLOTS * HG * HQ
        zt = [m.scratch[:, off + i * HQ:off + (i + 1) * HQ] for i in range(2)]
        minus_max = ctx.enter_context(nc.sbuf_tensor(f"minus_max_{layer}", [P, 2, UNITS], F32))
        max_parts = ctx.enter_context(nc.sbuf_tensor(f"max_parts_{layer}", [UNITS, 2, PARTS, P], BF16))
        max_rest = ctx.enter_context(nc.sbuf_tensor(f"max_rest_{layer}", [UNITS, P], F32))
        inverse = ctx.enter_context(nc.sbuf_tensor(f"inverse_{layer}", [P, 2, UNITS], F32))

        def items(n):
            out = []
            for s in range(KT):
                second = s < KT // 2
                half = n + 1 if second else n + 2
                if 0 <= half < HALVES:
                    out += [(s, "unit", UNITS // 2 * second + 2 * (s % (KT // 2)) + i) for i in range(2)]
                if s == 2 and 0 <= n - 1 < HALVES:
                    out.append((s, "out", None))
                if s == 5 and 0 <= n + 1 < HALVES:
                    out.append((s, "max", None))
            return out

        FIRST, LAST = -2, HALVES
        LOOP_FROM, PER = 1, 4
        LOOPS = (HALVES - 2 - LOOP_FROM) // PER
        starts, k = {}, 0
        for n in range(FIRST, LAST + 1):
            starts[n] = k
            k += len(items(n))
        FULL = len(items(LOOP_FROM))

        def start_of(J, r):
            return starts[r] if isinstance(J, int) else J * (PER * FULL) + starts[r]

        def loop(engine, period, chain=None, per_period=0):
            for n in range(FIRST, LOOP_FROM):
                period(0, n)
            before = chain.count if chain else 0
            with engine.Fori(0, LOOPS) as J:
                if chain:
                    chain.base, chain.count = J * (PER * per_period), before
                for r in range(LOOP_FROM, LOOP_FROM + PER):
                    period(J, r)
                assert not chain or chain.count == before + PER * per_period
            if chain:
                chain.base = (LOOPS - 1) * PER * per_period
            for n in range(LOOP_FROM + PER * LOOPS, LAST + 1):
                period(0, n)

        def ring(J, r):
            base = start_of(J, r)
            shape = items(r)
            return [(s, kind, unit, base + i, (starts[r] + i) % 2) for i, (s, kind, unit) in enumerate(shape)]

        def out_item(r):
            return [i for i, it in enumerate(items(r)) if it[1] == "out"][0]

        block = ctx.enter_context(nc.Block())

        @block.sync
        def _(sp):
            def load_q(J, r):
                slot = r % 4
                qh = r % 2
                g = 2 * J + r // 2
                src = q_dram[bass.ds(g, 1), :, :, qh * HQ:(qh + 1) * HQ].rearrange(
                    "o s (h d) t -> d (o s) h t", h=HG)
                for j, part in enumerate(Q_PARTS):
                    sp.dma_start(m.q_stack[j * DH:(j + 1) * DH, slot, :, :],
                                 src[:, part, :, :]).then_inc(q_loaded[slot], 16)

            def load_k(J, r):
                slot = r % 2
                if shared:
                    b = (2 * J + r) // (GROUPS // B)
                    src = k_dram[bass.ds(b, 1), :, :, :].rearrange("o s (h d) t -> d (o s) h t", h=1)
                else:
                    g = 2 * J + r
                    src = k_dram[bass.ds(g, 1), :, :, :].rearrange("o s (h d) t -> d (o s) h t", h=HG)
                for j, part in enumerate(K_PARTS):
                    one = src[:, part, :, :]
                    if shared:
                        one = one.to_broadcast([DH, HG, S])
                    sp.dma_start(m.k_stack[j * DH:(j + 1) * DH, slot, :, :], one).then_inc(k_loaded[slot], 16)

            def period(J, r):
                n = PER * J + r
                static = isinstance(J, int)
                ge(sp, st_full, n * KT * HG)
                if r == FIRST:
                    load_q(0, 0)
                    load_k(0, 0)
                    load_k(0, 1)
                if not static or n + 3 < HALVES:
                    load_q(J, r + 3)
                if r % 2 == 0 and (not static or (n >= 2 and n // 2 + 1 < GROUPS)):
                    load_k(J, r // 2 + 1)
                if not static or 0 <= n + 1 < HALVES:
                    nxt = (r + 1) % 2
                    sp.wait_ge(parts_ready, n + 2)
                    for s in range(PARTS):
                        dst = m.q_stack[ROWS + s:ROWS + s + 1, (r + 1) % 4, :, :]
                        sp.dma_start(dst.rearrange("o h (t q) -> o (h t) q", q=P),
                                     max_parts[:, nxt, s, :]).then_inc(max_loaded[nxt], 16)

            loop(sp, period)

        @block.gpsimd
        def _(pool):
            def v_copy(J, r):
                ge(pool, pv_done, (2 * J + r - 1) * 2 * KT)
                src = m.v[:, bass.ds(2 * J + r, 1), :, :].rearrange("p o t (h d) -> p (o t) h d", h=HG)
                pool.tensor_copy(m.v_group[:, r % 2, :, :, 0:DH], src).then_inc(v_ready, 1)

            v_copy(0, 0)
            v_copy(0, 1)
            with pool.Fori(1, GROUPS // 2) as J:
                v_copy(J, 0)
                v_copy(J, 1)

        @block.tensor
        def _(pe):
            def item(J, r, kind, unit, index, slot, half_r, last_unit_in_front=False):
                ge(pe, item_done, index if kind == "max" and last_unit_in_front else index - 1)
                banks = m.psum[:, S_BANK + 2 * slot:S_BANK + 2 * slot + 2, :]
                if kind == "unit":
                    h, t = unit // QT, unit % QT
                    if unit == 0:
                        pe.wait_ge(q_loaded[half_r % 4], 96 * (J + half_r // 4 + 1))
                        pe.wait_ge(k_loaded[half_r // 2 % 2], 96 * (J + half_r // 4 + 1))
                    for kh in range(2):
                        ins = pe.matmul(banks[:, kh, :], m.q_stack[0:ROWS, half_r % 4, h, t * P:(t + 1) * P],
                                        m.k_stack[0:ROWS, half_r // 2 % 2, h, kh * 512:(kh + 1) * 512],
                                        start=True, stop=True)
                elif kind == "max":
                    ins = pe.transpose(banks[0:UNITS, 0, 0:P], minus_max[:, half_r % 2, :], m.ident[:, :])
                else:
                    pe.wait_ge(zt_ready, PER * J + r)
                    for t in range(QT):
                        ins = pe.transpose(banks[:, 0, t * P:(t + 1) * P], zt[half_r % 2][:, t * P:(t + 1) * P],
                                           m.ident[:, :])
                ins.then_inc(item_full, 1)

            def pv(J, r, s):
                n = PER * J + r
                pe.wait_ge(exp_done, n * (KT * HG) + HG * (s + 1))
                if s == 0:
                    pe.wait_ge(v_ready, n // 2 + 1 if isinstance(J, int) else 2 * J + r // 2 + 1)
                    ge(pe, zt_ready, n)
                for h in range(HG):
                    ins = pe.matmul(m.psum[h * VW:(h + 1) * VW, PV_BANK, :], m.v_group[:, r // 2 % 2, s, h, :],
                                    probs[s % P_SLOTS][:, h, :], start=(s == 0), stop=(s == KT - 1),
                                    tile_position=(0, h * VW))
                ins.then_inc(pv_done, 1)

            def st(J, r, s, h):
                n = PER * J + r
                i = s * HG + h
                if i == 0:
                    pe.wait_ge(max_loaded[r % 2], 48 * (2 * J + r // 2 + 1))
                last = i - ST_BANKS if i >= ST_BANKS else {0: -2, 1: -1, 2: -3}[i]
                ge(pe, exp_done, n * (KT * HG) + last + 1)
                pe.matmul(m.psum[:, ST_BANK + i % ST_BANKS, :],
                          m.k_stack[0:ROWS + PARTS, r // 2 % 2, h, s * P:(s + 1) * P],
                          m.q_stack[0:ROWS + PARTS, r % 4, h, :], start=True, stop=True).then_inc(st_full, 1)

            def period(J, r):
                on = 0 <= r < HALVES
                todo = ring(J, r)
                for s in range(KT):
                    here = [x for x in todo if x[0] == s]
                    half_r = r + 1 if s < KT // 2 else r + 2
                    units = [x for x in here if x[1] == "unit"]
                    for pair in range(2):
                        if on:
                            st(J, r, s, 2 * pair)
                            st(J, r, s, 2 * pair + 1)
                        if units:
                            _, kind, unit, index, slot = units[pair]
                            item(J, r, kind, unit, index, slot, half_r)
                    if s >= 1 and on:
                        pv(J, r, s - 1)
                    if s == 0 and 0 <= r - 1 < HALVES:
                        pv(J, r - 1, KT - 1)
                    for _, kind, unit, index, slot in here:
                        if kind == "max":
                            front = todo[[x[1] for x in todo].index("max") - 1]
                            item(J, r, kind, unit, index, slot, r + 1, front[0] < KT // 2)
                        if kind == "out":
                            item(J, r, kind, unit, index, slot, r - 1)

            loop(pe, period)

        @block.scalar
        def _(act):
            def take_out(J, r):
                n = PER * J + r
                act.wait_ge(pv_done, n * KT)
                if not (isinstance(J, int) and n - 3 < 0):
                    act.wait_ge(item_done, start_of(J, r) - 2 * FULL + out_item(LOOP_FROM) + 1
                                if not isinstance(J, int) else starts[n - 2] + out_item(n - 2) + 1)
                act.copy(zt[(r - 1) % 2], m.psum[:, PV_BANK, :]).then_inc(zt_ready, 1)

            def period(J, r):
                n = PER * J + r
                if not 0 <= r < HALVES:
                    if r == HALVES:
                        take_out(J, r)
                    return
                for s in range(KT):
                    ge(act, pv_done, n * KT + s - P_SLOTS + 1)
                    for h in range(HG):
                        i = s * HG + h
                        act.wait_ge(st_full, n * (KT * HG) + i + 1)
                        act.activation(probs[s % P_SLOTS][:, h, :], m.psum[:, ST_BANK + i % ST_BANKS, :], ACT.Exp,
                                       scale=SCALE).then_inc(exp_done, 1)
                        if s == 1 and h == 0 and r - 1 >= 0:
                            take_out(J, r)

            loop(act, period)

        @block.vector
        def _(dve):
            chain = Chain(dve, dve_steps)

            def period(J, r):
                for s, kind, unit, index, slot in ring(J, r):
                    banks = m.psum[:, S_BANK + 2 * slot:S_BANK + 2 * slot + 2, :]
                    dve.wait_ge(item_full, index + 1)
                    if kind == "unit":
                        par = (r + 1 if s < KT // 2 else r + 2) % 2
                        dve.tensor_reduce(minus_max[:, par, unit:unit + 1], banks, AX.XY, ALU.max,
                                          negate=True).then_inc(item_done, 1)
                    elif kind == "max":
                        par = (r + 1) % 2
                        n = PER * J + r
                        ge(dve, max_loaded[par], 48 * (2 * J + (r + 1) // 2))
                        row = banks[0:UNITS, 0, 0:P]
                        chain.then(dve.tensor_copy(max_parts[:, par, 0, :], row))
                        ins = dve.tensor_tensor(max_rest[:, :], row, max_parts[:, par, 0, :], ALU.subtract)
                        ins.then_inc(item_done, 1)
                        dve.wait_ge(item_done, index + 1)
                        chain.then(dve.tensor_copy(max_parts[:, par, 1, :], max_rest[:, :]))
                        dve.tensor_tensor(max_parts[:, par, 2, :], max_rest[:, :], max_parts[:, par, 1, :],
                                          ALU.subtract).then_inc(parts_ready, 1)
                    else:
                        sums = banks[:, 0, :].rearrange("p (g w) -> p g w", w=VW)
                        par = (r - 1) % 2
                        chain.then(dve.reciprocal(inverse[:, par, :], sums[:, :, DH]))
                        qh = (r - 1) % 2
                        g = 2 * J + (r - 1) // 2
                        dst = m.z[:, bass.ds(g, 1), qh * QT:(qh + 1) * QT, :].rearrange(
                            "p o t (h d) -> p (o t h) d", d=DH)
                        inv = inverse[:, par, :].rearrange("p (g o) -> p g o", o=1).to_broadcast([P, UNITS, DH])
                        dve.tensor_tensor(dst, sums[:, :, 0:DH], inv, ALU.mult).then_inc(item_done, 1)

            loop(dve, period, chain, 3)


def mixture(nc, m):
    ZT_BANK, U_BANK, XT_BANK, BIAS_BANK, E_BANK = 0, 1, 2, 3, 4
    PAIRS = EXPERTS // 2
    AHEAD = 2
    with ExitStack() as ctx:
        def sem(name):
            return ctx.enter_context(nc.semaphore(f"mix_{name}"))

        zs_ready, zt_full, zt_ready, u_full, u_ready = (
            sem("zs_ready"), sem("zt_full"), sem("zt_ready"), sem("u_full"), sem("u_ready"))
        u_stats, u_rstd, x1_stats, x1_rstd = sem("u_stats"), sem("u_rstd"), sem("x1_stats"), sem("x1_rstd")
        xln_ready, xt_full, xt_ready = sem("xln_ready"), sem("xt_full"), sem("xt_ready")
        gate_full, shifted, exps_ready, weights_ready = (
            sem("gate_full"), sem("shifted"), sem("exps_ready"), sem("weights_ready"))
        wt_full, wt_ready, bias_full, bias_read = sem("wt_full"), sem("wt_ready"), sem("bias_full"), sem("bias_read")
        pair_full, pair_read = sem("pair_full"), sem("pair_read")
        y_stats, y_rstd = sem("y_stats"), sem("y_rstd")
        dve_steps, pool_steps = sem("dve_steps"), sem("pool_steps")

        def cut(i):
            return m.scratch[:, i * D:(i + 1) * D]

        zs, zt, u, xln, xt = ([cut(2 * k + i) for i in range(2)] for k in range(5))
        first_ln, normal, y = cut(10), cut(11), [cut(12), cut(13)]

        def sb(name, shape, dt=F32):
            return ctx.enter_context(nc.sbuf_tensor(f"mix_{name}", shape, dt))

        bn = [sb(f"bn{i}", [P, 6]) for i in range(3)]
        mv = [sb(f"mv{i}", [P, 2]) for i in range(3)]
        var = [sb(f"var{i}", [P, 1]) for i in range(3)]
        rstd = [sb(f"rstd{i}", [P, 1]) for i in range(3)]
        logits, top_logits = sb("logits", [P, GATES]), sb("top_logits", [P, 8])
        exps, exps_sum, inverse = sb("exps", [P, GATES]), sb("exps_sum", [P, 1]), sb("inverse", [P, 1])
        gates, top, where = sb("gates", [P, GATES]), sb("top", [P, 8]), sb("where", [P, 8], U32)
        index, real, kept = sb("index", [P, 2]), sb("real", [P, 2]), sb("kept", [P, 2])
        total, share = sb("total", [P, 1]), sb("share", [P, 2])
        picks = sb("picks", [P, 2, EXPERTS])
        weights = sb("weights", [P, 2, EXPERTS])
        wt = sb("wt", [EXPERTS, 2, P])

        def loop(engine, body, first, chain=None, per_tile=0):
            for i in range(first, 2):
                body(0, i)
            before = chain.count if chain else 0
            loops = (TILES - 6) // 2
            with engine.Fori(1, 1 + loops) as J:
                if chain:
                    chain.base, chain.count = (J - 1) * (2 * per_tile), before
                body(J, 0)
                body(J, 1)
                assert not chain or chain.count == before + 2 * per_tile, (chain.count, before)
            if chain:
                chain.base = (loops - 1) * 2 * per_tile
            for i in range(2 + 2 * loops, TILES):
                body(0, i)

        def ahead(J, r, by):
            return not isinstance(J, int) or 0 <= r + by < TILES

        block = ctx.enter_context(nc.Block())

        @block.gpsimd
        def _(pool):
            chain = Chain(pool, pool_steps)

            def take_rstd(k, stats, ready, count):
                pool.wait_ge(stats, count)
                chain.then(pool.tensor_tensor(var[k][:, :], mv[k][:, 1:2], m.eps[:, 0:1], ALU.add))
                pool.tensor_tensor(rstd[k][:, :], var[k][:, :], m.minus_half[:, 0:1], ALU.pow).then_inc(ready, 1)

            def body(J, r):
                i = 2 * J + r
                if ahead(J, r, AHEAD):
                    take_rstd(0, u_stats, u_rstd, i + 3)
                if ahead(J, r, 0):
                    take_rstd(1, y_stats, y_rstd, i + 1)
                if ahead(J, r, AHEAD):
                    take_rstd(2, x1_stats, x1_rstd, i + 3)
                if ahead(J, r, AHEAD + 1):
                    t = i + AHEAD + 1
                    b, qt = t // KT, t % KT
                    ge(pool, zt_full, t - 1)
                    src = m.z[:, bass.ds(b * (GROUPS // B), GROUPS // B), bass.ds(qt, 1), :]
                    pool.tensor_copy(zs[(r + 3) % 2].rearrange("p (g n) -> p g n", g=GROUPS // B),
                                     src.rearrange("p g o n -> p g (o n)")).then_inc(zs_ready, 1)

            loop(pool, body, -AHEAD - 1, chain, 3)

        @block.tensor
        def _(pe):
            def experts(i, par, pairs):
                for pair in pairs:
                    ge(pe, pair_read, PAIRS * (i - 1) + pair + 1)
                    for half in range(2):
                        for k in range(KC):
                            ins = pe.matmul(m.psum[:, E_BANK + pair, half * D:(half + 1) * D],
                                            xt[par][:, k * P:(k + 1) * P],
                                            m.expert_w[:, k, 2 * pair + half, :], start=(k == 0), stop=(k == KC - 1))
                    ins.then_inc(pair_full, 1)

            def turn(bank, src):
                for k in range(KC):
                    ins = pe.transpose(m.psum[:, bank, k * P:(k + 1) * P], src[:, k * P:(k + 1) * P], m.ident[:, :])
                return ins

            def body(J, r):
                i, par = 2 * J + r, r % 2
                if ahead(J, r, 0):
                    pe.wait_ge(xln_ready, i + 1)
                    ge(pe, shifted, i)
                    turn(XT_BANK, xln[par]).then_inc(xt_full, 1)
                if ahead(J, r, AHEAD):
                    pe.wait_ge(zs_ready, i + 3)
                    ge(pe, wt_ready, i)
                    ge(pe, zt_ready, i + 2)
                    turn(ZT_BANK, zs[par]).then_inc(zt_full, 1)
                if ahead(J, r, 0):
                    pe.wait_ge(xt_ready, i + 1)
                    for k in range(KC):
                        ins = pe.matmul(m.psum[:, XT_BANK, D:D + GATES], xt[par][:, k * P:(k + 1) * P],
                                        m.gate_w[:, k, :], start=(k == 0), stop=(k == KC - 1))
                    ins.then_inc(gate_full, 1)
                    experts(i, par, range(PAIRS // 2))
                if ahead(J, r, AHEAD):
                    pe.wait_ge(zt_ready, i + 3)
                    ge(pe, u_ready, i + 2)
                    for k in range(KC):
                        ins = pe.matmul(m.psum[:, U_BANK, 0:D], zt[par][:, k * P:(k + 1) * P], m.wout[:, k, :],
                                        start=(k == 0), stop=(k == KC - 1))
                    ins.then_inc(u_full, 1)
                if ahead(J, r, 0):
                    experts(i, par, range(PAIRS // 2, PAIRS - 1))
                    pe.wait_ge(weights_ready, i + 1)
                    pe.transpose(m.psum[0:EXPERTS, ZT_BANK, D:D + P], weights[:, par, :],
                                 m.ident[:, :]).then_inc(wt_full, 1)
                    experts(i, par, range(PAIRS - 1, PAIRS))
                    pe.wait_ge(wt_ready, i + 1)
                    ge(pe, bias_read, i)
                    pe.matmul(m.psum[:, BIAS_BANK, 0:D], wt[:, par, :], m.expert_b[:, :],
                              start=True, stop=True).then_inc(bias_full, 1)

            loop(pe, body, -AHEAD)

        @block.scalar
        def _(act):
            def body(J, r):
                i, par = 2 * J + r, r % 2
                if ahead(J, r, 0):
                    act.wait_ge(xt_full, i + 1)
                    ge(act, pair_full, PAIRS * (i - 1))
                    act.copy(xt[par], m.psum[:, XT_BANK, 0:D]).then_inc(xt_ready, 1)
                if ahead(J, r, AHEAD):
                    act.wait_ge(zt_full, i + 3)
                    ge(act, u_full, i + 1)
                    act.copy(zt[par], m.psum[:, ZT_BANK, 0:D]).then_inc(zt_ready, 1)
                if ahead(J, r, 0):
                    act.wait_ge(shifted, i + 1)
                    act.activation(exps[:, :], logits[:, :], ACT.Exp, accum_out=exps_sum[:, :]).then_inc(exps_ready, 1)
                    act.wait_ge(wt_full, i + 1)
                    ge(act, bias_full, i - 1)
                    act.copy(wt[:, par, :], m.psum[0:EXPERTS, ZT_BANK, D:D + P]).then_inc(wt_ready, 1)

            loop(act, body, -AHEAD)

        @block.vector
        def _(dve):
            chain = Chain(dve, dve_steps)

            def statistics(k, src, done):
                chain.then(dve.bn_stats(bn[k][:, :], src), bare=True)
                dve.bn_aggr(mv[k][:, :], bn[k][:, :]).then_inc(done, 1)

            def normalise(k, out, src):
                return dve.tensor_scalar(out, src, mv[k][:, 0:1], rstd[k][:, 0:1], ALU.subtract, ALU.mult)

            def gate(i, par):
                step = chain.then
                dve.wait_ge(gate_full, i + 1)
                step(dve.tensor_tensor(logits[:, :], m.psum[:, XT_BANK, D:D + GATES], m.gate_b[:, :], ALU.add), bare=True)
                step(dve.max(top_logits[:, :], logits[:, :]))
                dve.tensor_scalar(logits[:, :], logits[:, :], top_logits[:, 0:1], None,
                                  ALU.subtract).then_inc(shifted, 1)
                dve.wait_ge(exps_ready, i + 1)
                step(dve.reciprocal(inverse[:, :], exps_sum[:, :]))
                step(dve.tensor_scalar(gates[:, :], exps[:, :], inverse[:, 0:1], None, ALU.mult), bare=True)
                step(dve.max(top[:, :], gates[:, :]), bare=True)
                step(dve.max_index(where[:, :], top[:, :], gates[:, :]))
                step(dve.tensor_copy(index[:, :], where[:, 0:2]))
                step(dve.tensor_scalar(real[:, :], index[:, :], float(EXPERTS), None, ALU.is_lt))
                step(dve.tensor_tensor(kept[:, :], top[:, 0:2], real[:, :], ALU.mult))
                step(dve.tensor_reduce(total[:, :], kept[:, :], AX.X, ALU.add))
                step(dve.scalar_tensor_tensor(out=total[:, :], in0=total[:, :], scalar=0.0, in1=total[:, :],
                                              op0=ALU.is_equal, op1=ALU.add))
                step(dve.reciprocal(inverse[:, :], total[:, :]))
                step(dve.tensor_scalar(share[:, :], kept[:, :], inverse[:, 0:1], None, ALU.mult))
                dve.tensor_scalar(picks[:, 0, :], m.index[:, :], index[:, 0:1], share[:, 0:1], ALU.is_equal, ALU.mult)
                step(dve.tensor_scalar(picks[:, 1, :], m.index[:, :], index[:, 1:2], share[:, 1:2],
                                       ALU.is_equal, ALU.mult))
                dve.tensor_tensor(weights[:, par, :], picks[:, 0, :], picks[:, 1, :],
                                  ALU.add).then_inc(weights_ready, 1)
                dve.wait_ge(weights_ready, i + 1)

            def add_experts(i, par, pairs):
                for pair in pairs:
                    dve.wait_ge(pair_full, PAIRS * i + pair + 1)
                    for half in range(2):
                        e = 2 * pair + half
                        src, w = m.psum[:, E_BANK + pair, half * D:(half + 1) * D], weights[:, par, e:e + 1]
                        if e == 0:
                            ins = dve.tensor_scalar(y[0], src, w, None, ALU.mult)
                        else:
                            ins = dve.scalar_tensor_tensor(out=y[e % 2], in0=src, scalar=w, in1=y[1 - e % 2],
                                                           op0=ALU.mult, op1=ALU.add)
                        if half == 0:
                            chain.then(ins)
                        else:
                            ins.then_inc(pair_read, 1)
                            dve.wait_ge(pair_read, PAIRS * i + pair + 1)

            def body(J, r):
                i, par = 2 * J + r, r % 2
                tile_i, tile_a = bass.ds(i, 1), bass.ds(i + AHEAD, 1)
                if ahead(J, r, 0):
                    gate(i, par)
                    add_experts(i, par, range(PAIRS // 2))
                if ahead(J, r, AHEAD):
                    chain.then(dve.tensor_scalar(first_ln, m.x[:, tile_a, :], m.mean[:, tile_a],
                                                 m.rstd[:, tile_a], ALU.subtract, ALU.mult))
                    dve.wait_ge(u_full, i + 3)
                    dve.tensor_tensor(u[par], m.psum[:, U_BANK, 0:D], first_ln, ALU.add).then_inc(u_ready, 1)
                    ge_bare(dve, u_ready, i + 3)
                    statistics(0, u[par], u_stats)
                if ahead(J, r, 0):
                    add_experts(i, par, range(PAIRS // 2, PAIRS))
                    dve.wait_ge(bias_full, i + 1)
                    dve.tensor_tensor(y[0], y[1], m.psum[:, BIAS_BANK, 0:D], ALU.add).then_inc(bias_read, 1)
                    ge_bare(dve, bias_read, i + 1)
                    statistics(1, y[0], y_stats)
                if ahead(J, r, AHEAD):
                    dve.wait_ge(u_rstd, i + 3)
                    chain.then(normalise(0, normal, u[par]))
                    chain.then(dve.tensor_tensor(m.x[:, tile_a, :], m.x[:, tile_a, :], normal, ALU.add), bare=True)
                    statistics(2, m.x[:, tile_a, :], x1_stats)
                if ahead(J, r, 0):
                    dve.wait_ge(y_rstd, i + 1)
                    chain.then(normalise(1, normal, y[0]))
                    chain.then(dve.tensor_tensor(m.x[:, tile_i, :], m.x[:, tile_i, :], normal, ALU.add))
                if ahead(J, r, AHEAD):
                    dve.wait_ge(x1_rstd, i + 3)
                    ge(dve, xt_full, i + 1)
                    normalise(2, xln[par], m.x[:, tile_a, :]).then_inc(xln_ready, 1)

            loop(dve, body, -AHEAD, chain, 26)


def spectral(nc, m, out):
    XT_BANK, Y_BANK = 0, 2
    with ExitStack() as ctx:
        def sem(name):
            return ctx.enter_context(nc.semaphore(f"spec_{name}"))

        z_stats, z_rstd, x_stats, x_rstd, y_stats, y_rstd = (
            sem("z_stats"), sem("z_rstd"), sem("x_stats"), sem("x_rstd"), sem("y_stats"), sem("y_rstd"))
        xln_ready, xt_full, xt_ready, y_full, y_read = (
            sem("xln_ready"), sem("xt_full"), sem("xt_ready"), sem("y_full"), sem("y_read"))
        out_ready = sem("out_ready")
        out_stored = [sem(f"out_stored{i}") for i in range(2)]
        dve_steps, pool_steps = sem("dve_steps"), sem("pool_steps")
        W = CHUNK * D

        def tiles(i):
            return m.scratch[:, i * W:(i + 1) * W].rearrange("p (t d) -> p t d", t=CHUNK)

        xln, y, normal, res = tiles(0), tiles(1), tiles(2), [tiles(3), tiles(4)]
        xt = [m.scratch[:, (5 + i) * W:(6 + i) * W].rearrange("p (c t) -> p c t", c=KC) for i in range(2)]

        def sb(name, shape):
            return ctx.enter_context(nc.sbuf_tensor(f"spec_{name}", shape, F32))

        bn = [sb(f"bn{i}", [P, CHUNK, 6]) for i in range(3)]
        mv = [sb(f"mv{i}", [P, CHUNK, 2]) for i in range(3)]
        var = [sb(f"var{i}", [P, CHUNK]) for i in range(3)]
        rstd = [sb(f"rstd{i}", [P, CHUNK]) for i in range(3)]

        def loop(engine, body, chain=None, per_chunk=0):
            body(0, -1)
            body(0, 0)
            before = chain.count if chain else 0
            with engine.Fori(0, CHUNKS // 2 - 1) as J:
                if chain:
                    chain.base, chain.count = J * (2 * per_chunk), before
                body(J, 1)
                body(J, 2)
                assert not chain or chain.count == before + 2 * per_chunk, (chain.count, before)
            if chain:
                chain.base = (CHUNKS // 2 - 2) * 2 * per_chunk
            body(0, CHUNKS - 1)

        def ahead(J, u):
            return not isinstance(J, int) or u + 1 < CHUNKS

        block = ctx.enter_context(nc.Block())

        @block.gpsimd
        def _(pool):
            chain = Chain(pool, pool_steps)

            def take_rstd(k, stats, ready, count):
                pool.wait_ge(stats, count)
                chain.then(pool.tensor_tensor(var[k][:, :], mv[k][:, :, 1], m.eps[:, :], ALU.add))
                pool.tensor_tensor(rstd[k][:, :], var[k][:, :], m.minus_half[:, :], ALU.pow).then_inc(ready, 1)

            def body(J, u):
                c = 2 * J + u
                if ahead(J, u):
                    take_rstd(0, z_stats, z_rstd, c + 2)
                if u >= 0:
                    take_rstd(1, y_stats, y_rstd, c + 1)
                if ahead(J, u):
                    take_rstd(2, x_stats, x_rstd, c + 2)

            loop(pool, body, chain, 3)

        @block.tensor
        def _(pe):
            def body(J, u):
                c = 2 * J + u
                if u >= 0:
                    pe.wait_ge(xt_ready, c + 1)
                    ge(pe, y_read, c)
                    for t in range(CHUNK):
                        for k in range(KC):
                            ins = pe.matmul(m.psum[:, Y_BANK + t // 2, (t % 2) * D:(t % 2 + 1) * D],
                                            xt[u % 2][:, k, t * P:(t + 1) * P], m.fold[:, k, :],
                                            start=(k == 0), stop=(k == KC - 1))
                    ins.then_inc(y_full, 1)
                if ahead(J, u):
                    pe.wait_ge(xln_ready, c + 2)
                    ge(pe, xt_ready, c + 1)
                    for t in range(CHUNK):
                        for k in range(KC):
                            ins = pe.transpose(m.psum[:, XT_BANK + k, t * P:(t + 1) * P],
                                               xln[:, t, k * P:(k + 1) * P], m.ident[:, :])
                    ins.then_inc(xt_full, 1)

            loop(pe, body)

        @block.scalar
        def _(act):
            def body(J, u):
                c = 2 * J + u
                if ahead(J, u):
                    act.wait_ge(xt_full, c + 2)
                    ge(act, y_full, c)
                    act.copy(xt[(u + 1) % 2], m.psum[:, XT_BANK:XT_BANK + 2, :]).then_inc(xt_ready, 1)

            loop(act, body)

        @block.vector
        def _(dve):
            chain = Chain(dve, dve_steps)

            def statistics(k, src, done):
                for t in range(CHUNK):
                    ins = dve.bn_stats(bn[k][:, t, :], src(t))
                chain.then(ins, bare=True)
                for t in range(CHUNK):
                    ins = dve.bn_aggr(mv[k][:, t, :], bn[k][:, t, :])
                ins.then_inc(done, 1)

            def normalise(k, out, src):
                for t in range(CHUNK):
                    ins = dve.tensor_scalar(out(t), src(t), mv[k][:, t, 0:1], rstd[k][:, t:t + 1],
                                            ALU.subtract, ALU.mult)
                return ins

            def body(J, u):
                c = 2 * J + u
                b, qt = J + (u + 1) // 2, (u + 1) % 2 * CHUNK

                def z_tile(t):
                    return m.z[:, bass.ds(b * (GROUPS // B), GROUPS // B), qt + t, :]

                def x_chunk(first):
                    return m.x[:, bass.ds(first * CHUNK, CHUNK), :]

                if ahead(J, u):
                    for t in range(CHUNK):
                        ins = dve.tensor_copy(normal[:, t, :].rearrange("p (g n) -> p g n", g=GROUPS // B), z_tile(t))
                    chain.then(ins, bare=True)
                    statistics(0, lambda t: normal[:, t, :], z_stats)
                if u >= 0:
                    dve.wait_ge(y_full, c + 1)
                    in_psum = m.psum[:, Y_BANK:Y_BANK + 2, :].rearrange("p b (t d) -> p (b t) d", d=D)
                    bias = m.bias[:, :].rearrange("p (o d) -> p o d", o=1).to_broadcast([P, CHUNK, D])
                    dve.tensor_tensor(y, in_psum, bias, ALU.add).then_inc(y_read, 1)
                    ge_bare(dve, y_read, c + 1)
                    statistics(1, lambda t: y[:, t, :], y_stats)
                if ahead(J, u):
                    dve.wait_ge(z_rstd, c + 2)
                    chain.then(normalise(0, lambda t: normal[:, t, :], lambda t: normal[:, t, :]))
                    chain.then(dve.tensor_tensor(x_chunk(c + 1), x_chunk(c + 1), normal, ALU.add), bare=True)
                    statistics(2, lambda t: m.x[:, bass.ds((c + 1) * CHUNK + t, 1), :], x_stats)
                if u >= 0:
                    dve.wait_ge(y_rstd, c + 1)
                    chain.then(normalise(1, lambda t: y[:, t, :], lambda t: y[:, t, :]))
                    ge(dve, out_stored[u % 2], 16 * (J + u // 2))
                    dve.tensor_tensor(res[u % 2], x_chunk(c), y, ALU.add).then_inc(out_ready, 1)
                if ahead(J, u):
                    dve.wait_ge(x_rstd, c + 2)
                    ge(dve, xt_full, c + 1)
                    normalise(2, lambda t: xln[:, t, :],
                              lambda t: m.x[:, bass.ds((c + 1) * CHUNK + t, 1), :]).then_inc(xln_ready, 1)

            loop(dve, body, chain, 7)

        @block.sync
        def _(sp):
            out_view = out.rearrange("(c t p) d -> c p t d", p=P, t=CHUNK)

            def body(J, u):
                if u < 0:
                    return
                c = 2 * J + u
                sp.wait_ge(out_ready, c + 1)
                sp.dma_start(out_view[bass.ds(c, 1), :, :, :].rearrange("o p t d -> p (o t) d"),
                             res[u % 2]).then_inc(out_stored[u % 2], 16)

            loop(sp, body)
            sp.wait_ge(out_stored[0], 16 * CHUNKS // 2)
            sp.wait_ge(out_stored[1], 16 * CHUNKS // 2)


def build(nc, io, out):
    q_dram = [nc.dram_tensor(f"q_parts{i}", [GROUPS, PARTS, GF, S], BF16).ap() for i in range(2)]
    k_dram = [nc.dram_tensor("k_parts0", [GROUPS, PARTS, GF, S], BF16).ap(),
              nc.dram_tensor("k_parts1", [B, PARTS, DH, S], BF16).ap()]
    with ExitStack() as ctx:
        m = Memory(nc, ctx)
        setup(nc, m, io)
        projection(nc, m, 0, q_dram[0], k_dram[0])
        attention(nc, m, 0, q_dram[0], k_dram[0])
        mixture(nc, m)
        projection(nc, m, 1, q_dram[1], k_dram[1])
        attention(nc, m, 1, q_dram[1], k_dram[1])
        spectral(nc, m, out)


def constants():
    n = np.arange(D)
    angle = 2.0 * np.pi * (np.outer(n, n) % D) / D
    return {
        "dft_cos": np.cos(angle).astype(np.float32),
        "dft_sin": np.sin(angle).astype(np.float32),
        "dft_minus_cos": (-np.cos(angle)).astype(np.float32),
        "ident": np.eye(P, dtype=np.float32),
        "index": np.broadcast_to(np.arange(EXPERTS, dtype=np.float32), (P, EXPERTS)).copy(),
    }


def kernel(L0_attn_x, L0_attn_mask, L0_attn_Wq, L0_attn_Wk, L0_attn_Wv, L0_attn_Wout, L0_ffn_gate_w, L0_ffn_gate_b,
           L0_ffn_expert_w, L0_ffn_expert_b, L1_attn_Wq, L1_attn_Wk, L1_attn_Wv, L1_ffn_w_freq_real,
           L1_ffn_w_freq_imag, L1_ffn_bias):
    import concourse.bacc as bacc
    from concourse.bass_utils import run_bass_kernel_spmd

    arrays = {
        "x": np.reshape(L0_attn_x, (B * S, D)),
        "wq0": L0_attn_Wq, "wk0": L0_attn_Wk, "wv0": L0_attn_Wv, "wout": L0_attn_Wout,
        "gate_w": np.transpose(L0_ffn_gate_w), "gate_b": np.broadcast_to(L0_ffn_gate_b, (P, GATES)),
        "expert_w": L0_ffn_expert_w, "expert_b": L0_ffn_expert_b,
        "wq1": np.transpose(L1_attn_Wq), "wk1": np.transpose(L1_attn_Wk), "wv1": np.transpose(L1_attn_Wv),
        "w_real": L1_ffn_w_freq_real, "w_imag": L1_ffn_w_freq_imag,
        "bias": np.broadcast_to(L1_ffn_bias, (P, D)),
    }
    arrays.update(constants())
    nc = bacc.Bacc("TRN2", target_bir_lowering=False, num_devices=1)
    feed, io = {}, {}
    for name, a in arrays.items():
        a = np.ascontiguousarray(a)
        feed[f"in_{name}"] = a
        io[name] = nc.dram_tensor(f"in_{name}", a.shape, mybir.dt.from_np(a.dtype), kind="ExternalInput").ap()
    out = nc.dram_tensor("out", (B * S, D), F32, kind="ExternalOutput").ap()
    build(nc, io, out)
    result = run_bass_kernel_spmd(nc, [feed], core_ids=[0])
    return np.reshape(result.results[0]["out"], (B, S, D))
```

```python
from contextlib import ExitStack

import numpy as np

import concourse.bass as bass
from concourse import mybir

F32 = mybir.dt.float32
BF16 = mybir.dt.bfloat16
U32 = mybir.dt.uint32
ALU = mybir.AluOpType
ACT = mybir.ActivationFunctionType
AX = mybir.AxisListType

P = 128
B, S, D, H = 4, 1024, 256, 16
DH = D // H
KC = D // P
TILES = B * S // P
CHUNK = 4
CHUNKS = TILES // CHUNK
CT = CHUNK * P
HG = 4
GROUPS = B * H // HG
GF = HG * DH
HALVES = 2 * GROUPS
HQ = S // 2
KT = S // P
QT = HQ // P
PARTS = 3
Q_PARTS = (0, 0, 0, 1, 1, 2)
K_PARTS = (0, 1, 2, 0, 1, 0)
ROWS = len(Q_PARTS) * DH
VW = 32
EXPERTS, NULLS = 8, 2
GATES = EXPERTS + NULLS
EPS = 1e-5
SCALE = DH ** -0.5

SCRATCH = 9216


def ge(engine, semaphore, value):
    if isinstance(value, int) and value <= 0:
        return
    engine.wait_ge(semaphore, value)


def ge_bare(engine, semaphore, value):
    if not isinstance(value, int):
        engine.lower_val(value)
        engine.wait_ge(semaphore, 1)
    engine.wait_ge(semaphore, value)


class Chain:

    def __init__(self, engine, semaphore):
        self.engine, self.semaphore, self.base, self.count = engine, semaphore, 0, 0

    def then(self, instruction, bare=False):
        instruction.then_inc(self.semaphore, 1)
        self.count += 1
        (ge_bare if bare else ge)(self.engine, self.semaphore, self.base + self.count)


def chunk_loop(engine, body, first, last=CHUNKS - 1, chain=None, per_chunk=0):
    lead, loops = 1, (CHUNKS - 4) // 2
    for c in range(first, lead):
        body(0, c)
    before = chain.count if chain else 0
    with engine.Fori(0, loops) as J:
        if chain:
            chain.base, chain.count = J * (2 * per_chunk), before
        body(J, lead)
        body(J, lead + 1)
        assert not chain or chain.count == before + 2 * per_chunk, (chain.count, before)
    if chain:
        chain.base = (loops - 1) * 2 * per_chunk
    for c in range(lead + 2 * loops, last + 1):
        body(0, c)


def on(J, u, by=0):
    return not isinstance(J, int) or 0 <= u + by < CHUNKS


class Memory:

    def __init__(self, nc, ctx):
        def sb(name, shape, dt=F32):
            return ctx.enter_context(nc.sbuf_tensor(name, shape, dt))

        self.x = sb("x_res", [P, TILES, D])
        self.z = sb("z_res", [P, GROUPS, KT, GF])
        self.v = sb("v_res", [P, GROUPS, KT, GF])
        self.mean = sb("mean_first", [P, TILES])
        self.rstd = sb("rstd_first", [P, TILES])
        self.q_stack = sb("q_stack", [P, 4, HG, HQ], BF16)
        self.k_stack = sb("k_stack", [P, 2, HG, S], BF16)
        self.v_group = sb("v_group", [P, 2, KT, HG, VW])
        self.scratch = sb("scratch", [P, SCRATCH])
        self.ident = sb("ident", [P, P])
        self.wq0 = sb("wq0", [P, KC, D])
        self.wk0 = sb("wk0", [P, KC, D])
        self.wv0 = sb("wv0", [P, KC, D])
        self.wout = sb("wout", [P, KC, D])
        self.wq1 = sb("wq1", [P, KC, D])
        self.wk1 = sb("wk1", [P, KC, DH])
        self.wv1 = sb("wv1", [P, KC, DH])
        self.gate_w = sb("gate_w_sb", [P, KC, GATES])
        self.gate_b = sb("gate_b_sb", [P, GATES])
        self.expert_w = sb("expert_w_sb", [P, KC, EXPERTS, D])
        self.expert_b = sb("expert_b_sb", [EXPERTS, D])
        self.bias = sb("bias_sb", [1, D])
        self.index = sb("index_row", [P, EXPERTS])
        self.fold = sb("fold", [P, KC, D])
        self.eps = sb("eps_col", [P, CHUNK])
        self.minus_half = sb("minus_half", [P, CHUNK])
        self.minus_one = sb("minus_one", [P, CHUNK])
        self.ones = sb("ones_row", [1, P])
        self.psum = ctx.enter_context(nc.psum_tensor("psum", [P, 8, 512], F32))


class Loads:

    def __init__(self, nc, ctx):
        def sem(name):
            return ctx.enter_context(nc.semaphore(name))

        self.x_first = [sem("x_loaded0"), sem("x_loaded1")]
        self.x_rest = sem("x_loaded_rest")
        self.projection, self.dft, self.rest = sem("proj_w_loaded"), sem("dft_loaded"), sem("rest_loaded")
        self.n_projection = self.n_dft = self.n_rest = 0


def setup(nc, m, io, loads):
    with ExitStack() as ctx:
        presets = ctx.enter_context(nc.semaphore("presets"))

        def chunked(w):
            return w.rearrange("(c p) n -> p c n", p=P)

        block = ctx.enter_context(nc.Block())

        @block.sync
        def _(sp):
            x_view = io["x"].rearrange("(t p) d -> p t d", p=P)
            for c in range(CHUNKS):
                t = c * CHUNK
                sem = loads.x_first[c] if c < 2 else loads.x_rest
                sp.dma_start(m.x[:, t:t + CHUNK, :], x_view[:, t:t + CHUNK, :]).then_inc(sem, 16)
            for dst, name in zip(dft_views(m), ("dft_cos", "dft_sin", "dft_minus_cos", "w_real", "w_imag")):
                sp.dma_start(dst, chunked(io[name])).then_inc(loads.dft, 16)
                loads.n_dft += 16

        @block.scalar
        def _(act):
            act.dma_start(m.ident[:, :], io["ident"]).then_inc(loads.projection, 16)
            for dst, name in ((m.wq0, "wq0"), (m.wk0, "wk0"), (m.wv0, "wv0")):
                act.dma_start(dst[:, :, :], chunked(io[name])).then_inc(loads.projection, 16)
            loads.n_projection = 16 * 4
            rest = [(m.gate_b[:, :], io["gate_b"]), (m.bias[:, :], io["bias"]),
                    (m.index[:, :], io["index"]), (m.expert_b[:, :], io["expert_b"])]
            for dst, name in ((m.wout, "wout"), (m.wq1, "wq1"), (m.wk1, "wk1"), (m.wv1, "wv1"),
                              (m.gate_w, "gate_w")):
                rest.append((dst[:, :, :], chunked(io[name])))
            experts = io["expert_w"].rearrange("e (c p) n -> p c e n", p=P)
            rest += [(m.expert_w[:, c, :, :], experts[:, c, :, :]) for c in range(KC)]
            for dst, src in rest:
                act.dma_start(dst, src).then_inc(loads.rest, 16)
                loads.n_rest += 16

        @block.vector
        def _(dve):
            dve.memset(m.eps[:, :], EPS)
            dve.memset(m.minus_half[:, :], -0.5)
            dve.memset(m.minus_one[:, :], -1.0)
            dve.memset(m.ones[:, :], 1.0)
            dve.memset(m.v_group[:, :, :, :, :], 0.0).then_inc(presets, 1)
            dve.wait_ge(presets, 1)
            dve.memset(m.v_group[:, :, :, :, DH:DH + 1], 1.0)
            dve.memset(m.k_stack[ROWS:ROWS + PARTS, :, :, :], 1.0)


def dft_views(m):
    flat = m.z[:, :, :, :].rearrange("p g t n -> p (g t n)")
    W = KC * D
    return [flat[:, i * W:(i + 1) * W].rearrange("p (c n) -> p c n", c=KC) for i in range(7)]


def projection(nc, m, layer, q_dram, k_dram, loads=None):
    shared = layer == 1
    wq, wk, wv = (m.wq1, m.wk1, m.wv1) if shared else (m.wq0, m.wk0, m.wv0)
    KB = 1 if shared else KC
    KR = DH if shared else P
    VN = DH if shared else D
    XT_BANK, Q_BANK, K_BANK, V_BANK = 0, 2, 4, 6
    with ExitStack() as ctx:
        def sem(name):
            return ctx.enter_context(nc.semaphore(f"{name}_{layer}"))

        stats_ready, rstd_ready, xln_ready = sem("stats_ready"), sem("rstd_ready"), sem("xln_ready")
        xt_full, xt_ready = sem("xt_full"), sem("xt_ready")
        v_full, v_copied = sem("v_full"), sem("v_copied")
        full = [sem("q_full"), sem("k_full")]
        high = [sem("q_high"), sem("k_high")]
        rest = [sem("q_rest"), sem("k_rest")]
        middle = [sem("q_middle"), sem("k_middle")]
        low = [sem("q_low"), sem("k_low")]
        stored = [sem("q_stored"), sem("k_stored")]
        dve_steps, pool_steps = sem("dve_steps"), sem("pool_steps")

        def cut(start, words):
            return m.scratch[:, start:start + words]

        W = CHUNK * D
        xln = [cut(i * W, W).rearrange("p (t d) -> p t d", t=CHUNK) for i in range(2)]
        xt = [cut((2 + i) * W, W).rearrange("p (c t) -> p c t", c=KC) for i in range(2)]
        rests = [cut((4 + i) * W, W).rearrange("p (c t) -> p c t", c=KC) for i in range(2)]
        parts = [cut(6 * W + i * W * PARTS // 2, W * PARTS // 2).bitcast(BF16).rearrange(
            "p (s c t) -> p s c t", s=PARTS, c=KC) for i in range(2)]
        bn = ctx.enter_context(nc.sbuf_tensor(f"bn_{layer}", [P, CHUNK, 6], F32))
        mv = ctx.enter_context(nc.sbuf_tensor(f"mv_{layer}", [P, 2, CHUNK, 2], F32))
        var = ctx.enter_context(nc.sbuf_tensor(f"var_{layer}", [P, CHUNK], F32))
        rstd = ctx.enter_context(nc.sbuf_tensor(f"rstd_{layer}", [P, 2, CHUNK], F32))

        blocks, rows = (KC, KB), (P, KR)
        banks = (Q_BANK, K_BANK)

        def in_psum(i):
            return m.psum[0:rows[i], banks[i]:banks[i] + blocks[i], :]

        def at(J, u):
            return 2 * J + u, u % 2, J + u // 2, u % 2

        block = ctx.enter_context(nc.Block())

        @block.sync
        def _(sp):
            def body(J, u):
                if not on(J, u):
                    return
                c, _, b, qh = at(J, u)
                for i, dram in enumerate((q_dram, k_dram)):
                    sp.wait_ge(low[i], c + 1)
                    dst = dram[bass.ds(b, 1), :, :, qh * CT:(qh + 1) * CT]
                    if i == 1 and shared:
                        sp.dma_start(dst.rearrange("o s r t -> r (o s) t"),
                                     parts[i][0:KR, :, 0, :]).then_inc(stored[i], 16)
                    else:
                        sp.dma_start(dst.rearrange("o s (c r) t -> r (o s c) t", r=P),
                                     parts[i][:, :, :, :].rearrange("p s c t -> p (s c) t")).then_inc(stored[i], 16)

            chunk_loop(sp, body, 0)
            sp.wait_ge(stored[0], 16 * CHUNKS)
            sp.wait_ge(stored[1], 16 * CHUNKS)
            if loads:
                sp.wait_ge(loads.rest, loads.n_rest)

        @block.gpsimd
        def _(pool):
            chain = Chain(pool, pool_steps)

            def body(J, u):
                if not on(J, u, 2):
                    return
                c, nxt = 2 * J + u, u % 2
                pool.wait_ge(stats_ready, c + 3)
                chain.then(pool.tensor_tensor(var[:, :], mv[:, nxt, :, 1], m.eps[:, :], ALU.add))
                pool.tensor_tensor(rstd[:, nxt, :], var[:, :], m.minus_half[:, :], ALU.pow).then_inc(rstd_ready, 1)

            chunk_loop(pool, body, -2, chain=chain, per_chunk=1)

        @block.vector
        def _(dve):
            chain = Chain(dve, dve_steps)

            def body(J, u):
                c = 2 * J + u
                if on(J, u, 1):
                    nxt = (u + 1) % 2
                    dve.wait_ge(rstd_ready, c + 2)
                    ge(dve, xt_ready, c)
                    for t in range(CHUNK):
                        ins = dve.tensor_scalar(xln[nxt][:, t, :], m.x[:, bass.ds((c + 1) * CHUNK + t, 1), :],
                                                mv[:, nxt, t, 0:1], rstd[:, nxt, t:t + 1], ALU.subtract, ALU.mult)
                    ins.then_inc(xln_ready, 1)
                    if not shared:
                        dve.tensor_copy(m.mean[:, bass.ds((c + 1) * CHUNK, CHUNK)], mv[:, nxt, :, 0])
                        dve.tensor_copy(m.rstd[:, bass.ds((c + 1) * CHUNK, CHUNK)], rstd[:, nxt, :])
                if on(J, u, 2):
                    if loads and isinstance(J, int):
                        sem, n = (loads.x_first[c + 2], 16) if c + 2 < 2 else (loads.x_rest, 16 * (CHUNKS - 2))
                        dve.wait_ge(sem, n)
                    if loads and not isinstance(J, int):
                        dve.wait_ge(loads.x_rest, 16 * (CHUNKS - 2))
                    for t in range(CHUNK):
                        ins = dve.bn_stats(bn[:, t, :], m.x[:, bass.ds((c + 2) * CHUNK + t, 1), :])
                    chain.then(ins, bare=True)
                    for t in range(CHUNK):
                        ins = dve.bn_aggr(mv[:, u % 2, t, :], bn[:, t, :])
                    ins.then_inc(stats_ready, 1)
                if not on(J, u):
                    return
                for i in range(2):
                    r = slice(0, rows[i])
                    dve.wait_ge(high[i], c + 1)
                    dve.tensor_tensor(rests[i][r, 0:blocks[i], :], in_psum(i), parts[i][r, 0, 0:blocks[i], :],
                                      ALU.subtract).then_inc(rest[i], 1)
                    dve.wait_ge(middle[i], c + 1)
                    dve.tensor_tensor(parts[i][r, 2, 0:blocks[i], :], rests[i][r, 0:blocks[i], :],
                                      parts[i][r, 1, 0:blocks[i], :], ALU.subtract).then_inc(low[i], 1)

            chunk_loop(dve, body, -2, chain=chain, per_chunk=1)

        @block.scalar
        def _(act):
            def take_high(i, c):
                act.wait_ge(full[i], c + 1)
                ge(act, stored[i], 16 * c)
                r = slice(0, rows[i])
                act.copy(parts[i][r, 0, 0:blocks[i], :], in_psum(i)).then_inc(high[i], 1)

            def take_middle(i, c):
                act.wait_ge(rest[i], c + 1)
                r = slice(0, rows[i])
                act.copy(parts[i][r, 1, 0:blocks[i], :], rests[i][r, 0:blocks[i], :]).then_inc(middle[i], 1)

            def body(J, u):
                c, par, b, qh = at(J, u)
                if on(J, u):
                    take_high(0, c)
                    take_middle(0, c)
                    take_high(1, c)
                if on(J, u, 1):
                    act.wait_ge(xt_full, c + 2)
                    ge(act, v_full, c)
                    act.copy(xt[(u + 1) % 2], m.psum[:, XT_BANK:XT_BANK + 2, :]).then_inc(xt_ready, 1)
                if not on(J, u):
                    return
                take_middle(1, c)
                act.wait_ge(v_full, c + 1)
                v_new = m.psum[:, V_BANK:V_BANK + 2, :].rearrange("p b (t n) -> p (b t) n", n=D)
                if shared:
                    dst = m.v[:, bass.ds(b * (GROUPS // B), 1), qh * CHUNK:(qh + 1) * CHUNK, 0:DH]
                    act.copy(dst.rearrange("p o t n -> p (o t) n"), v_new[:, :, 0:DH]).then_inc(v_copied, 1)
                    return
                for hg in range(GROUPS // B):
                    dst = m.v[:, bass.ds(b * (GROUPS // B) + hg, 1), qh * CHUNK:(qh + 1) * CHUNK, :]
                    ins = act.copy(dst.rearrange("p o t n -> p (o t) n"), v_new[:, :, hg * GF:(hg + 1) * GF])
                ins.then_inc(v_copied, 1)

            chunk_loop(act, body, -1)

        @block.tensor
        def _(pe):
            def body(J, u):
                c, par, _, _ = at(J, u)
                nxt = (u + 1) % 2
                if on(J, u):
                    pe.wait_ge(xt_ready, c + 1)
                    for i, w in enumerate((wq, wk)):
                        ge(pe, rest[i], c)
                        for blk in range(blocks[i]):
                            for k in range(KC):
                                ins = pe.matmul(m.psum[0:rows[i], banks[i] + blk, :],
                                                w[:, k, blk * P:blk * P + rows[i]], xt[par][:, k, :],
                                                start=(k == 0), stop=(k == KC - 1))
                        ins.then_inc(full[i], 1)
                if on(J, u, 1):
                    pe.wait_ge(xln_ready, c + 2)
                    ge(pe, xt_ready, c + 1)
                    for t in range(CHUNK):
                        for k in range(KC):
                            ins = pe.transpose(m.psum[:, XT_BANK + k, t * P:(t + 1) * P],
                                               xln[nxt][:, t, k * P:(k + 1) * P], m.ident[:, :])
                    ins.then_inc(xt_full, 1)
                if not on(J, u):
                    return
                ge(pe, v_copied, c)
                for t in range(CHUNK):
                    for k in range(KC):
                        ins = pe.matmul(m.psum[:, V_BANK + t // 2, (t % 2) * D:(t % 2) * D + VN],
                                        xt[par][:, k, t * P:(t + 1) * P], wv[:, k, :],
                                        start=(k == 0), stop=(k == KC - 1))
                ins.then_inc(v_full, 1)

            if loads:
                pe.wait_ge(loads.projection, loads.n_projection)
            chunk_loop(pe, body, -1)


def attention(nc, m, layer, q_dram, k_dram, loads=None):
    shared = layer == 1
    S_BANK, ST_BANK, ST_BANKS, PV_BANK = 0, 4, 3, 7
    P_SLOTS = 4
    UNITS = HG * QT
    with ExitStack() as ctx:
        def sem(name):
            return ctx.enter_context(nc.semaphore(f"{name}_{layer}"))

        q_loaded = [sem(f"q_loaded{i}") for i in range(4)]
        k_loaded = [sem(f"k_loaded{i}") for i in range(2)]
        v_ready = sem("v_ready")
        item_full, item_done = sem("item_full"), sem("item_done")
        parts_ready = sem("max_parts_ready")
        max_loaded = [sem(f"max_loaded{i}") for i in range(2)]
        st_full, exp_done, pv_done = sem("st_full"), sem("exp_done"), sem("pv_done")
        zt_ready = sem("zt_ready")
        dve_steps = sem("dve_steps_att")

        probs = [m.scratch[:, i * HG * HQ:(i + 1) * HG * HQ].rearrange("p (h q) -> p h q", h=HG)
                 for i in range(P_SLOTS)]
        off = P_SLOTS * HG * HQ
        zt = [m.scratch[:, off + i * HQ:off + (i + 1) * HQ] for i in range(2)]
        minus_max = ctx.enter_context(nc.sbuf_tensor(f"minus_max_{layer}", [P, 2, UNITS], F32))
        max_parts = ctx.enter_context(nc.sbuf_tensor(f"max_parts_{layer}", [UNITS, 2, PARTS, P], BF16))
        max_rest = ctx.enter_context(nc.sbuf_tensor(f"max_rest_{layer}", [UNITS, P], F32))
        inverse = ctx.enter_context(nc.sbuf_tensor(f"inverse_{layer}", [P, 2, UNITS], F32))

        transforms, scaled, folded = sem("transforms"), sem("scaled"), sem("folded")
        if loads:
            cos, sin, minus_cos, w_real, w_imag, a_t, nb_t = dft_views(m)
            FOLD_BANKS = (ST_BANK, ST_BANK + 1, ST_BANK + 2)

        def fold_step(pe, k):
            which, j, i, kc = k // 8, k // 4 % 2, k // 2 % 2, k % 2
            pairs = (((w_real, cos), (w_imag, sin)), ((w_real, sin), (w_imag, minus_cos)), ((a_t, cos), (nb_t, sin)))
            left, right = pairs[which][i]
            if k == 0:
                pe.wait_ge(loads.dft, loads.n_dft)
            if k == 16:
                pe.wait_ge(scaled, 2)
            ins = pe.matmul(m.psum[:, FOLD_BANKS[which], j * D:(j + 1) * D], left[:, kc, j * P:(j + 1) * P],
                            right[:, kc, :], start=(i == 0 and kc == 0), stop=(i == 1 and kc == KC - 1))
            if k % 8 == 7:
                ins.then_inc(transforms, 1)

        def fold_copies(act):
            for i, (dst, scale) in enumerate(((a_t, 1.0 / D), (nb_t, 1.0 / D), (m.fold[:, :, :], 1.0))):
                act.wait_ge(transforms, i + 1)
                act.activation(dst, m.psum[:, FOLD_BANKS[i], :].rearrange("p (c n) -> p c n", c=KC), ACT.Copy,
                               scale=scale).then_inc(scaled if i < 2 else folded, 1)

        def items(n):
            out = []
            for s in range(KT):
                second = s < KT // 2
                half = n + 1 if second else n + 2
                if 0 <= half < HALVES:
                    out += [(s, "unit", UNITS // 2 * second + 2 * (s % (KT // 2)) + i) for i in range(2)]
                if s == 2 and 0 <= n - 1 < HALVES:
                    out.append((s, "out", None))
                if s == 5 and 0 <= n + 1 < HALVES:
                    out.append((s, "max", None))
            return out

        FIRST, LAST = -2, HALVES
        LOOP_FROM, PER = 1, 4
        LOOPS = (HALVES - 2 - LOOP_FROM) // PER
        starts, k = {}, 0
        for n in range(FIRST, LAST + 1):
            starts[n] = k
            k += len(items(n))
        FULL = len(items(LOOP_FROM))

        def start_of(J, r):
            return starts[r] if isinstance(J, int) else J * (PER * FULL) + starts[r]

        def loop(engine, period, chain=None, per_period=0):
            for n in range(FIRST, LOOP_FROM):
                period(0, n)
            before = chain.count if chain else 0
            with engine.Fori(0, LOOPS) as J:
                if chain:
                    chain.base, chain.count = J * (PER * per_period), before
                for r in range(LOOP_FROM, LOOP_FROM + PER):
                    period(J, r)
                assert not chain or chain.count == before + PER * per_period
            if chain:
                chain.base = (LOOPS - 1) * PER * per_period
            for n in range(LOOP_FROM + PER * LOOPS, LAST + 1):
                period(0, n)

        def ring(J, r):
            base = start_of(J, r)
            shape = items(r)
            return [(s, kind, unit, base + i, (starts[r] + i) % 2) for i, (s, kind, unit) in enumerate(shape)]

        def out_item(r):
            return [i for i, it in enumerate(items(r)) if it[1] == "out"][0]

        block = ctx.enter_context(nc.Block())

        @block.sync
        def _(sp):
            def of_group(dram, g):
                b, hg = g // (GROUPS // B), g % (GROUPS // B)
                return dram[bass.ds(b, 1), :, bass.ds(hg * GF, GF), :].rearrange("o s (h d) t -> d (o s) h t", h=HG)

            def load_q(J, r):
                slot = r % 4
                qh = r % 2
                src = of_group(q_dram, 2 * J + r // 2)[:, :, :, qh * HQ:(qh + 1) * HQ]
                for j, part in enumerate(Q_PARTS):
                    sp.dma_start(m.q_stack[j * DH:(j + 1) * DH, slot, :, :],
                                 src[:, part, :, :]).then_inc(q_loaded[slot], 16)

            def load_k(J, r):
                slot = r % 2
                if shared:
                    b = (2 * J + r) // (GROUPS // B)
                    src = k_dram[bass.ds(b, 1), :, :, :].rearrange("o s (h d) t -> d (o s) h t", h=1)
                else:
                    src = of_group(k_dram, 2 * J + r)
                for j, part in enumerate(K_PARTS):
                    one = src[:, part, :, :]
                    if shared:
                        one = one.to_broadcast([DH, HG, S])
                    sp.dma_start(m.k_stack[j * DH:(j + 1) * DH, slot, :, :], one).then_inc(k_loaded[slot], 16)

            def period(J, r):
                n = PER * J + r
                static = isinstance(J, int)
                ge(sp, st_full, n * KT * HG)
                if r == FIRST:
                    load_q(0, 0)
                    load_k(0, 0)
                    load_k(0, 1)
                if not static or n + 3 < HALVES:
                    load_q(J, r + 3)
                if r % 2 == 0 and (not static or (n >= 2 and n // 2 + 1 < GROUPS)):
                    load_k(J, r // 2 + 1)
                if not static or 0 <= n + 1 < HALVES:
                    nxt = (r + 1) % 2
                    sp.wait_ge(parts_ready, n + 2)
                    for s in range(PARTS):
                        dst = m.q_stack[ROWS + s:ROWS + s + 1, (r + 1) % 4, :, :]
                        sp.dma_start(dst.rearrange("o h (t q) -> o (h t) q", q=P),
                                     max_parts[:, nxt, s, :]).then_inc(max_loaded[nxt], 16)

            loop(sp, period)

        @block.gpsimd
        def _(pool):
            def v_copy(J, r):
                ge(pool, pv_done, (2 * J + r - 1) * 2 * KT)
                if shared:
                    b = (2 * J + r) // (GROUPS // B)
                    src = m.v[:, bass.ds(b * (GROUPS // B), 1), :, 0:DH].rearrange("p o t (h d) -> p (o t) h d", h=1)
                    src = src.to_broadcast([P, KT, HG, DH])
                else:
                    src = m.v[:, bass.ds(2 * J + r, 1), :, :].rearrange("p o t (h d) -> p (o t) h d", h=HG)
                pool.tensor_copy(m.v_group[:, r % 2, :, :, 0:DH], src).then_inc(v_ready, 1)

            v_copy(0, 0)
            v_copy(0, 1)
            with pool.Fori(1, GROUPS // 2) as J:
                v_copy(J, 0)
                v_copy(J, 1)

        @block.tensor
        def _(pe):
            def item(J, r, kind, unit, index, slot, half_r, last_unit_in_front=False):
                ge(pe, item_done, index if kind == "max" and last_unit_in_front else index - 1)
                banks = m.psum[:, S_BANK + 2 * slot:S_BANK + 2 * slot + 2, :]
                if kind == "unit":
                    h, t = unit // QT, unit % QT
                    if unit == 0:
                        pe.wait_ge(q_loaded[half_r % 4], 96 * (J + half_r // 4 + 1))
                        pe.wait_ge(k_loaded[half_r // 2 % 2], 96 * (J + half_r // 4 + 1))
                    for kh in range(2):
                        ins = pe.matmul(banks[:, kh, :], m.q_stack[0:ROWS, half_r % 4, h, t * P:(t + 1) * P],
                                        m.k_stack[0:ROWS, half_r // 2 % 2, h, kh * 512:(kh + 1) * 512],
                                        start=True, stop=True)
                elif kind == "max":
                    ins = pe.transpose(banks[0:UNITS, 0, 0:P], minus_max[:, half_r % 2, :], m.ident[:, :])
                else:
                    pe.wait_ge(zt_ready, PER * J + r)
                    for t in range(QT):
                        ins = pe.transpose(banks[:, 0, t * P:(t + 1) * P], zt[half_r % 2][:, t * P:(t + 1) * P],
                                           m.ident[:, :])
                ins.then_inc(item_full, 1)

            def pv(J, r, s):
                n = PER * J + r
                pe.wait_ge(exp_done, n * (KT * HG) + HG * (s + 1))
                if s == 0:
                    pe.wait_ge(v_ready, n // 2 + 1 if isinstance(J, int) else 2 * J + r // 2 + 1)
                    ge(pe, zt_ready, n)
                for h in range(HG):
                    ins = pe.matmul(m.psum[h * VW:(h + 1) * VW, PV_BANK, :], m.v_group[:, r // 2 % 2, s, h, :],
                                    probs[s % P_SLOTS][:, h, :], start=(s == 0), stop=(s == KT - 1),
                                    tile_position=(0, h * VW))
                ins.then_inc(pv_done, 1)

            def st(J, r, s, h):
                n = PER * J + r
                i = s * HG + h
                if loads and r == 0 and i == 0:
                    pe.wait_ge(folded, 1)
                if i == 0:
                    pe.wait_ge(max_loaded[r % 2], 48 * (2 * J + r // 2 + 1))
                last = i - ST_BANKS if i >= ST_BANKS else {0: -2, 1: -1, 2: -3}[i]
                ge(pe, exp_done, n * (KT * HG) + last + 1)
                pe.matmul(m.psum[:, ST_BANK + i % ST_BANKS, :],
                          m.k_stack[0:ROWS + PARTS, r // 2 % 2, h, s * P:(s + 1) * P],
                          m.q_stack[0:ROWS + PARTS, r % 4, h, :], start=True, stop=True).then_inc(st_full, 1)

            def period(J, r):
                on = 0 <= r < HALVES
                todo = ring(J, r)
                for s in range(KT):
                    here = [x for x in todo if x[0] == s]
                    half_r = r + 1 if s < KT // 2 else r + 2
                    units = [x for x in here if x[1] == "unit"]
                    for pair in range(2):
                        if on:
                            st(J, r, s, 2 * pair)
                            st(J, r, s, 2 * pair + 1)
                        if units:
                            _, kind, unit, index, slot = units[pair]
                            item(J, r, kind, unit, index, slot, half_r)
                            if loads and r < 0:
                                fold_step(pe, unit if half_r == 0 else UNITS + unit)
                    if s >= 1 and on:
                        pv(J, r, s - 1)
                    if s == 0 and 0 <= r - 1 < HALVES:
                        pv(J, r - 1, KT - 1)
                    for _, kind, unit, index, slot in here:
                        if kind == "max":
                            front = todo[[x[1] for x in todo].index("max") - 1]
                            item(J, r, kind, unit, index, slot, r + 1, front[0] < KT // 2)
                        if kind == "out":
                            item(J, r, kind, unit, index, slot, r - 1)

            loop(pe, period)

        @block.scalar
        def _(act):
            if loads:
                fold_copies(act)

            def take_out(J, r):
                n = PER * J + r
                act.wait_ge(pv_done, n * KT)
                if not (isinstance(J, int) and n - 3 < 0):
                    act.wait_ge(item_done, start_of(J, r) - 2 * FULL + out_item(LOOP_FROM) + 1
                                if not isinstance(J, int) else starts[n - 2] + out_item(n - 2) + 1)
                act.copy(zt[(r - 1) % 2], m.psum[:, PV_BANK, :]).then_inc(zt_ready, 1)

            def period(J, r):
                n = PER * J + r
                if not 0 <= r < HALVES:
                    if r == HALVES:
                        take_out(J, r)
                    return
                for s in range(KT):
                    ge(act, pv_done, n * KT + s - P_SLOTS + 1)
                    for h in range(HG):
                        i = s * HG + h
                        act.wait_ge(st_full, n * (KT * HG) + i + 1)
                        act.activation(probs[s % P_SLOTS][:, h, :], m.psum[:, ST_BANK + i % ST_BANKS, :], ACT.Exp,
                                       scale=SCALE).then_inc(exp_done, 1)
                        if s == 1 and h == 0 and r - 1 >= 0:
                            take_out(J, r)

            loop(act, period)

        @block.vector
        def _(dve):
            chain = Chain(dve, dve_steps)

            def period(J, r):
                for s, kind, unit, index, slot in ring(J, r):
                    banks = m.psum[:, S_BANK + 2 * slot:S_BANK + 2 * slot + 2, :]
                    dve.wait_ge(item_full, index + 1)
                    if kind == "unit":
                        par = (r + 1 if s < KT // 2 else r + 2) % 2
                        dve.tensor_reduce(minus_max[:, par, unit:unit + 1], banks, AX.XY, ALU.max,
                                          negate=True).then_inc(item_done, 1)
                    elif kind == "max":
                        par = (r + 1) % 2
                        n = PER * J + r
                        ge(dve, max_loaded[par], 48 * (2 * J + (r + 1) // 2))
                        row = banks[0:UNITS, 0, 0:P]
                        chain.then(dve.tensor_copy(max_parts[:, par, 0, :], row))
                        ins = dve.tensor_tensor(max_rest[:, :], row, max_parts[:, par, 0, :], ALU.subtract)
                        ins.then_inc(item_done, 1)
                        dve.wait_ge(item_done, index + 1)
                        chain.then(dve.tensor_copy(max_parts[:, par, 1, :], max_rest[:, :]))
                        dve.tensor_tensor(max_parts[:, par, 2, :], max_rest[:, :], max_parts[:, par, 1, :],
                                          ALU.subtract).then_inc(parts_ready, 1)
                    else:
                        sums = banks[:, 0, :].rearrange("p (g w) -> p g w", w=VW)
                        par = (r - 1) % 2
                        chain.then(dve.reciprocal(inverse[:, par, :], sums[:, :, DH]))
                        qh = (r - 1) % 2
                        g = 2 * J + (r - 1) // 2
                        dst = m.z[:, bass.ds(g, 1), qh * QT:(qh + 1) * QT, :].rearrange(
                            "p o t (h d) -> p (o t h) d", d=DH)
                        inv = inverse[:, par, :].rearrange("p (g o) -> p g o", o=1).to_broadcast([P, UNITS, DH])
                        dve.tensor_tensor(dst, sums[:, :, 0:DH], inv, ALU.mult).then_inc(item_done, 1)

            loop(dve, period, chain, 3)


def mixture(nc, m):
    ZT_BANK, U_BANK, XT_BANK, GATE_BANK, E_BANK = 0, 1, 2, 3, 4
    PAIRS = TILES // 2
    SETS = EXPERTS // 2
    W = 2 * D
    GATE_STEP = 16
    with ExitStack() as ctx:
        def sem(name):
            return ctx.enter_context(nc.semaphore(f"mix_{name}"))

        zs_ready, zt_full, zt_ready, u_full, u_ready = (
            sem("zs_ready"), sem("zt_full"), sem("zt_ready"), sem("u_full"), sem("u_ready"))
        u_stats, u_rstd, x1_stats, x1_rstd = sem("u_stats"), sem("u_rstd"), sem("x1_stats"), sem("x1_rstd")
        xln_ready, xt_full, xt_ready = sem("xln_ready"), sem("xt_full"), sem("xt_ready")
        gate_full, shifted, exps_ready, weights_ready = (
            sem("gate_full"), sem("shifted"), sem("exps_ready"), sem("weights_ready"))
        wt_full, wt_ready, bias_full, bias_ready = sem("wt_full"), sem("wt_ready"), sem("bias_full"), sem("bias_ready")
        set_full, set_read, even_added = sem("set_full"), sem("set_read"), sem("even_added")
        first_normal = sem("first_normal")
        y_stats, y_rstd = sem("y_stats"), sem("y_rstd")
        dve_steps, pool_steps = sem("dve_steps"), sem("pool_steps")

        def by_tile(start):
            return m.scratch[:, start * W:(start + 1) * W].rearrange("p (t d) -> p t d", t=2)

        def by_chunk(start):
            return m.scratch[:, start * W:(start + 1) * W].rearrange("p (c t q) -> p c t q", c=KC, t=2)

        zs, xln = [by_tile(0), by_tile(1)], [by_tile(2), by_tile(3)]
        zt, xt = [by_chunk(4), by_chunk(5)], [by_chunk(6), by_chunk(7)]
        u, normal, first_ln, even, odd, y = (by_tile(i) for i in range(8, 14))
        y_bias = [by_tile(14), by_tile(15)]

        def sb(name, shape, dt=F32):
            return ctx.enter_context(nc.sbuf_tensor(f"mix_{name}", shape, dt))

        bn = [sb(f"bn{i}", [P, 2, 6]) for i in range(3)]
        mv = [sb(f"mv{i}", [P, 2, 2]) for i in range(3)]
        var = [sb(f"var{i}", [P, 2]) for i in range(3)]
        rstd = [sb(f"rstd{i}", [P, 2]) for i in range(3)]
        logits, top_logits = sb("logits", [P, 2, GATES]), sb("top_logits", [P, 2, 8])
        exps, exps_sum, inverse = sb("exps", [P, 2, GATES]), sb("exps_sum", [P, 2]), sb("inverse", [P, 2])
        gates, top, where = sb("gates", [P, 2, GATES]), sb("top", [P, 2, 8]), sb("where", [P, 2, 8], U32)
        index, real, kept, share = (sb(name, [P, 2, 2]) for name in ("index", "real", "kept", "share"))
        total = sb("total", [P, 2])
        picks = sb("picks", [P, 2, 2, EXPERTS])
        weights = sb("weights", [P, 2, 2, EXPERTS])
        wt = sb("wt", [EXPERTS, 2, 2, P])

        def over(ap, n):
            return ap.rearrange("p (a o) -> p a o", o=1).to_broadcast([ap.shape[0], ap.shape[1], n])

        def loop(engine, body, chain=None, per_pair=0):
            first, lead, loops = -3, 2, (PAIRS - 6) // 2
            for p in range(first, lead):
                body(0, p)
            before = chain.count if chain else 0
            with engine.Fori(lead // 2, lead // 2 + loops) as J:
                if chain:
                    chain.base, chain.count = (J - lead // 2) * (2 * per_pair), before
                body(J, 0)
                body(J, 1)
                assert not chain or chain.count == before + 2 * per_pair, (chain.count, before)
            if chain:
                chain.base = (loops - 1) * 2 * per_pair
            for p in range(lead + 2 * loops, PAIRS + 1):
                body(0, p)

        def on(J, r, by):
            return not isinstance(J, int) or 0 <= r + by < PAIRS

        block = ctx.enter_context(nc.Block())

        @block.gpsimd
        def _(pool):
            chain = Chain(pool, pool_steps)

            def take_rstd(k, stats, ready, count):
                pool.wait_ge(stats, count)
                chain.then(pool.tensor_tensor(var[k][:, :], mv[k][:, :, 1], m.eps[:, 0:2], ALU.add))
                pool.tensor_tensor(rstd[k][:, :], var[k][:, :], m.minus_half[:, 0:2], ALU.pow).then_inc(ready, 1)

            def body(J, r):
                p = 2 * J + r
                if on(J, r, -1):
                    take_rstd(1, y_stats, y_rstd, p)
                if on(J, r, 3):
                    pair = p + 3
                    b, qt = pair // (KT // 2), pair % (KT // 2) * 2
                    ge(pool, zt_full, pair - 1)
                    for t in range(2):
                        src = m.z[:, bass.ds(b * (GROUPS // B), GROUPS // B), bass.ds(qt + t, 1), :]
                        ins = pool.tensor_copy(zs[(r + 3) % 2][:, t, :].rearrange("p (g n) -> p g n", g=GROUPS // B),
                                               src.rearrange("p g o n -> p g (o n)"))
                    ins.then_inc(zs_ready, 1)
                if on(J, r, 2):
                    take_rstd(0, u_stats, u_rstd, p + 3)
                    take_rstd(2, x1_stats, x1_rstd, p + 3)

            loop(pool, body, chain, 3)

        @block.tensor
        def _(pe):
            def experts(p, par, t, sets):
                for s in sets:
                    use = 2 * SETS * p + SETS * t + s
                    ge(pe, set_read, use - SETS + 1)
                    for half in range(2):
                        for k in range(KC):
                            ins = pe.matmul(m.psum[:, E_BANK + s, half * D:(half + 1) * D], xt[par][:, k, t, :],
                                            m.expert_w[:, k, 2 * s + half, :], start=(k == 0), stop=(k == KC - 1))
                    ins.then_inc(set_full, 1)

            def turn(bank, src):
                for k in range(KC):
                    for t in range(2):
                        ins = pe.transpose(m.psum[:, bank, (2 * k + t) * P:(2 * k + t + 1) * P],
                                           src[:, t, k * P:(k + 1) * P], m.ident[:, :])
                return ins

            def body(J, r):
                p, par, nxt = 2 * J + r, r % 2, (r + 1) % 2
                if on(J, r, 1):
                    pe.wait_ge(xln_ready, p + 2)
                    ge(pe, bias_ready, p + 1)
                    turn(XT_BANK, xln[nxt]).then_inc(xt_full, 1)
                if on(J, r, 2):
                    pe.wait_ge(zs_ready, p + 3)
                    ge(pe, zt_ready, p + 2)
                    turn(ZT_BANK, zs[par]).then_inc(zt_full, 1)
                if on(J, r, 0):
                    experts(p, par, 0, range(0, 2))
                if on(J, r, 1):
                    pe.wait_ge(xt_ready, p + 2)
                    ge(pe, wt_ready, p + 1)
                    for t in range(2):
                        for k in range(KC):
                            ins = pe.matmul(m.psum[:, GATE_BANK, t * GATE_STEP:t * GATE_STEP + GATES],
                                            xt[nxt][:, k, t, :], m.gate_w[:, k, :], start=(k == 0), stop=(k == KC - 1))
                    ins.then_inc(gate_full, 1)
                if on(J, r, 2):
                    pe.wait_ge(zt_ready, p + 3)
                    ge(pe, u_ready, p + 2)
                    for t in range(2):
                        for k in range(KC):
                            ins = pe.matmul(m.psum[:, U_BANK, t * D:(t + 1) * D], zt[par][:, k, t, :], m.wout[:, k, :],
                                            start=(k == 0), stop=(k == KC - 1))
                    ins.then_inc(u_full, 1)
                if on(J, r, 0):
                    experts(p, par, 0, range(2, SETS))
                    experts(p, par, 1, range(0, 2))
                if on(J, r, 1):
                    pe.wait_ge(weights_ready, p + 2)
                    for t in range(2):
                        ins = pe.transpose(m.psum[0:EXPERTS, GATE_BANK, (1 + t) * P:(2 + t) * P], weights[:, nxt, t, :],
                                           m.ident[:, :])
                    ins.then_inc(wt_full, 1)
                if on(J, r, 0):
                    experts(p, par, 1, range(2, 3))
                if on(J, r, 1):
                    pe.wait_ge(wt_ready, p + 2)
                    for t in range(2):
                        ins = pe.matmul(m.psum[:, XT_BANK, t * D:(t + 1) * D], wt[:, nxt, t, :], m.expert_b[:, :],
                                        start=True, stop=True)
                    ins.then_inc(bias_full, 1)
                if on(J, r, 0):
                    experts(p, par, 1, range(3, SETS))

            loop(pe, body)

        @block.scalar
        def _(act):
            def flat(ap):
                return ap.rearrange("p a b c -> p (a b c)") if len(ap.shape) == 4 else ap.rearrange("p a b -> p (a b)")

            def body(J, r):
                p, par, nxt = 2 * J + r, r % 2, (r + 1) % 2
                if on(J, r, 1):
                    act.wait_ge(xt_full, p + 2)
                    ge(act, set_full, 2 * SETS * p)
                    act.copy(flat(xt[nxt]), m.psum[:, XT_BANK, :]).then_inc(xt_ready, 1)
                if on(J, r, 2):
                    act.wait_ge(zt_full, p + 3)
                    ge(act, u_full, p + 1)
                    act.copy(flat(zt[par]), m.psum[:, ZT_BANK, :]).then_inc(zt_ready, 1)
                if on(J, r, 1):
                    act.wait_ge(shifted, p + 2)
                    act.activation(exps[:, :, :], logits[:, :, :], ACT.Exp).then_inc(exps_ready, 1)
                    act.wait_ge(wt_full, p + 2)
                    ge(act, bias_full, p)
                    act.copy(wt[:, nxt, :, :].rearrange("e t q -> e (t q)"),
                             m.psum[0:EXPERTS, GATE_BANK, P:3 * P]).then_inc(wt_ready, 1)
                    act.wait_ge(bias_full, p + 2)
                    ge(act, set_read, 2 * SETS * p)
                    act.copy(flat(y_bias[nxt]), m.psum[:, XT_BANK, :]).then_inc(bias_ready, 1)

            loop(act, body)

        @block.vector
        def _(dve):
            chain = Chain(dve, dve_steps)
            step = chain.then

            def x_pair(pair):
                return m.x[:, bass.ds(2 * pair, 2), :]

            def statistics(k, src, done):
                dve.bn_stats(bn[k][:, 0, :], src(0))
                step(dve.bn_stats(bn[k][:, 1, :], src(1)), bare=True)
                dve.bn_aggr(mv[k][:, 0, :], bn[k][:, 0, :])
                dve.bn_aggr(mv[k][:, 1, :], bn[k][:, 1, :]).then_inc(done, 1)

            def normalise(k, out, src):
                for t in range(2):
                    ins = dve.tensor_scalar(out[:, t, :], src(t), mv[k][:, t, 0:1], rstd[k][:, t:t + 1],
                                            ALU.subtract, ALU.mult)
                return ins

            def gate_logits(p):
                dve.wait_ge(gate_full, p + 2)
                new = m.psum[:, GATE_BANK, 0:2 * GATE_STEP].rearrange("p (t n) -> p t n", t=2)[:, :, 0:GATES]
                gate_b = m.gate_b[:, :].rearrange("p (o n) -> p o n", o=1).to_broadcast([P, 2, GATES])
                step(dve.tensor_tensor(logits[:, :, :], new, gate_b, ALU.add), bare=True)
                dve.max(top_logits[:, 0, :], logits[:, 0, :])
                step(dve.max(top_logits[:, 1, :], logits[:, 1, :]))
                dve.tensor_tensor(logits[:, :, :], logits[:, :, :], over(top_logits[:, :, 0], GATES),
                                  ALU.subtract).then_inc(shifted, 1)

            def gate_weights(p, nxt):
                dve.wait_ge(exps_ready, p + 2)
                step(dve.tensor_reduce(exps_sum[:, :], exps[:, :, :], AX.X, ALU.add))
                step(dve.reciprocal(inverse[:, :], exps_sum[:, :]))
                step(dve.tensor_tensor(gates[:, :, :], exps[:, :, :], over(inverse[:, :], GATES), ALU.mult), bare=True)
                dve.max(top[:, 0, :], gates[:, 0, :])
                step(dve.max(top[:, 1, :], gates[:, 1, :]), bare=True)
                dve.max_index(where[:, 0, :], top[:, 0, :], gates[:, 0, :])
                step(dve.max_index(where[:, 1, :], top[:, 1, :], gates[:, 1, :]))
                step(dve.tensor_copy(index[:, :, :], where[:, :, 0:2]))
                step(dve.tensor_scalar(real[:, :, :], index[:, :, :], float(EXPERTS), None, ALU.is_lt))
                step(dve.tensor_tensor(kept[:, :, :], top[:, :, 0:2], real[:, :, :], ALU.mult))
                step(dve.tensor_reduce(total[:, :], kept[:, :, :], AX.X, ALU.add))
                step(dve.scalar_tensor_tensor(out=total[:, :], in0=total[:, :], scalar=0.0, in1=total[:, :],
                                              op0=ALU.is_equal, op1=ALU.add))
                step(dve.reciprocal(inverse[:, :], total[:, :]))
                step(dve.tensor_tensor(share[:, :, :], kept[:, :, :], over(inverse[:, :], 2), ALU.mult))
                picks_flat = picks[:, :, :, :].rearrange("p t j e -> p (t j) e")
                experts = m.index[:, :].rearrange("p (o e) -> p o e", o=1).to_broadcast([P, 4, EXPERTS])
                step(dve.tensor_tensor(picks_flat, experts, over(index[:, :, :].rearrange("p t j -> p (t j)"), EXPERTS),
                                       ALU.is_equal))
                step(dve.tensor_tensor(picks_flat, picks_flat, over(share[:, :, :].rearrange("p t j -> p (t j)"), EXPERTS),
                                       ALU.mult))
                dve.tensor_tensor(weights[:, nxt, :, :], picks[:, :, 0, :], picks[:, :, 1, :],
                                  ALU.add).then_inc(weights_ready, 1)

            def add_experts(p, par, t, sets):
                for s in sets:
                    use = 2 * SETS * p + SETS * t + s
                    if s == 0 and t == 0:
                        dve.wait_ge(weights_ready, p + 1)
                        dve.wait_ge(bias_ready, p + 1)
                        ge(dve, y_stats, p)
                    dve.wait_ge(set_full, use + 1)
                    bank = m.psum[:, E_BANK + s, :]
                    if s > 0:
                        dve.wait_ge(even_added, use)
                    start = y_bias[par] if s == 0 else even
                    dve.scalar_tensor_tensor(out=even[:, t, :], in0=bank[:, 0:D], scalar=weights[:, par, t, 2 * s:2 * s + 1],
                                             in1=start[:, t, :], op0=ALU.mult, op1=ALU.add).then_inc(even_added, 1)
                    w = weights[:, par, t, 2 * s + 1:2 * s + 2]
                    if s == 0:
                        ins = dve.tensor_scalar(odd[:, t, :], bank[:, D:], w, None, ALU.mult)
                    else:
                        dve.wait_ge(set_read, use)
                        ins = dve.scalar_tensor_tensor(out=odd[:, t, :], in0=bank[:, D:], scalar=w, in1=odd[:, t, :],
                                                       op0=ALU.mult, op1=ALU.add)
                    ins.then_inc(set_read, 1)

            def body(J, r):
                p, par, nxt = 2 * J + r, r % 2, (r + 1) % 2
                now, ahead, last = on(J, r, 0), on(J, r, 2), on(J, r, -1)
                if ahead:
                    for t in range(2):
                        tile = 2 * p + 4 + t
                        ins = dve.tensor_scalar(first_ln[:, t, :], m.x[:, bass.ds(tile, 1), :],
                                                m.mean[:, bass.ds(tile, 1)], m.rstd[:, bass.ds(tile, 1)],
                                                ALU.subtract, ALU.mult)
                    ins.then_inc(first_normal, 1)
                if now:
                    add_experts(p, par, 0, range(0, 2))
                if last:
                    dve.wait_ge(y_rstd, p)
                    step(normalise(1, normal, lambda t: y[:, t, :]))
                    step(dve.tensor_tensor(x_pair(p - 1), x_pair(p - 1), normal, ALU.add))
                if on(J, r, 1):
                    gate_logits(p)
                if ahead:
                    dve.wait_ge(first_normal, p + 3)
                    dve.wait_ge(u_full, p + 3)
                    new = m.psum[:, U_BANK, :].rearrange("p (t d) -> p t d", t=2)
                    dve.tensor_tensor(u, new, first_ln, ALU.add).then_inc(u_ready, 1)
                    ge_bare(dve, u_ready, p + 3)
                    statistics(0, lambda t: u[:, t, :], u_stats)
                if now:
                    add_experts(p, par, 0, range(2, 3))
                if on(J, r, 1):
                    gate_weights(p, nxt)
                if now:
                    add_experts(p, par, 0, range(3, SETS))
                if ahead:
                    dve.wait_ge(u_rstd, p + 3)
                    step(normalise(0, normal, lambda t: u[:, t, :]))
                    step(dve.tensor_tensor(x_pair(p + 2), x_pair(p + 2), normal, ALU.add), bare=True)
                    statistics(2, lambda t: m.x[:, bass.ds(2 * p + 4 + t, 1), :], x1_stats)
                if now:
                    add_experts(p, par, 1, range(0, 2))
                if ahead:
                    dve.wait_ge(x1_rstd, p + 3)
                    ge(dve, xt_full, p + 1)
                    normalise(2, xln[par], lambda t: m.x[:, bass.ds(2 * p + 4 + t, 1), :]).then_inc(xln_ready, 1)
                if now:
                    add_experts(p, par, 1, range(2, SETS))
                    dve.wait_ge(set_read, 2 * SETS * (p + 1))
                    dve.wait_ge(even_added, 2 * SETS * (p + 1))
                    step(dve.tensor_tensor(y, even, odd, ALU.add), bare=True)
                    statistics(1, lambda t: y[:, t, :], y_stats)

            loop(dve, body, chain, 24)


def spectral(nc, m, out):
    XT_BANK, Y_BANK = 0, 4
    with ExitStack() as ctx:
        def sem(name):
            return ctx.enter_context(nc.semaphore(f"spec_{name}"))

        z_stats, z_rstd, x_stats, x_rstd, y_stats, y_rstd = (
            sem("z_stats"), sem("z_rstd"), sem("x_stats"), sem("x_rstd"), sem("y_stats"), sem("y_rstd"))
        z_normal, x_added, xln_ready, xt_full, xt_ready, y_full, y_normal = (
            sem("z_normal"), sem("x_added"), sem("xln_ready"), sem("xt_full"), sem("xt_ready"), sem("y_full"),
            sem("y_normal"))
        res_ready = sem("res_ready")
        stored = [sem(f"stored{i}") for i in range(2)]
        dve_steps, pool_steps = sem("dve_steps"), sem("pool_steps")
        W = CHUNK * D

        def tiles(i):
            return m.scratch[:, i * W:(i + 1) * W].rearrange("p (t d) -> p t d", t=CHUNK)

        xln, zn, yn, res = tiles(0), tiles(1), [tiles(2), tiles(3)], [tiles(4), tiles(5)]
        xt = [m.scratch[:, (6 + i) * W:(7 + i) * W].rearrange("p (c t) -> p c t", c=KC) for i in range(2)]

        def sb(name, shape):
            return ctx.enter_context(nc.sbuf_tensor(f"spec_{name}", shape, F32))

        bn = [sb(f"bn{i}", [P, CHUNK, 6]) for i in range(3)]
        mv = [sb(f"mv{i}", [P, 2, CHUNK, 2]) for i in range(3)]
        var = [sb(f"var{i}", [P, CHUNK]) for i in range(3)]
        minus_mean = [sb(f"minus_mean{i}", [P, CHUNK]) for i in range(3)]
        rstd = [sb(f"rstd{i}", [P, 2, CHUNK]) for i in range(3)]
        shift = [sb(f"shift{i}", [P, 2, CHUNK]) for i in range(3)]
        FIRST, LAST = -3, CHUNKS

        block = ctx.enter_context(nc.Block())

        @block.gpsimd
        def _(pool):
            chain = Chain(pool, pool_steps)

            def take_rstd(k, par, stats, ready, count):
                pool.wait_ge(stats, count)
                ge(pool, ready, count - 1)
                pool.tensor_tensor(minus_mean[k][:, :], mv[k][:, par, :, 0], m.minus_one[:, :], ALU.mult)
                chain.then(pool.tensor_tensor(var[k][:, :], mv[k][:, par, :, 1], m.eps[:, :], ALU.add))
                chain.then(pool.tensor_tensor(rstd[k][:, par, :], var[k][:, :], m.minus_half[:, :], ALU.pow))
                pool.tensor_tensor(shift[k][:, par, :], minus_mean[k][:, :], rstd[k][:, par, :],
                                   ALU.mult).then_inc(ready, 1)

            def body(J, u):
                c = 2 * J + u
                if on(J, u, 2):
                    take_rstd(1, u % 2, x_stats, x_rstd, c + 3)
                if on(J, u, 3):
                    take_rstd(0, (u + 1) % 2, z_stats, z_rstd, c + 4)
                if on(J, u, 0):
                    take_rstd(2, u % 2, y_stats, y_rstd, c + 1)
                if on(J, u, -1):
                    old = (u + 1) % 2
                    pool.wait_ge(y_normal, c)
                    ge(pool, stored[old], 16 * (J + (u - 1) // 2))
                    pool.tensor_tensor(res[old], m.x[:, bass.ds((c - 1) * CHUNK, CHUNK), :], yn[old],
                                       ALU.add).then_inc(res_ready, 1)

            chunk_loop(pool, body, FIRST, LAST, chain, 6)

        @block.tensor
        def _(pe):
            def body(J, u):
                c = 2 * J + u
                if on(J, u):
                    pe.wait_ge(xt_ready, c + 1)
                    ge(pe, y_normal, c - 1)
                    for t in range(CHUNK):
                        dst = m.psum[:, Y_BANK + 2 * (u % 2) + t // 2, (t % 2) * D:(t % 2 + 1) * D]
                        for k in range(KC):
                            pe.matmul(dst, xt[u % 2][:, k, t * P:(t + 1) * P], m.fold[:, k, :],
                                      start=(k == 0), stop=False)
                        ins = pe.matmul(dst, m.ones[:, :], m.bias[:, :], start=False, stop=True)
                    ins.then_inc(y_full, 1)
                if on(J, u, 1):
                    pe.wait_ge(xln_ready, c + 2)
                    ge(pe, xt_ready, c + 1)
                    for t in range(CHUNK):
                        for k in range(KC):
                            ins = pe.transpose(m.psum[:, XT_BANK + k, t * P:(t + 1) * P],
                                               xln[:, t, k * P:(k + 1) * P], m.ident[:, :])
                    ins.then_inc(xt_full, 1)

            chunk_loop(pe, body, FIRST, LAST)

        @block.scalar
        def _(act):
            def normalise(k, par, out, src):
                for t in range(CHUNK):
                    ins = act.activation(out(t), src(t), ACT.Identity, scale=rstd[k][:, par, t:t + 1],
                                         bias=shift[k][:, par, t:t + 1])
                return ins

            def by_group(ap):
                return ap.rearrange("p (g n) -> p g n", g=GROUPS // B)

            def body(J, u):
                c = 2 * J + u
                if on(J, u, 1):
                    act.wait_ge(x_rstd, c + 2)
                    ge(act, xt_full, c + 1)
                    normalise(1, (u + 1) % 2, lambda t: xln[:, t, :],
                              lambda t: m.x[:, bass.ds((c + 1) * CHUNK + t, 1), :].rearrange("p o d -> p (o d)")
                              ).then_inc(xln_ready, 1)
                if on(J, u, 3):
                    b, qt = J + (u + 3) // 2, (u + 3) % 2 * CHUNK
                    act.wait_ge(z_rstd, c + 4)
                    ge(act, x_added, c + 3)
                    normalise(0, (u + 1) % 2, lambda t: by_group(zn[:, t, :]),
                              lambda t: m.z[:, bass.ds(b * (GROUPS // B), GROUPS // B), qt + t, :]
                              ).then_inc(z_normal, 1)
                if on(J, u, 1):
                    act.wait_ge(xt_full, c + 2)
                    ge(act, y_full, c)
                    act.copy(xt[(u + 1) % 2], m.psum[:, XT_BANK:XT_BANK + 2, :]).then_inc(xt_ready, 1)
                if on(J, u, 0):
                    act.wait_ge(y_rstd, c + 1)
                    ge(act, res_ready, c - 1)
                    bank = Y_BANK + 2 * (u % 2)
                    normalise(2, u % 2, lambda t: yn[u % 2][:, t, :],
                              lambda t: m.psum[:, bank + t // 2, (t % 2) * D:(t % 2 + 1) * D]).then_inc(y_normal, 1)

            chunk_loop(act, body, FIRST, LAST)

        @block.vector
        def _(dve):
            chain = Chain(dve, dve_steps)

            def statistics(k, par, src, done):
                for t in range(CHUNK):
                    ins = dve.bn_stats(bn[k][:, t, :], src(t))
                chain.then(ins, bare=True)
                for t in range(CHUNK):
                    ins = dve.bn_aggr(mv[k][:, par, t, :], bn[k][:, t, :])
                ins.then_inc(done, 1)

            def body(J, u):
                c = 2 * J + u
                if on(J, u, 2):
                    dve.wait_ge(z_normal, c + 3)
                    x_chunk = m.x[:, bass.ds((c + 2) * CHUNK, CHUNK), :]
                    dve.tensor_tensor(x_chunk, x_chunk, zn, ALU.add).then_inc(x_added, 1)
                    ge_bare(dve, x_added, c + 3)
                    statistics(1, u % 2, lambda t: m.x[:, bass.ds((c + 2) * CHUNK + t, 1), :], x_stats)
                if on(J, u, 3):
                    b, qt = J + (u + 3) // 2, (u + 3) % 2 * CHUNK
                    statistics(0, (u + 1) % 2,
                               lambda t: m.z[:, bass.ds(b * (GROUPS // B), GROUPS // B), qt + t, :], z_stats)
                if on(J, u, 0):
                    bank = Y_BANK + 2 * (u % 2)
                    if not on(J, u, 2):
                        ge(dve, y_stats, c)
                    ge_bare(dve, y_full, c + 1)
                    statistics(2, u % 2, lambda t: m.psum[:, bank + t // 2, (t % 2) * D:(t % 2 + 1) * D], y_stats)

            chunk_loop(dve, body, FIRST, LAST, chain, 3)

        @block.sync
        def _(sp):
            out_view = out.rearrange("(c t p) d -> c p t d", p=P, t=CHUNK)

            def body(J, u):
                if not on(J, u, -1):
                    return
                c, old = 2 * J + u, (u + 1) % 2
                sp.wait_ge(res_ready, c)
                sp.dma_start(out_view[bass.ds(c - 1, 1), :, :, :].rearrange("o p t d -> p (o t) d"),
                             res[old]).then_inc(stored[old], 16)

            chunk_loop(sp, body, FIRST, LAST)
            for i in range(2):
                sp.wait_ge(stored[i], 16 * CHUNKS // 2)


def build(nc, io, out):
    q_dram = [nc.dram_tensor(f"q_parts{i}", [B, PARTS, D, S], BF16).ap() for i in range(2)]
    k_dram = [nc.dram_tensor("k_parts0", [B, PARTS, D, S], BF16).ap(),
              nc.dram_tensor("k_parts1", [B, PARTS, DH, S], BF16).ap()]
    with ExitStack() as ctx:
        m = Memory(nc, ctx)
        loads = Loads(nc, ctx)
        setup(nc, m, io, loads)
        projection(nc, m, 0, q_dram[0], k_dram[0], loads)
        attention(nc, m, 0, q_dram[0], k_dram[0], loads)
        mixture(nc, m)
        projection(nc, m, 1, q_dram[1], k_dram[1])
        attention(nc, m, 1, q_dram[1], k_dram[1])
        spectral(nc, m, out)


def constants():
    n = np.arange(D)
    angle = 2.0 * np.pi * (np.outer(n, n) % D) / D
    return {
        "dft_cos": np.cos(angle).astype(np.float32),
        "dft_sin": np.sin(angle).astype(np.float32),
        "dft_minus_cos": (-np.cos(angle)).astype(np.float32),
        "ident": np.eye(P, dtype=np.float32),
        "index": np.broadcast_to(np.arange(EXPERTS, dtype=np.float32), (P, EXPERTS)).copy(),
    }


def kernel(L0_attn_x, L0_attn_mask, L0_attn_Wq, L0_attn_Wk, L0_attn_Wv, L0_attn_Wout, L0_ffn_gate_w, L0_ffn_gate_b,
           L0_ffn_expert_w, L0_ffn_expert_b, L1_attn_Wq, L1_attn_Wk, L1_attn_Wv, L1_ffn_w_freq_real,
           L1_ffn_w_freq_imag, L1_ffn_bias):
    import concourse.bacc as bacc
    from concourse.bass_utils import run_bass_kernel_spmd

    arrays = {
        "x": np.reshape(L0_attn_x, (B * S, D)),
        "wq0": L0_attn_Wq, "wk0": L0_attn_Wk, "wv0": L0_attn_Wv, "wout": L0_attn_Wout,
        "gate_w": np.transpose(L0_ffn_gate_w), "gate_b": np.broadcast_to(L0_ffn_gate_b, (P, GATES)),
        "expert_w": L0_ffn_expert_w, "expert_b": L0_ffn_expert_b,
        "wq1": np.transpose(L1_attn_Wq), "wk1": np.transpose(L1_attn_Wk), "wv1": np.transpose(L1_attn_Wv),
        "w_real": L1_ffn_w_freq_real, "w_imag": L1_ffn_w_freq_imag,
        "bias": np.reshape(L1_ffn_bias, (1, D)),
    }
    arrays.update(constants())
    nc = bacc.Bacc("TRN2", target_bir_lowering=False, num_devices=1)
    feed, io = {}, {}
    for name, a in arrays.items():
        a = np.ascontiguousarray(a)
        feed[f"in_{name}"] = a
        io[name] = nc.dram_tensor(f"in_{name}", a.shape, mybir.dt.from_np(a.dtype), kind="ExternalInput").ap()
    out = nc.dram_tensor("out", (B * S, D), F32, kind="ExternalOutput").ap()
    build(nc, io, out)
    result = run_bass_kernel_spmd(nc, [feed], core_ids=[0])
    return np.reshape(result.results[0]["out"], (B, S, D))
```

```python
from contextlib import ExitStack

import numpy as np

import concourse.bass as bass
from concourse import mybir

F32 = mybir.dt.float32
BF16 = mybir.dt.bfloat16
U32 = mybir.dt.uint32
ALU = mybir.AluOpType
ACT = mybir.ActivationFunctionType
AX = mybir.AxisListType

P = 128
B, S, D, H = 4, 1024, 256, 16
DH = D // H
KC = D // P
TILES = B * S // P
CHUNK = 4
CHUNKS = TILES // CHUNK
CT = CHUNK * P
HG = 4
GROUPS = B * H // HG
GF = HG * DH
HALVES = 2 * GROUPS
HQ = S // 2
KT = S // P
QT = HQ // P
PARTS = 3
Q_PARTS = (0, 0, 0, 1, 1, 2)
K_PARTS = (0, 1, 2, 0, 1, 0)
ROWS = len(Q_PARTS) * DH
VW = 32
EXPERTS, NULLS = 8, 2
GATES = EXPERTS + NULLS
EPS = 1e-5
SCALE = DH ** -0.5

SCRATCH = 9216


def ge(engine, semaphore, value):
    if isinstance(value, int) and value <= 0:
        return
    engine.wait_ge(semaphore, value)


def ge_bare(engine, semaphore, value):
    if not isinstance(value, int):
        engine.lower_val(value)
        engine.wait_ge(semaphore, 1)
    ge(engine, semaphore, value)


class Chain:

    def __init__(self, engine, semaphore):
        self.engine, self.semaphore, self.base, self.count = engine, semaphore, 0, 0

    def then(self, instruction, bare=False):
        instruction.then_inc(self.semaphore, 1)
        self.count += 1
        (ge_bare if bare else ge)(self.engine, self.semaphore, self.base + self.count)


def chunk_loop(engine, body, first, last=CHUNKS - 1, chain=None, per_chunk=0):
    lead, loops = 1, (CHUNKS - 4) // 2
    for c in range(first, lead):
        body(0, c)
    before = chain.count if chain else 0
    with engine.Fori(0, loops) as J:
        if chain:
            chain.base, chain.count = J * (2 * per_chunk), before
        body(J, lead)
        body(J, lead + 1)
        assert not chain or chain.count == before + 2 * per_chunk, (chain.count, before)
    if chain:
        chain.base = (loops - 1) * 2 * per_chunk
    for c in range(lead + 2 * loops, last + 1):
        body(0, c)


def on(J, u, by=0):
    return not isinstance(J, int) or 0 <= u + by < CHUNKS


class Memory:

    def __init__(self, nc, ctx):
        def sb(name, shape, dt=F32):
            return ctx.enter_context(nc.sbuf_tensor(name, shape, dt))

        self.x = sb("x_res", [P, TILES, D])
        self.z = sb("z_res", [P, GROUPS, KT, GF])
        self.v = sb("v_res", [P, GROUPS, KT, GF])
        self.mean = sb("mean_first", [P, TILES])
        self.rstd = sb("rstd_first", [P, TILES])
        self.q_stack = sb("q_stack", [P, 4, HG, HQ], BF16)
        self.k_stack = sb("k_stack", [P, 2, HG, S], BF16)
        self.v_group = sb("v_group", [P, 2, KT, HG, VW])
        self.scratch = sb("scratch", [P, SCRATCH])
        self.ident = sb("ident", [P, P])
        self.wq0 = sb("wq0", [P, KC, D])
        self.wk0 = sb("wk0", [P, KC, D])
        self.wv0 = sb("wv0", [P, KC, D])
        self.wout = sb("wout", [P, KC, D])
        self.wq1 = sb("wq1", [P, KC, D])
        self.wk1 = sb("wk1", [P, KC, DH])
        self.wv1 = sb("wv1", [P, KC, DH])
        self.gate_w = sb("gate_w_sb", [P, KC, GATES])
        self.gate_b = sb("gate_b_sb", [P, GATES])
        self.expert_w = sb("expert_w_sb", [P, KC, EXPERTS, D])
        self.expert_b = sb("expert_b_sb", [EXPERTS, D])
        self.bias = sb("bias_sb", [1, D])
        self.index = sb("index_row", [P, EXPERTS])
        self.fold = sb("fold", [P, KC, D])
        self.eps = sb("eps_col", [P, CHUNK])
        self.minus_half = sb("minus_half", [P, CHUNK])
        self.minus_one = sb("minus_one", [P, CHUNK])
        self.ones = sb("ones_row", [1, P])
        self.psum = ctx.enter_context(nc.psum_tensor("psum", [P, 8, 512], F32))


class Loads:

    def __init__(self, nc, ctx):
        def sem(name):
            return ctx.enter_context(nc.semaphore(name))

        self.x_first = [sem("x_loaded0"), sem("x_loaded1")]
        self.x_rest = sem("x_loaded_rest")
        self.projection, self.dft, self.rest = sem("proj_w_loaded"), sem("dft_loaded"), sem("rest_loaded")
        self.n_projection = self.n_dft = self.n_rest = 0


def chunked(w):
    return w.rearrange("(c p) n -> p c n", p=P)


def setup(nc, m, io, loads):
    with ExitStack() as ctx:
        block = ctx.enter_context(nc.Block())

        @block.sync
        def _(sp):
            for c in range(2):
                load_x(sp, m, io, c, loads.x_first[c])

        @block.scalar
        def _(act):
            act.dma_start(m.ident[:, :], io["ident"]).then_inc(loads.projection, 16)
            for dst, name in ((m.wq0, "wq0"), (m.wk0, "wk0"), (m.wv0, "wv0")):
                act.dma_start(dst[:, :, :], chunked(io[name])).then_inc(loads.projection, 16)
            loads.n_projection = 16 * 4

        @block.vector
        def _(dve):
            dve.memset(m.eps[:, :], EPS)
            dve.memset(m.minus_half[:, :], -0.5)
            dve.memset(m.minus_one[:, :], -1.0)
            dve.memset(m.ones[:, :], 1.0)


def load_x(sp, m, io, c, semaphore):
    x_view = io["x"].rearrange("(t p) d -> p t d", p=P)
    sp.dma_start(m.x[:, c * CHUNK:(c + 1) * CHUNK, :], x_view[:, c * CHUNK:(c + 1) * CHUNK, :]).then_inc(semaphore, 16)


def load_later_weights(sp, m, io, loads):
    for dst, name in zip(dft_views(m), ("dft_cos", "dft_sin", "dft_minus_cos", "w_real", "w_imag")):
        sp.dma_start(dst, chunked(io[name])).then_inc(loads.dft, 16)
        loads.n_dft += 16
    rest = [(m.gate_b[:, :], io["gate_b"]), (m.bias[:, :], io["bias"]),
            (m.index[:, :], io["index"]), (m.expert_b[:, :], io["expert_b"])]
    for dst, name in ((m.wout, "wout"), (m.wq1, "wq1"), (m.wk1, "wk1"), (m.wv1, "wv1"), (m.gate_w, "gate_w")):
        rest.append((dst[:, :, :], chunked(io[name])))
    experts = io["expert_w"].rearrange("e (c p) n -> p c e n", p=P)
    rest += [(m.expert_w[:, c, :, :], experts[:, c, :, :]) for c in range(KC)]
    for dst, src in rest:
        sp.dma_start(dst, src).then_inc(loads.rest, 16)
        loads.n_rest += 16




class Stacks:
    EARLY_HALVES = 2

    def __init__(self, nc, ctx, m, layer, q_dram, k_dram):
        self.m, self.shared, self.q_dram, self.k_dram = m, layer == 1, q_dram, k_dram
        self.q_loaded = [ctx.enter_context(nc.semaphore(f"q_loaded{i}_{layer}")) for i in range(4)]
        self.k_loaded = [ctx.enter_context(nc.semaphore(f"k_loaded{i}_{layer}")) for i in range(2)]
        self.stored = [ctx.enter_context(nc.semaphore(f"{name}_stored_{layer}")) for name in "qk"]

    def of_group(self, dram, g):
        b, hg = g // (GROUPS // B), g % (GROUPS // B)
        return dram[bass.ds(b, 1), :, bass.ds(hg * GF, GF), :].rearrange("o s (h d) t -> d (o s) h t", h=HG)

    def load_q(self, sp, J, r):
        slot, qh = r % 4, r % 2
        src = self.of_group(self.q_dram, 2 * J + r // 2)[:, :, :, qh * HQ:(qh + 1) * HQ]
        for j, part in enumerate(Q_PARTS):
            sp.dma_start(self.m.q_stack[j * DH:(j + 1) * DH, slot, :, :],
                         src[:, part, :, :]).then_inc(self.q_loaded[slot], 16)

    def load_k(self, sp, J, r):
        slot = r % 2
        if self.shared:
            b = (2 * J + r) // (GROUPS // B)
            src = self.k_dram[bass.ds(b, 1), :, :, :].rearrange("o s (h d) t -> d (o s) h t", h=1)
        else:
            src = self.of_group(self.k_dram, 2 * J + r)
        for j, part in enumerate(K_PARTS):
            one = src[:, part, :, :]
            if self.shared:
                one = one.to_broadcast([DH, HG, S])
            sp.dma_start(self.m.k_stack[j * DH:(j + 1) * DH, slot, :, :], one).then_inc(self.k_loaded[slot], 16)



def dft_views(m):
    flat = m.z[:, :, :, :].rearrange("p g t n -> p (g t n)")
    W = KC * D
    return [flat[:, i * W:(i + 1) * W].rearrange("p (c n) -> p c n", c=KC) for i in range(7)]


def projection(nc, m, ctx, layer, stacks, io, loads=None):
    shared = layer == 1
    wq, wk, wv = (m.wq1, m.wk1, m.wv1) if shared else (m.wq0, m.wk0, m.wv0)
    KB = 1 if shared else KC
    KR = DH if shared else P
    VN = DH if shared else D
    XT_BANK, Q_BANK, K_BANK, V_BANK = 0, 2, 4, 6

    def sem(name):
        return ctx.enter_context(nc.semaphore(f"{name}_{layer}"))

    stats_ready, rstd_ready, xln_ready = sem("stats_ready"), sem("rstd_ready"), sem("xln_ready")
    xt_full, xt_ready = sem("xt_full"), sem("xt_ready")
    v_full, v_copied = sem("v_full"), sem("v_copied")
    full = [sem("q_full"), sem("k_full")]
    high = [sem("q_high"), sem("k_high")]
    rest = [sem("q_rest"), sem("k_rest")]
    middle = [sem("q_middle"), sem("k_middle")]
    low = [sem("q_low"), sem("k_low")]
    stored = stacks.stored
    dve_steps, pool_steps, presets = sem("dve_steps"), sem("pool_steps"), sem("presets")

    def cut(start, words):
        return m.scratch[:, start:start + words]

    W = CHUNK * D
    free = m.z[:, :, :, :].rearrange("p g t n -> p (g t n)")
    xln = [free[:, (4 + i) * W:(5 + i) * W].rearrange("p (t d) -> p t d", t=CHUNK) for i in range(2)]
    xt = [cut(i * W, W).rearrange("p (c t) -> p c t", c=KC) for i in range(2)]
    rests = [cut((2 + i) * W, W).rearrange("p (c t) -> p c t", c=KC) for i in range(2)]
    parts = [cut(4 * W + i * W * PARTS // 2, W * PARTS // 2).bitcast(BF16).rearrange(
        "p (s c t) -> p s c t", s=PARTS, c=KC) for i in range(2)]
    bn = ctx.enter_context(nc.sbuf_tensor(f"bn_{layer}", [P, CHUNK, 6], F32))
    mv = ctx.enter_context(nc.sbuf_tensor(f"mv_{layer}", [P, 2, CHUNK, 2], F32))
    var = ctx.enter_context(nc.sbuf_tensor(f"var_{layer}", [P, CHUNK], F32))
    rstd = ctx.enter_context(nc.sbuf_tensor(f"rstd_{layer}", [P, 2, CHUNK], F32))

    dve_chain, pool_chain = Chain(nc.vector, dve_steps), Chain(nc.gpsimd, pool_steps)
    EARLY = 2 if shared else 0
    blocks, rows = (KC, KB), (P, KR)
    banks = (Q_BANK, K_BANK)

    def in_psum(i):
        return m.psum[0:rows[i], banks[i]:banks[i] + blocks[i], :]

    def at(J, u):
        return 2 * J + u, u % 2, J + u // 2, u % 2

    def sync(sp):
        def body(J, u):
            if not on(J, u):
                return
            c, _, b, qh = at(J, u)
            for i, dram in enumerate((stacks.q_dram, stacks.k_dram)):
                sp.wait_ge(low[i], c + 1)
                dst = dram[bass.ds(b, 1), :, :, qh * CT:(qh + 1) * CT]
                if i == 1 and shared:
                    sp.dma_start(dst.rearrange("o s r t -> r (o s) t"),
                                 parts[i][0:KR, :, 0, :]).then_inc(stored[i], 16)
                else:
                    sp.dma_start(dst.rearrange("o s (c r) t -> r (o s c) t", r=P),
                                 parts[i][:, :, :, :].rearrange("p s c t -> p (s c) t")).then_inc(stored[i], 16)
            if isinstance(c, int) and c == CHUNKS - 3:
                for i in range(2):
                    sp.wait_ge(stored[i], 16 * (CHUNKS - 2))
                stacks.load_q(sp, 0, 0)
                stacks.load_k(sp, 0, 0)
            if isinstance(c, int) and c == CHUNKS - 2:
                stacks.load_q(sp, 0, 1)

        if loads:
            for c in range(2, CHUNKS):
                load_x(sp, m, io, c, loads.x_rest)
            load_later_weights(sp, m, io, loads)
        chunk_loop(sp, body, 0)
        if loads:
            sp.wait_ge(loads.rest, loads.n_rest)

    def gpsimd(pool, part="rest"):
        def body(J, u):
            if not on(J, u, 2):
                return
            c, nxt = 2 * J + u, u % 2
            pool.wait_ge(stats_ready, c + 3)
            pool_chain.then(pool.tensor_tensor(var[:, :], mv[:, nxt, :, 1], m.eps[:, :], ALU.add))
            pool.tensor_tensor(rstd[:, nxt, :], var[:, :], m.minus_half[:, :], ALU.pow).then_inc(rstd_ready, 1)

        if part != "rest":
            body(0, part)
            return
        chunk_loop(pool, body, EARLY - 2, chain=pool_chain, per_chunk=1)
        if loads:
            pool.memset(m.v_group[:, :, :, :, :], 0.0).then_inc(presets, 1)
            pool.wait_ge(presets, 1)
            pool.memset(m.v_group[:, :, :, :, DH:DH + 1], 1.0).then_inc(presets, 1)
            pool.wait_ge(presets, 2)
            pool.memset(m.k_stack[ROWS:ROWS + PARTS, :, :, :], 1.0)

    def vector(dve, part="rest"):
        def body(J, u):
            c = 2 * J + u
            if on(J, u, 1):
                nxt = (u + 1) % 2
                dve.wait_ge(rstd_ready, c + 2)
                ge(dve, xt_ready, c)
                for t in range(CHUNK):
                    ins = dve.tensor_scalar(xln[nxt][:, t, :], m.x[:, bass.ds((c + 1) * CHUNK + t, 1), :],
                                            mv[:, nxt, t, 0:1], rstd[:, nxt, t:t + 1], ALU.subtract, ALU.mult)
                ins.then_inc(xln_ready, 1)
                if not shared:
                    dve.tensor_copy(m.mean[:, bass.ds((c + 1) * CHUNK, CHUNK)], mv[:, nxt, :, 0])
                    dve.tensor_copy(m.rstd[:, bass.ds((c + 1) * CHUNK, CHUNK)], rstd[:, nxt, :])
            if on(J, u, 2):
                if loads and isinstance(J, int):
                    sem, n = (loads.x_first[c + 2], 16) if c + 2 < 2 else (loads.x_rest, 16 * (CHUNKS - 2))
                    dve.wait_ge(sem, n)
                if loads and not isinstance(J, int):
                    dve.wait_ge(loads.x_rest, 16 * (CHUNKS - 2))
                for t in range(CHUNK):
                    ins = dve.bn_stats(bn[:, t, :], m.x[:, bass.ds((c + 2) * CHUNK + t, 1), :])
                dve_chain.then(ins, bare=True)
                for t in range(CHUNK):
                    ins = dve.bn_aggr(mv[:, u % 2, t, :], bn[:, t, :])
                ins.then_inc(stats_ready, 1)
            if not on(J, u):
                return
            for i in range(2):
                r = slice(0, rows[i])
                dve.wait_ge(high[i], c + 1)
                dve.tensor_tensor(rests[i][r, 0:blocks[i], :], in_psum(i), parts[i][r, 0, 0:blocks[i], :],
                                  ALU.subtract).then_inc(rest[i], 1)
                dve.wait_ge(middle[i], c + 1)
                dve.tensor_tensor(parts[i][r, 2, 0:blocks[i], :], rests[i][r, 0:blocks[i], :],
                                  parts[i][r, 1, 0:blocks[i], :], ALU.subtract).then_inc(low[i], 1)

        if part != "rest":
            body(0, part)
            return
        chunk_loop(dve, body, EARLY - 2, chain=dve_chain, per_chunk=1)

    def scalar(act):
        def take_high(i, c):
            act.wait_ge(full[i], c + 1)
            ge(act, stored[i], 16 * c)
            r = slice(0, rows[i])
            act.copy(parts[i][r, 0, 0:blocks[i], :], in_psum(i)).then_inc(high[i], 1)

        def take_middle(i, c):
            act.wait_ge(rest[i], c + 1)
            r = slice(0, rows[i])
            act.copy(parts[i][r, 1, 0:blocks[i], :], rests[i][r, 0:blocks[i], :]).then_inc(middle[i], 1)

        def body(J, u):
            c, par, b, qh = at(J, u)
            if on(J, u):
                take_high(0, c)
                if not shared:
                    take_middle(0, c)
                take_high(1, c)
            if on(J, u, 1):
                act.wait_ge(xt_full, c + 2)
                ge(act, v_full, c)
                act.copy(xt[(u + 1) % 2], m.psum[:, XT_BANK:XT_BANK + 2, :]).then_inc(xt_ready, 1)
            if not on(J, u):
                return
            if shared:
                take_middle(0, c)
            take_middle(1, c)
            act.wait_ge(v_full, c + 1)
            v_new = m.psum[:, V_BANK:V_BANK + 2, :].rearrange("p b (t n) -> p (b t) n", n=D)
            if shared:
                dst = m.v[:, bass.ds(b * (GROUPS // B), 1), qh * CHUNK:(qh + 1) * CHUNK, 0:DH]
                act.copy(dst.rearrange("p o t n -> p (o t) n"), v_new[:, :, 0:DH]).then_inc(v_copied, 1)
                return
            for hg in range(GROUPS // B):
                dst = m.v[:, bass.ds(b * (GROUPS // B) + hg, 1), qh * CHUNK:(qh + 1) * CHUNK, :]
                ins = act.copy(dst.rearrange("p o t n -> p (o t) n"), v_new[:, :, hg * GF:(hg + 1) * GF])
            ins.then_inc(v_copied, 1)

        chunk_loop(act, body, -1)

    def tensor(pe):
        def body(J, u):
            c, par, _, _ = at(J, u)
            nxt = (u + 1) % 2
            if on(J, u):
                pe.wait_ge(xt_ready, c + 1)
                for i, w in enumerate((wq, wk)):
                    ge(pe, rest[i], c)
                    for blk in range(blocks[i]):
                        for k in range(KC):
                            ins = pe.matmul(m.psum[0:rows[i], banks[i] + blk, :],
                                            w[:, k, blk * P:blk * P + rows[i]], xt[par][:, k, :],
                                            start=(k == 0), stop=(k == KC - 1))
                    ins.then_inc(full[i], 1)
            if on(J, u, 1):
                pe.wait_ge(xln_ready, c + 2)
                ge(pe, xt_ready, c + 1)
                for t in range(CHUNK):
                    for k in range(KC):
                        ins = pe.transpose(m.psum[:, XT_BANK + k, t * P:(t + 1) * P],
                                           xln[nxt][:, t, k * P:(k + 1) * P], m.ident[:, :])
                ins.then_inc(xt_full, 1)
            if not on(J, u):
                return
            ge(pe, v_copied, c)
            for t in range(CHUNK):
                for k in range(KC):
                    ins = pe.matmul(m.psum[:, V_BANK + t // 2, (t % 2) * D:(t % 2) * D + VN],
                                    xt[par][:, k, t * P:(t + 1) * P], wv[:, k, :],
                                    start=(k == 0), stop=(k == KC - 1))
            ins.then_inc(v_full, 1)

        if loads:
            pe.wait_ge(loads.projection, loads.n_projection)
        chunk_loop(pe, body, -1)

    def run():
        with nc.Block() as block:
            @block.gpsimd
            def _(pool):
                gpsimd(pool)

            @block.tensor
            def _(pe):
                tensor(pe)

            @block.scalar
            def _(act):
                scalar(act)

            @block.vector
            def _(dve):
                vector(dve)

            @block.sync
            def _(sp):
                sync(sp)

    return {"gpsimd": gpsimd, "vector": vector, "run": run}


def attention(nc, m, layer, stacks, nxt, loads=None):
    shared = layer == 1
    S_BANK, ST_BANK, ST_BANKS, PV_BANK = 0, 4, 3, 7
    P_SLOTS = 4
    UNITS = HG * QT
    with ExitStack() as ctx:
        def sem(name):
            return ctx.enter_context(nc.semaphore(f"{name}_{layer}"))

        q_loaded, k_loaded = stacks.q_loaded, stacks.k_loaded
        v_ready = sem("v_ready")
        item_full, item_done = sem("item_full"), sem("item_done")
        parts_ready = sem("max_parts_ready")
        max_loaded = [sem(f"max_loaded{i}") for i in range(2)]
        st_full, exp_done, pv_done = sem("st_full"), sem("exp_done"), sem("pv_done")
        zt_ready = sem("zt_ready")
        dve_steps = sem("dve_steps_att")

        probs = [m.scratch[:, i * HG * HQ:(i + 1) * HG * HQ].rearrange("p (h q) -> p h q", h=HG)
                 for i in range(P_SLOTS)]
        off = P_SLOTS * HG * HQ
        zt = [m.scratch[:, off + i * HQ:off + (i + 1) * HQ] for i in range(2)]
        minus_max = ctx.enter_context(nc.sbuf_tensor(f"minus_max_{layer}", [P, 2, UNITS], F32))
        max_parts = ctx.enter_context(nc.sbuf_tensor(f"max_parts_{layer}", [UNITS, 2, PARTS, P], BF16))
        max_rest = ctx.enter_context(nc.sbuf_tensor(f"max_rest_{layer}", [UNITS, P], F32))
        inverse = ctx.enter_context(nc.sbuf_tensor(f"inverse_{layer}", [P, 2, UNITS], F32))

        transforms, scaled, folded = sem("transforms"), sem("scaled"), sem("folded")
        if loads:
            cos, sin, minus_cos, w_real, w_imag, a_t, nb_t = dft_views(m)
            FOLD_BANKS = (ST_BANK, ST_BANK + 1, ST_BANK + 2)

        def fold_step(pe, k):
            which, j, i, kc = k // 8, k // 4 % 2, k // 2 % 2, k % 2
            pairs = (((w_real, cos), (w_imag, sin)), ((w_real, sin), (w_imag, minus_cos)), ((a_t, cos), (nb_t, sin)))
            left, right = pairs[which][i]
            if k == 0:
                pe.wait_ge(loads.dft, loads.n_dft)
            if k == 16:
                pe.wait_ge(scaled, 2)
            ins = pe.matmul(m.psum[:, FOLD_BANKS[which], j * D:(j + 1) * D], left[:, kc, j * P:(j + 1) * P],
                            right[:, kc, :], start=(i == 0 and kc == 0), stop=(i == 1 and kc == KC - 1))
            if k % 8 == 7:
                ins.then_inc(transforms, 1)

        def fold_copies(act):
            for i, (dst, scale) in enumerate(((a_t, 1.0 / D), (nb_t, 1.0 / D), (m.fold[:, :, :], 1.0))):
                act.wait_ge(transforms, i + 1)
                act.activation(dst, m.psum[:, FOLD_BANKS[i], :].rearrange("p (c n) -> p c n", c=KC), ACT.Copy,
                               scale=scale).then_inc(scaled if i < 2 else folded, 1)

        def items(n):
            out = []
            for s in range(KT):
                second = s < KT // 2
                half = n + 1 if second else n + 2
                if 0 <= half < HALVES:
                    out += [(s, "unit", UNITS // 2 * second + 2 * (s % (KT // 2)) + i) for i in range(2)]
                if s == 2 and 0 <= n - 1 < HALVES:
                    out.append((s, "out", None))
                if s == 5 and 0 <= n + 1 < HALVES:
                    out.append((s, "max", None))
            return out

        FIRST, LAST = -2, HALVES
        LOOP_FROM, PER = 1, 4
        LOOPS = (HALVES - 2 - LOOP_FROM) // PER
        starts, k = {}, 0
        for n in range(FIRST, LAST + 1):
            starts[n] = k
            k += len(items(n))
        FULL = len(items(LOOP_FROM))

        def start_of(J, r):
            return starts[r] if isinstance(J, int) else J * (PER * FULL) + starts[r]

        def loop(engine, period, chain=None, per_period=0):
            for n in range(FIRST, LOOP_FROM):
                period(0, n)
            before = chain.count if chain else 0
            with engine.Fori(0, LOOPS) as J:
                if chain:
                    chain.base, chain.count = J * (PER * per_period), before
                for r in range(LOOP_FROM, LOOP_FROM + PER):
                    period(J, r)
                assert not chain or chain.count == before + PER * per_period
            if chain:
                chain.base = (LOOPS - 1) * PER * per_period
            for n in range(LOOP_FROM + PER * LOOPS, LAST + 1):
                period(0, n)

        def ring(J, r):
            base = start_of(J, r)
            shape = items(r)
            return [(s, kind, unit, base + i, (starts[r] + i) % 2) for i, (s, kind, unit) in enumerate(shape)]

        def out_item(r):
            return [i for i, it in enumerate(items(r)) if it[1] == "out"][0]

        block = ctx.enter_context(nc.Block())

        @block.sync
        def _(sp):
            def period(J, r):
                n = PER * J + r
                static = isinstance(J, int)
                ge(sp, st_full, n * KT * HG)
                if r == FIRST:
                    stacks.load_k(sp, 0, 1)
                if not static or stacks.EARLY_HALVES <= n + 3 < HALVES:
                    stacks.load_q(sp, J, r + 3)
                if r % 2 == 0 and (not static or (n >= 2 and n // 2 + 1 < GROUPS)):
                    stacks.load_k(sp, J, r // 2 + 1)
                if not static or 0 <= n + 1 < HALVES:
                    nxt = (r + 1) % 2
                    sp.wait_ge(parts_ready, n + 2)
                    for s in range(PARTS):
                        dst = m.q_stack[ROWS + s:ROWS + s + 1, (r + 1) % 4, :, :]
                        sp.dma_start(dst.rearrange("o h (t q) -> o (h t) q", q=P),
                                     max_parts[:, nxt, s, :]).then_inc(max_loaded[nxt], 16)

            for i in range(2):
                sp.wait_ge(stacks.stored[i], 16 * CHUNKS)
            loop(sp, period)

        @block.gpsimd
        def _(pool):
            def v_copy(J, r):
                ge(pool, pv_done, (2 * J + r - 1) * 2 * KT)
                if shared:
                    b = (2 * J + r) // (GROUPS // B)
                    src = m.v[:, bass.ds(b * (GROUPS // B), 1), :, 0:DH].rearrange("p o t (h d) -> p (o t) h d", h=1)
                    src = src.to_broadcast([P, KT, HG, DH])
                else:
                    src = m.v[:, bass.ds(2 * J + r, 1), :, :].rearrange("p o t (h d) -> p (o t) h d", h=HG)
                pool.tensor_copy(m.v_group[:, r % 2, :, :, 0:DH], src).then_inc(v_ready, 1)

            v_copy(0, 0)
            v_copy(0, 1)
            with pool.Fori(1, GROUPS // 2) as J:
                v_copy(J, 0)
                v_copy(J, 1)
            nxt["gpsimd"](pool, "early")

        @block.tensor
        def _(pe):
            def item(J, r, kind, unit, index, slot, half_r, last_unit_in_front=False):
                ge(pe, item_done, index if kind == "max" and last_unit_in_front else index - 1)
                banks = m.psum[:, S_BANK + 2 * slot:S_BANK + 2 * slot + 2, :]
                if kind == "unit":
                    h, t = unit // QT, unit % QT
                    if unit == 0:
                        pe.wait_ge(q_loaded[half_r % 4], 96 * (J + half_r // 4 + 1))
                        pe.wait_ge(k_loaded[half_r // 2 % 2], 96 * (J + half_r // 4 + 1))
                    for kh in range(2):
                        ins = pe.matmul(banks[:, kh, :], m.q_stack[0:ROWS, half_r % 4, h, t * P:(t + 1) * P],
                                        m.k_stack[0:ROWS, half_r // 2 % 2, h, kh * 512:(kh + 1) * 512],
                                        start=True, stop=True)
                elif kind == "max":
                    ins = pe.transpose(banks[0:UNITS, 0, 0:P], minus_max[:, half_r % 2, :], m.ident[:, :])
                else:
                    pe.wait_ge(zt_ready, PER * J + r)
                    for t in range(QT):
                        ins = pe.transpose(banks[:, 0, t * P:(t + 1) * P], zt[half_r % 2][:, t * P:(t + 1) * P],
                                           m.ident[:, :])
                ins.then_inc(item_full, 1)

            def pv(J, r, s):
                n = PER * J + r
                pe.wait_ge(exp_done, n * (KT * HG) + HG * (s + 1))
                if s == 0:
                    pe.wait_ge(v_ready, n // 2 + 1 if isinstance(J, int) else 2 * J + r // 2 + 1)
                    ge(pe, zt_ready, n)
                for h in range(HG):
                    ins = pe.matmul(m.psum[h * VW:(h + 1) * VW, PV_BANK, :], m.v_group[:, r // 2 % 2, s, h, :],
                                    probs[s % P_SLOTS][:, h, :], start=(s == 0), stop=(s == KT - 1),
                                    tile_position=(0, h * VW))
                ins.then_inc(pv_done, 1)

            def st(J, r, s, h):
                n = PER * J + r
                i = s * HG + h
                if loads and r == 0 and i == 0:
                    pe.wait_ge(folded, 1)
                if i == 0:
                    pe.wait_ge(max_loaded[r % 2], 48 * (2 * J + r // 2 + 1))
                last = i - ST_BANKS if i >= ST_BANKS else {0: -2, 1: -1, 2: -3}[i]
                ge(pe, exp_done, n * (KT * HG) + last + 1)
                pe.matmul(m.psum[:, ST_BANK + i % ST_BANKS, :],
                          m.k_stack[0:ROWS + PARTS, r // 2 % 2, h, s * P:(s + 1) * P],
                          m.q_stack[0:ROWS + PARTS, r % 4, h, :], start=True, stop=True).then_inc(st_full, 1)

            def period(J, r):
                on = 0 <= r < HALVES
                todo = ring(J, r)
                for s in range(KT):
                    here = [x for x in todo if x[0] == s]
                    half_r = r + 1 if s < KT // 2 else r + 2
                    units = [x for x in here if x[1] == "unit"]
                    for pair in range(2):
                        if on:
                            st(J, r, s, 2 * pair)
                            st(J, r, s, 2 * pair + 1)
                        if units:
                            _, kind, unit, index, slot = units[pair]
                            item(J, r, kind, unit, index, slot, half_r)
                            if loads and r < 0:
                                fold_step(pe, unit if half_r == 0 else UNITS + unit)
                    if s >= 1 and on:
                        pv(J, r, s - 1)
                    if s == 0 and 0 <= r - 1 < HALVES:
                        pv(J, r - 1, KT - 1)
                    for _, kind, unit, index, slot in here:
                        if kind == "max":
                            front = todo[[x[1] for x in todo].index("max") - 1]
                            item(J, r, kind, unit, index, slot, r + 1, front[0] < KT // 2)
                        if kind == "out":
                            item(J, r, kind, unit, index, slot, r - 1)
                    if not shared and r == HALVES - 1 and s == 4:
                        assert starts[r] % 2 == 0
                        pe.wait_ge(item_done, starts[r] + 1)
                        nxt["tensor"](pe, "turn")
                    if not shared and r == HALVES - 1 and s == 6:
                        nxt["tensor"](pe, "product")

            loop(pe, period)

        @block.scalar
        def _(act):
            if loads:
                fold_copies(act)

            def take_out(J, r):
                n = PER * J + r
                act.wait_ge(pv_done, n * KT)
                if not (isinstance(J, int) and n - 3 < 0):
                    act.wait_ge(item_done, start_of(J, r) - 2 * FULL + out_item(LOOP_FROM) + 1
                                if not isinstance(J, int) else starts[n - 2] + out_item(n - 2) + 1)
                act.copy(zt[(r - 1) % 2], m.psum[:, PV_BANK, :]).then_inc(zt_ready, 1)

            def period(J, r):
                n = PER * J + r
                if not 0 <= r < HALVES:
                    if r == HALVES:
                        take_out(J, r)
                        nxt["scalar"](act, "x1")
                    return
                for s in range(KT):
                    ge(act, pv_done, n * KT + s - P_SLOTS + 1)
                    for h in range(HG):
                        i = s * HG + h
                        act.wait_ge(st_full, n * (KT * HG) + i + 1)
                        act.activation(probs[s % P_SLOTS][:, h, :], m.psum[:, ST_BANK + i % ST_BANKS, :], ACT.Exp,
                                       scale=SCALE).then_inc(exp_done, 1)
                        if s == 1 and h == 0 and r - 1 >= 0:
                            take_out(J, r)
                    if not shared and r == HALVES - 1 and s == 5:
                        nxt["scalar"](act, "turned")
                    if shared and r == HALVES - 2 and s == 3:
                        nxt["scalar"](act, "z")
                if not shared and r == HALVES - 1:
                    nxt["scalar"](act, "u")

            loop(act, period)

        @block.vector
        def _(dve):
            chain = Chain(dve, dve_steps)

            def period(J, r):
                if shared and r == HALVES - 1:
                    nxt["vector"](dve, -2)
                if not shared and r == HALVES:
                    nxt["vector"](dve, "early")
                for s, kind, unit, index, slot in ring(J, r):
                    banks = m.psum[:, S_BANK + 2 * slot:S_BANK + 2 * slot + 2, :]
                    dve.wait_ge(item_full, index + 1)
                    if kind == "unit":
                        par = (r + 1 if s < KT // 2 else r + 2) % 2
                        dve.tensor_reduce(minus_max[:, par, unit:unit + 1], banks, AX.XY, ALU.max,
                                          negate=True).then_inc(item_done, 1)
                    elif kind == "max":
                        par = (r + 1) % 2
                        n = PER * J + r
                        ge(dve, max_loaded[par], 48 * (2 * J + (r + 1) // 2))
                        row = banks[0:UNITS, 0, 0:P]
                        chain.then(dve.tensor_copy(max_parts[:, par, 0, :], row))
                        ins = dve.tensor_tensor(max_rest[:, :], row, max_parts[:, par, 0, :], ALU.subtract)
                        ins.then_inc(item_done, 1)
                        dve.wait_ge(item_done, index + 1)
                        chain.then(dve.tensor_copy(max_parts[:, par, 1, :], max_rest[:, :]))
                        dve.tensor_tensor(max_parts[:, par, 2, :], max_rest[:, :], max_parts[:, par, 1, :],
                                          ALU.subtract).then_inc(parts_ready, 1)
                    else:
                        sums = banks[:, 0, :].rearrange("p (g w) -> p g w", w=VW)
                        par = (r - 1) % 2
                        chain.then(dve.reciprocal(inverse[:, par, :], sums[:, :, DH]))
                        qh = (r - 1) % 2
                        g = 2 * J + (r - 1) // 2
                        dst = m.z[:, bass.ds(g, 1), qh * QT:(qh + 1) * QT, :].rearrange(
                            "p o t (h d) -> p (o t h) d", d=DH)
                        inv = inverse[:, par, :].rearrange("p (g o) -> p g o", o=1).to_broadcast([P, UNITS, DH])
                        dve.tensor_tensor(dst, sums[:, :, 0:DH], inv, ALU.mult).then_inc(item_done, 1)
                    if shared and r == HALVES - 3 and kind == "max":
                        nxt["vector"](dve, -3)

            loop(dve, period, chain, 3)


def mixture(nc, m, ctx):
    ZT_BANK, U_BANK, XT_BANK, GATE_BANK, E_BANK = 0, 1, 2, 3, 4
    PAIRS = TILES // 2
    SETS = EXPERTS // 2
    W = 2 * D
    NEXT_AT = {PAIRS - 2: -2, PAIRS - 1: -1}
    GATE_STEP = 16

    def sem(name):
        return ctx.enter_context(nc.semaphore(f"mix_{name}"))

    zs_ready, zt_full, zt_ready, u_full, u_ready = (
        sem("zs_ready"), sem("zt_full"), sem("zt_ready"), sem("u_full"), sem("u_ready"))
    u_stats, u_rstd, x1_stats, x1_rstd = sem("u_stats"), sem("u_rstd"), sem("x1_stats"), sem("x1_rstd")
    xln_ready, xt_full, xt_ready = sem("xln_ready"), sem("xt_full"), sem("xt_ready")
    gate_full, shifted, exps_ready, weights_ready = (
        sem("gate_full"), sem("shifted"), sem("exps_ready"), sem("weights_ready"))
    wt_full, wt_ready, bias_full, bias_ready = sem("wt_full"), sem("wt_ready"), sem("bias_full"), sem("bias_ready")
    set_full, set_read, even_added = sem("set_full"), sem("set_read"), sem("even_added")
    first_shift, first_normal, u_normal, u_added, y_normal, y_added = (
        sem("first_shift"), sem("first_normal"), sem("u_normal"), sem("u_added"), sem("y_normal"), sem("y_added"))
    y_stats, y_rstd = sem("y_stats"), sem("y_rstd")
    dve_steps, pool_steps = sem("dve_steps"), sem("pool_steps")

    def by_tile(memory, start):
        return memory[:, start * W:(start + 1) * W].rearrange("p (t d) -> p t d", t=2)

    def by_chunk(memory, start):
        return memory[:, start * W:(start + 1) * W].rearrange("p (c t q) -> p c t q", c=KC, t=2)

    free = m.v[:, :, :, :].rearrange("p g t n -> p (g t n)")
    zs, xln = [by_tile(free, 0), by_tile(free, 1)], [by_tile(free, 2), by_tile(free, 3)]
    zt = [by_chunk(free, 4), by_chunk(free, 5)]
    u, un, first_ln = (by_tile(free, i) for i in range(6, 9))
    xt = [by_chunk(m.scratch, 0), by_chunk(m.scratch, 1)]
    even, odd, y, yn = (by_tile(m.scratch, i) for i in range(2, 6))
    y_bias = [by_tile(m.scratch, 6), by_tile(m.scratch, 7)]

    def sb(name, shape, dt=F32):
        return ctx.enter_context(nc.sbuf_tensor(f"mix_{name}", shape, dt))

    bn = [sb(f"bn{i}", [P, 2, 6]) for i in range(3)]
    mv = [sb(f"mv{i}", [P, 2, 2]) for i in range(3)]
    var = [sb(f"var{i}", [P, 2]) for i in range(3)]
    rstd = [sb(f"rstd{i}", [P, 2]) for i in range(3)]
    minus_mean = [sb(f"minus_mean{i}", [P, 2]) for i in range(3)]
    shift = [sb(f"shift{i}", [P, 2]) for i in range(3)]
    logits, top_logits = sb("logits", [P, 2, GATES]), sb("top_logits", [P, 2, 8])
    exps, exps_sum, inverse = sb("exps", [P, 2, GATES]), sb("exps_sum", [P, 2]), sb("inverse", [P, 2])
    gates, top, where = sb("gates", [P, 2, GATES]), sb("top", [P, 2, 8]), sb("where", [P, 2, 8], U32)
    index, real, kept, share = (sb(name, [P, 2, 2]) for name in ("index", "real", "kept", "share"))
    total = sb("total", [P, 2])
    picks = sb("picks", [P, 2, 2, EXPERTS])
    weights = sb("weights", [P, 2, 2, EXPERTS])
    wt = by_tile(m.scratch, 8)[0:EXPERTS, :, :].rearrange("e a (t q) -> e a t q", t=2)

    dve_chain, pool_chain = Chain(nc.vector, dve_steps), Chain(nc.gpsimd, pool_steps)

    def over(ap, n):
        return ap.rearrange("p (a o) -> p a o", o=1).to_broadcast([ap.shape[0], ap.shape[1], n])

    def loop(engine, body, first, chain=None, per_pair=0):
        lead, loops = 2, (PAIRS - 6) // 2
        for p in range(first, lead):
            body(0, p)
        before = chain.count if chain else 0
        with engine.Fori(lead // 2, lead // 2 + loops) as J:
            if chain:
                chain.base, chain.count = (J - lead // 2) * (2 * per_pair), before
            body(J, 0)
            body(J, 1)
            assert not chain or chain.count == before + 2 * per_pair, (chain.count, before)
        if chain:
            chain.base = (loops - 1) * 2 * per_pair
        for p in range(lead + 2 * loops, PAIRS + 1):
            body(0, p)

    def on(J, r, by):
        return not isinstance(J, int) or 0 <= r + by < PAIRS

    def gpsimd(pool, part="rest", follow=None):
        def take_rstd(k, stats, ready, count):
            pool.wait_ge(stats, count)
            ge(pool, ready, count - 1)
            pool.tensor_tensor(minus_mean[k][:, :], mv[k][:, :, 0], m.minus_one[:, 0:2], ALU.mult)
            pool_chain.then(pool.tensor_tensor(var[k][:, :], mv[k][:, :, 1], m.eps[:, 0:2], ALU.add))
            pool_chain.then(pool.tensor_tensor(rstd[k][:, :], var[k][:, :], m.minus_half[:, 0:2], ALU.pow))
            pool.tensor_tensor(shift[k][:, :], minus_mean[k][:, :], rstd[k][:, :], ALU.mult).then_inc(ready, 1)

        def body(J, r):
            p = 2 * J + r
            if on(J, r, -1):
                take_rstd(1, y_stats, y_rstd, p)
            if on(J, r, 3):
                pair = p + 3
                b, qt = pair // (KT // 2), pair % (KT // 2) * 2
                ge(pool, zt_full, pair - 1)
                for t in range(2):
                    src = m.z[:, bass.ds(b * (GROUPS // B), GROUPS // B), bass.ds(qt + t, 1), :]
                    ins = pool.tensor_copy(zs[(r + 3) % 2][:, t, :].rearrange("p (g n) -> p g n", g=GROUPS // B),
                                           src.rearrange("p g o n -> p g (o n)"))
                ins.then_inc(zs_ready, 1)
            if on(J, r, 2):
                take_rstd(0, u_stats, u_rstd, p + 3)
                take_rstd(2, x1_stats, x1_rstd, p + 3)
            if on(J, r, -1):
                pool.wait_ge(y_normal, p)
                last = m.x[:, bass.ds(2 * (p - 1), 2), :]
                pool.tensor_tensor(last, last, yn, ALU.add).then_inc(y_added, 1)
            if isinstance(J, int) and p in NEXT_AT:
                follow["gpsimd"](pool, NEXT_AT[p])

        if part == "early":
            body(0, -3)
            body(0, -2)
        else:
            loop(pool, body, -1, pool_chain, 6)

    def tensor(pe, part="rest"):
        def experts(p, par, t, sets):
            for s in sets:
                use = 2 * SETS * p + SETS * t + s
                ge(pe, set_read, use - SETS + 1)
                for half in range(2):
                    for k in range(KC):
                        ins = pe.matmul(m.psum[:, E_BANK + s, half * D:(half + 1) * D], xt[par][:, k, t, :],
                                        m.expert_w[:, k, 2 * s + half, :], start=(k == 0), stop=(k == KC - 1))
                ins.then_inc(set_full, 1)

        def turn(bank, src):
            for k in range(KC):
                for t in range(2):
                    ins = pe.transpose(m.psum[:, bank, (2 * k + t) * P:(2 * k + t + 1) * P],
                                       src[:, t, k * P:(k + 1) * P], m.ident[:, :])
            return ins

        def turn_z(p, par):
            pe.wait_ge(zs_ready, p + 3)
            ge(pe, zt_ready, p + 2)
            turn(ZT_BANK, zs[par]).then_inc(zt_full, 1)

        def product_u(p, par):
            pe.wait_ge(zt_ready, p + 3)
            ge(pe, u_ready, p + 2)
            for t in range(2):
                for k in range(KC):
                    ins = pe.matmul(m.psum[:, U_BANK, t * D:(t + 1) * D], zt[par][:, k, t, :], m.wout[:, k, :],
                                    start=(k == 0), stop=(k == KC - 1))
            ins.then_inc(u_full, 1)

        def body(J, r):
            p, par, nxt = 2 * J + r, r % 2, (r + 1) % 2
            if on(J, r, 2):
                turn_z(p, par)
            first = isinstance(J, int) and p == 0
            if on(J, r, 0) and not first:
                experts(p, par, 0, range(0, 1))
            if on(J, r, 1):
                pe.wait_ge(xln_ready, p + 2)
                ge(pe, bias_ready, p + 1)
                turn(XT_BANK, xln[nxt]).then_inc(xt_full, 1)
            if on(J, r, 2):
                product_u(p, par)
            if on(J, r, 0) and not first:
                experts(p, par, 0, range(1, 2))
            if on(J, r, 1):
                pe.wait_ge(xt_ready, p + 2)
                ge(pe, wt_ready, p + 1)
                for t in range(2):
                    for k in range(KC):
                        ins = pe.matmul(m.psum[:, GATE_BANK, t * GATE_STEP:t * GATE_STEP + GATES],
                                        xt[nxt][:, k, t, :], m.gate_w[:, k, :], start=(k == 0), stop=(k == KC - 1))
                ins.then_inc(gate_full, 1)
            if on(J, r, 0):
                if not first:
                    experts(p, par, 0, range(2, SETS))
                experts(p, par, 1, range(0, 2))
            if isinstance(J, int) and p == -1:
                experts(0, 0, 0, range(0, SETS))
            if on(J, r, 1):
                pe.wait_ge(weights_ready, p + 2)
                for t in range(2):
                    ins = pe.transpose(m.psum[0:EXPERTS, GATE_BANK, (1 + t) * P:(2 + t) * P], weights[:, nxt, t, :],
                                       m.ident[:, :])
                ins.then_inc(wt_full, 1)
            if on(J, r, 0):
                experts(p, par, 1, range(2, 3))
            if on(J, r, 1):
                pe.wait_ge(wt_ready, p + 2)
                for t in range(2):
                    ins = pe.matmul(m.psum[:, XT_BANK, t * D:(t + 1) * D], wt[:, nxt, t, :], m.expert_b[:, :],
                                    start=True, stop=True)
                ins.then_inc(bias_full, 1)
            if on(J, r, 0):
                experts(p, par, 1, range(3, SETS))

        if part == "turn":
            turn_z(-2, 0)
        elif part == "product":
            product_u(-2, 0)
        else:
            loop(pe, body, -1)

    def scalar(act, part="rest"):
        def flat(ap):
            return ap.rearrange("p a b c -> p (a b c)") if len(ap.shape) == 4 else ap.rearrange("p a b -> p (a b)")

        def normalise(k, out, src):
            for t in range(2):
                ins = act.activation(out[:, t, :], src(t), ACT.Identity, scale=rstd[k][:, t:t + 1],
                                     bias=shift[k][:, t:t + 1])
            return ins

        def x_tile(tile):
            return m.x[:, bass.ds(tile, 1), :].rearrange("p o d -> p (o d)")

        def first_norm(p):
            ge_bare(act, u_ready, p + 2)
            for t in range(2):
                tile = 2 * p + 4 + t
                ins = act.activation(first_ln[:, t, :], x_tile(tile), ACT.Identity,
                                     scale=m.rstd[:, bass.ds(tile, 1)], bias=m.mean[:, bass.ds(tile, 1)])
            ins.then_inc(first_normal, 1)

        def copy_zt(p, par):
            act.wait_ge(zt_full, p + 3)
            ge(act, u_full, p + 1)
            act.copy(flat(zt[par]), m.psum[:, ZT_BANK, :]).then_inc(zt_ready, 1)

        def u_norm(p):
            act.wait_ge(u_rstd, p + 3)
            ge(act, u_added, p + 2)
            normalise(0, un, lambda t: u[:, t, :]).then_inc(u_normal, 1)

        def x1_norm(p, par):
            ge_bare(act, x1_rstd, p + 3)
            ge(act, xt_full, p + 1)
            normalise(2, xln[par], lambda t: x_tile(2 * p + 4 + t)).then_inc(xln_ready, 1)

        def body(J, r):
            p, par, nxt = 2 * J + r, r % 2, (r + 1) % 2
            if on(J, r, 2):
                first_norm(p)
            if on(J, r, 2):
                copy_zt(p, par)
            if on(J, r, 1):
                act.wait_ge(xt_full, p + 2)
                ge(act, set_full, 2 * SETS * p)
                act.copy(flat(xt[nxt]), m.psum[:, XT_BANK, :]).then_inc(xt_ready, 1)
            if on(J, r, -1):
                act.wait_ge(y_rstd, p)
                ge(act, y_added, p - 1)
                normalise(1, yn, lambda t: y[:, t, :]).then_inc(y_normal, 1)
            if on(J, r, 1):
                act.wait_ge(shifted, p + 2)
                act.activation(exps[:, :, :], logits[:, :, :], ACT.Exp).then_inc(exps_ready, 1)
            if on(J, r, 2):
                u_norm(p)
            if on(J, r, 1):
                act.wait_ge(wt_full, p + 2)
                ge(act, bias_full, p)
                act.copy(wt[:, nxt, :, :].rearrange("e t q -> e (t q)"),
                         m.psum[0:EXPERTS, GATE_BANK, P:3 * P]).then_inc(wt_ready, 1)
                act.wait_ge(bias_full, p + 2)
                ge(act, set_read, 2 * SETS * p)
                act.copy(flat(y_bias[nxt]), m.psum[:, XT_BANK, :]).then_inc(bias_ready, 1)
            if on(J, r, 2):
                x1_norm(p, par)

        if part == "turned":
            act.wait_ge(first_shift, 1)
            first_norm(-2)
            copy_zt(-2, 0)
        elif part == "u":
            u_norm(-2)
        elif part == "x1":
            x1_norm(-2, 0)
        else:
            loop(act, body, -1)

    def vector(dve, part="rest", follow=None):
        step = dve_chain.then

        def x_pair(pair):
            return m.x[:, bass.ds(2 * pair, 2), :]

        def statistics(k, src, done):
            dve.bn_stats(bn[k][:, 0, :], src(0))
            step(dve.bn_stats(bn[k][:, 1, :], src(1)), bare=True)
            dve.bn_aggr(mv[k][:, 0, :], bn[k][:, 0, :])
            dve.bn_aggr(mv[k][:, 1, :], bn[k][:, 1, :]).then_inc(done, 1)

        def gate_logits(p):
            dve.wait_ge(gate_full, p + 2)
            new = m.psum[:, GATE_BANK, 0:2 * GATE_STEP].rearrange("p (t n) -> p t n", t=2)[:, :, 0:GATES]
            gate_b = m.gate_b[:, :].rearrange("p (o n) -> p o n", o=1).to_broadcast([P, 2, GATES])
            step(dve.tensor_tensor(logits[:, :, :], new, gate_b, ALU.add), bare=True)
            dve.max(top_logits[:, 0, :], logits[:, 0, :])
            step(dve.max(top_logits[:, 1, :], logits[:, 1, :]))
            dve.tensor_tensor(logits[:, :, :], logits[:, :, :], over(top_logits[:, :, 0], GATES),
                              ALU.subtract).then_inc(shifted, 1)

        def gate_weights(p, nxt):
            dve.wait_ge(exps_ready, p + 2)
            step(dve.tensor_reduce(exps_sum[:, :], exps[:, :, :], AX.X, ALU.add))
            step(dve.reciprocal(inverse[:, :], exps_sum[:, :]))
            step(dve.tensor_tensor(gates[:, :, :], exps[:, :, :], over(inverse[:, :], GATES), ALU.mult), bare=True)
            dve.max(top[:, 0, :], gates[:, 0, :])
            step(dve.max(top[:, 1, :], gates[:, 1, :]), bare=True)
            dve.max_index(where[:, 0, :], top[:, 0, :], gates[:, 0, :])
            step(dve.max_index(where[:, 1, :], top[:, 1, :], gates[:, 1, :]))
            step(dve.tensor_copy(index[:, :, :], where[:, :, 0:2]))
            step(dve.tensor_scalar(real[:, :, :], index[:, :, :], float(EXPERTS), None, ALU.is_lt))
            step(dve.tensor_tensor(kept[:, :, :], top[:, :, 0:2], real[:, :, :], ALU.mult))
            step(dve.tensor_reduce(total[:, :], kept[:, :, :], AX.X, ALU.add))
            step(dve.scalar_tensor_tensor(out=total[:, :], in0=total[:, :], scalar=0.0, in1=total[:, :],
                                          op0=ALU.is_equal, op1=ALU.add))
            step(dve.reciprocal(inverse[:, :], total[:, :]))
            step(dve.tensor_tensor(share[:, :, :], kept[:, :, :], over(inverse[:, :], 2), ALU.mult))
            picks_flat = picks[:, :, :, :].rearrange("p t j e -> p (t j) e")
            experts = m.index[:, :].rearrange("p (o e) -> p o e", o=1).to_broadcast([P, 4, EXPERTS])
            step(dve.tensor_tensor(picks_flat, experts, over(index[:, :, :].rearrange("p t j -> p (t j)"), EXPERTS),
                                   ALU.is_equal))
            step(dve.tensor_tensor(picks_flat, picks_flat, over(share[:, :, :].rearrange("p t j -> p (t j)"), EXPERTS),
                                   ALU.mult))
            dve.tensor_tensor(weights[:, nxt, :, :], picks[:, :, 0, :], picks[:, :, 1, :],
                              ALU.add).then_inc(weights_ready, 1)

        def add_experts(p, par, t, sets):
            for s in sets:
                use = 2 * SETS * p + SETS * t + s
                if s == 0 and t == 0:
                    dve.wait_ge(weights_ready, p + 1)
                    dve.wait_ge(bias_ready, p + 1)
                    ge(dve, y_stats, p)
                dve.wait_ge(set_full, use + 1)
                bank = m.psum[:, E_BANK + s, :]
                if s > 0:
                    dve.wait_ge(even_added, use)
                start = y_bias[par] if s == 0 else even
                dve.scalar_tensor_tensor(out=even[:, t, :], in0=bank[:, 0:D], scalar=weights[:, par, t, 2 * s:2 * s + 1],
                                         in1=start[:, t, :], op0=ALU.mult, op1=ALU.add).then_inc(even_added, 1)
                w = weights[:, par, t, 2 * s + 1:2 * s + 2]
                if s == 0:
                    ins = dve.tensor_scalar(odd[:, t, :], bank[:, D:], w, None, ALU.mult)
                else:
                    dve.wait_ge(set_read, use)
                    ins = dve.scalar_tensor_tensor(out=odd[:, t, :], in0=bank[:, D:], scalar=w, in1=odd[:, t, :],
                                                   op0=ALU.mult, op1=ALU.add)
                ins.then_inc(set_read, 1)

        def body(J, r):
            p, par, nxt = 2 * J + r, r % 2, (r + 1) % 2
            now, ahead = on(J, r, 0), on(J, r, 2)
            if isinstance(J, int) and p in NEXT_AT:
                follow["vector"](dve, NEXT_AT[p])
            if now:
                add_experts(p, par, 0, range(0, 1))
            if ahead:
                dve.wait_ge(first_normal, p + 3)
                dve.wait_ge(u_full, p + 3)
                new = m.psum[:, U_BANK, :].rearrange("p (t d) -> p t d", t=2)
                dve.tensor_tensor(u, new, first_ln, ALU.add).then_inc(u_ready, 1)
                ge_bare(dve, u_ready, p + 3)
                statistics(0, lambda t: u[:, t, :], u_stats)
            if now:
                add_experts(p, par, 0, range(1, 2))
            if on(J, r, 1):
                gate_logits(p)
            if now:
                add_experts(p, par, 0, range(2, 3))
            if on(J, r, 1):
                gate_weights(p, nxt)
            if ahead:
                dve.wait_ge(u_normal, p + 3)
                dve.tensor_tensor(x_pair(p + 2), x_pair(p + 2), un, ALU.add).then_inc(u_added, 1)
                ge_bare(dve, u_added, p + 3)
                statistics(2, lambda t: m.x[:, bass.ds(2 * p + 4 + t, 1), :], x1_stats)
            if now:
                add_experts(p, par, 0, range(3, SETS))
            if now:
                add_experts(p, par, 1, range(0, 2))
            if now:
                add_experts(p, par, 1, range(2, SETS))
                dve.wait_ge(set_read, 2 * SETS * (p + 1))
                dve.wait_ge(even_added, 2 * SETS * (p + 1))
                ge(dve, y_normal, p)
                step(dve.tensor_tensor(y, even, odd, ALU.add), bare=True)
                statistics(1, lambda t: y[:, t, :], y_stats)

        if part == "early":
            dve.scalar_tensor_tensor(out=m.mean[:, :], in0=m.mean[:, :], scalar=-1.0, in1=m.rstd[:, :],
                                     op0=ALU.mult, op1=ALU.mult).then_inc(first_shift, 1)
            body(0, -2)
        else:
            loop(dve, body, -1, dve_chain, 20)

    def run(follow):
        with nc.Block() as block:
            @block.gpsimd
            def _(pool):
                gpsimd(pool, follow=follow)

            @block.tensor
            def _(pe):
                tensor(pe)

            @block.scalar
            def _(act):
                scalar(act)

            @block.vector
            def _(dve):
                vector(dve, follow=follow)

    return {"gpsimd": gpsimd, "tensor": tensor, "scalar": scalar, "vector": vector, "run": run}


def spectral(nc, m, ctx, out):
    XT_BANK, Y_BANK = 0, 4

    def sem(name):
        return ctx.enter_context(nc.semaphore(f"spec_{name}"))

    z_stats, z_rstd, x_stats, x_rstd, y_stats, y_rstd = (
        sem("z_stats"), sem("z_rstd"), sem("x_stats"), sem("x_rstd"), sem("y_stats"), sem("y_rstd"))
    z_normal, x_added, xln_ready, xt_full, xt_ready, y_full, y_normal = (
        sem("z_normal"), sem("x_added"), sem("xln_ready"), sem("xt_full"), sem("xt_ready"), sem("y_full"),
        sem("y_normal"))
    res_ready = sem("res_ready")
    stored = sem("stored")
    dve_steps, pool_steps = sem("dve_steps"), sem("pool_steps")
    W = CHUNK * D

    def tiles(memory, i):
        return memory[:, i * W:(i + 1) * W].rearrange("p (t d) -> p t d", t=CHUNK)

    free = m.v[:, :, :, :].rearrange("p g t n -> p (g t n)")
    xln, zn = tiles(free, 0), tiles(free, 1)
    yn = [tiles(m.scratch, 0), tiles(m.scratch, 1)]
    xt = [m.scratch[:, (2 + i) * W:(3 + i) * W].rearrange("p (c t) -> p c t", c=KC) for i in range(2)]

    def sb(name, shape):
        return ctx.enter_context(nc.sbuf_tensor(f"spec_{name}", shape, F32))

    bn = [sb(f"bn{i}", [P, CHUNK, 6]) for i in range(3)]
    mv = [sb(f"mv{i}", [P, 2, CHUNK, 2]) for i in range(3)]
    var = [sb(f"var{i}", [P, CHUNK]) for i in range(3)]
    minus_mean = [sb(f"minus_mean{i}", [P, CHUNK]) for i in range(3)]
    rstd = [sb(f"rstd{i}", [P, 2, CHUNK]) for i in range(3)]
    shift = [sb(f"shift{i}", [P, 2, CHUNK]) for i in range(3)]
    LAST = CHUNKS
    dve_chain, pool_chain = Chain(nc.vector, dve_steps), Chain(nc.gpsimd, pool_steps)

    def is_last(J, u):
        return isinstance(J, int) and 2 * J + u == LAST

    def gpsimd(pool, part="rest"):
        def take_rstd(k, par, stats, ready, count):
            pool.wait_ge(stats, count)
            if isinstance(count, int):
                ge(pool, ready, count - 1)
            pool.tensor_tensor(minus_mean[k][:, :], mv[k][:, par, :, 0], m.minus_one[:, :], ALU.mult)
            pool_chain.then(pool.tensor_tensor(var[k][:, :], mv[k][:, par, :, 1], m.eps[:, :], ALU.add))
            pool_chain.then(pool.tensor_tensor(rstd[k][:, par, :], var[k][:, :], m.minus_half[:, :], ALU.pow))
            pool.tensor_tensor(shift[k][:, par, :], minus_mean[k][:, :], rstd[k][:, par, :],
                               ALU.mult).then_inc(ready, 1)

        def body(J, u):
            c = 2 * J + u
            if on(J, u, -1):
                take_rstd(2, (u + 1) % 2, y_stats, y_rstd, c)
            if on(J, u, 3):
                take_rstd(0, (u + 1) % 2, z_stats, z_rstd, c + 4)
            if on(J, u, 2):
                take_rstd(1, u % 2, x_stats, x_rstd, c + 3)
            if on(J, u, -1) and not is_last(J, u):
                old = (u + 1) % 2
                pool.wait_ge(y_normal, c)
                x_chunk = m.x[:, bass.ds((c - 1) * CHUNK, CHUNK), :]
                pool.tensor_tensor(x_chunk, x_chunk, yn[old], ALU.add).then_inc(res_ready, 1)

        if part == "early":
            body(0, -3)
            body(0, -2)
        else:
            chunk_loop(pool, body, -1, LAST, pool_chain, 6)

    def tensor(pe, part="rest"):
        def body(J, u):
            c = 2 * J + u
            def product(t):
                dst = m.psum[:, Y_BANK + 2 * (u % 2) + t // 2, (t % 2) * D:(t % 2 + 1) * D]
                for k in range(KC):
                    pe.matmul(dst, xt[u % 2][:, k, t * P:(t + 1) * P], m.fold[:, k, :],
                              start=(k == 0), stop=False)
                return pe.matmul(dst, m.ones[:, :], m.bias[:, :], start=False, stop=True)

            if on(J, u):
                pe.wait_ge(xt_ready, c + 1)
                for t in range(CHUNK - 1):
                    product(t)
            if on(J, u, 1):
                pe.wait_ge(xln_ready, c + 2)
                ge(pe, xt_ready, c + 1)
                for t in range(CHUNK):
                    for k in range(KC):
                        ins = pe.transpose(m.psum[:, XT_BANK + k, t * P:(t + 1) * P],
                                           xln[:, t, k * P:(k + 1) * P], m.ident[:, :])
                ins.then_inc(xt_full, 1)
            if on(J, u):
                product(CHUNK - 1).then_inc(y_full, 1)

        chunk_loop(pe, body, -1, LAST)

    def scalar(act, part="rest"):
        def normalise(k, par, out, src):
            for t in range(CHUNK):
                ins = act.activation(out(t), src(t), ACT.Identity, scale=rstd[k][:, par, t:t + 1],
                                     bias=shift[k][:, par, t:t + 1])
            return ins

        def by_group(ap):
            return ap.rearrange("p (g n) -> p g n", g=GROUPS // B)

        def z_norm(J, u):
            c = 2 * J + u
            if on(J, u, 2):
                b, qt = J + (u + 2) // 2, u % 2 * CHUNK
                act.wait_ge(z_rstd, c + 3)
                ge(act, x_added, c + 2)
                normalise(0, u % 2, lambda t: by_group(zn[:, t, :]),
                          lambda t: m.z[:, bass.ds(b * (GROUPS // B), GROUPS // B), qt + t, :]
                          ).then_inc(z_normal, 1)

        def x_norm(J, u):
            c = 2 * J + u
            if on(J, u, 1):
                act.wait_ge(x_rstd, c + 2)
                ge(act, xt_full, c + 1)
                normalise(1, (u + 1) % 2, lambda t: xln[:, t, :],
                          lambda t: m.x[:, bass.ds((c + 1) * CHUNK + t, 1), :].rearrange("p o d -> p (o d)")
                          ).then_inc(xln_ready, 1)

        def copy_xt(J, u):
            c = 2 * J + u
            if on(J, u, 1):
                act.wait_ge(xt_full, c + 2)
                ge(act, y_full, c)
                act.copy(xt[(u + 1) % 2], m.psum[:, XT_BANK:XT_BANK + 2, :]).then_inc(xt_ready, 1)

        def body(J, u):
            c = 2 * J + u
            z_norm(J, u)
            x_norm(J, u)
            if on(J, u, -1):
                old = (u + 1) % 2
                act.wait_ge(y_rstd, c)
                bank = Y_BANK + 2 * old
                normalise(2, old, lambda t: yn[old][:, t, :],
                          lambda t: m.psum[:, bank + t // 2, (t % 2) * D:(t % 2 + 1) * D]).then_inc(y_normal, 1)
            copy_xt(J, u)

        if part == "rest":
            z_norm(0, -1)
            copy_xt(0, -1)
            chunk_loop(act, body, 0, LAST)
        elif part == "z":
            z_norm(0, -2)
        else:
            x_norm(0, -1)

    def vector(dve, part="rest"):
        def statistics(k, par, src, done):
            for t in range(CHUNK):
                ins = dve.bn_stats(bn[k][:, t, :], src(t))
            dve_chain.then(ins, bare=True)
            for t in range(CHUNK):
                ins = dve.bn_aggr(mv[k][:, par, t, :], bn[k][:, t, :])
            ins.then_inc(done, 1)

        def body(J, u):
            c = 2 * J + u
            if on(J, u, -1):
                old = (u + 1) % 2
                bank = Y_BANK + 2 * old
                if not on(J, u, 2):
                    ge(dve, y_stats, c - 1)
                ge_bare(dve, y_full, c)
                statistics(2, old, lambda t: m.psum[:, bank + t // 2, (t % 2) * D:(t % 2 + 1) * D], y_stats)
            if on(J, u, 3):
                b, qt = J + (u + 3) // 2, (u + 3) % 2 * CHUNK
                statistics(0, (u + 1) % 2,
                           lambda t: m.z[:, bass.ds(b * (GROUPS // B), GROUPS // B), qt + t, :], z_stats)
            if on(J, u, 2):
                dve.wait_ge(z_normal, c + 3)
                x_chunk = m.x[:, bass.ds((c + 2) * CHUNK, CHUNK), :]
                dve.tensor_tensor(x_chunk, x_chunk, zn, ALU.add).then_inc(x_added, 1)
                ge_bare(dve, x_added, c + 3)
                statistics(1, u % 2, lambda t: m.x[:, bass.ds((c + 2) * CHUNK + t, 1), :], x_stats)
            if is_last(J, u):
                old = (u + 1) % 2
                dve.wait_ge(y_normal, c)
                x_chunk = m.x[:, (c - 1) * CHUNK:c * CHUNK, :]
                dve.tensor_tensor(x_chunk, x_chunk, yn[old], ALU.add).then_inc(res_ready, 1)

        if part == "rest":
            chunk_loop(dve, body, -1, LAST, dve_chain, 3)
        else:
            body(0, part)

    def sync(sp, part="rest"):
        out_view = out.rearrange("(c t p) d -> c p t d", p=P, t=CHUNK)

        def body(J, u):
            if not on(J, u, -1):
                return
            c = 2 * J + u
            sp.wait_ge(res_ready, c)
            sp.dma_start(out_view[bass.ds(c - 1, 1), :, :, :].rearrange("o p t d -> p (o t) d"),
                         m.x[:, bass.ds((c - 1) * CHUNK, CHUNK), :]).then_inc(stored, 16)

        chunk_loop(sp, body, 0, LAST)
        sp.wait_ge(stored, 16 * CHUNKS)

    def run():
        with nc.Block() as block:
            @block.gpsimd
            def _(pool):
                gpsimd(pool)

            @block.tensor
            def _(pe):
                tensor(pe)

            @block.scalar
            def _(act):
                scalar(act)

            @block.vector
            def _(dve):
                vector(dve)

            @block.sync
            def _(sp):
                sync(sp)

    return {"gpsimd": gpsimd, "scalar": scalar, "vector": vector, "run": run}


def build(nc, io, out):
    q_dram = [nc.dram_tensor(f"q_parts{i}", [B, PARTS, D, S], BF16).ap() for i in range(2)]
    k_dram = [nc.dram_tensor("k_parts0", [B, PARTS, D, S], BF16).ap(),
              nc.dram_tensor("k_parts1", [B, PARTS, DH, S], BF16).ap()]
    with ExitStack() as ctx:
        m = Memory(nc, ctx)
        loads = Loads(nc, ctx)
        stacks = [Stacks(nc, ctx, m, layer, q_dram[layer], k_dram[layer]) for layer in range(2)]
        setup(nc, m, io, loads)
        with ExitStack() as phase_ctx:
            projection(nc, m, phase_ctx, 0, stacks[0], io, loads)["run"]()
        with ExitStack() as phase_ctx:
            experts = mixture(nc, m, phase_ctx)
            attention(nc, m, 0, stacks[0], experts, loads)
            second = projection(nc, m, phase_ctx, 1, stacks[1], io)
            experts["run"](second)
            second["run"]()
        with ExitStack() as phase_ctx:
            last = spectral(nc, m, phase_ctx, out)
            attention(nc, m, 1, stacks[1], last)
            last["run"]()


def constants():
    n = np.arange(D)
    angle = 2.0 * np.pi * (np.outer(n, n) % D) / D
    return {
        "dft_cos": np.cos(angle).astype(np.float32),
        "dft_sin": np.sin(angle).astype(np.float32),
        "dft_minus_cos": (-np.cos(angle)).astype(np.float32),
        "ident": np.eye(P, dtype=np.float32),
        "index": np.broadcast_to(np.arange(EXPERTS, dtype=np.float32), (P, EXPERTS)).copy(),
    }


def kernel(L0_attn_x, L0_attn_mask, L0_attn_Wq, L0_attn_Wk, L0_attn_Wv, L0_attn_Wout, L0_ffn_gate_w, L0_ffn_gate_b,
           L0_ffn_expert_w, L0_ffn_expert_b, L1_attn_Wq, L1_attn_Wk, L1_attn_Wv, L1_ffn_w_freq_real,
           L1_ffn_w_freq_imag, L1_ffn_bias):
    import concourse.bacc as bacc
    from concourse.bass_utils import run_bass_kernel_spmd

    arrays = {
        "x": np.reshape(L0_attn_x, (B * S, D)),
        "wq0": L0_attn_Wq, "wk0": L0_attn_Wk, "wv0": L0_attn_Wv, "wout": L0_attn_Wout,
        "gate_w": np.transpose(L0_ffn_gate_w), "gate_b": np.broadcast_to(L0_ffn_gate_b, (P, GATES)),
        "expert_w": L0_ffn_expert_w, "expert_b": L0_ffn_expert_b,
        "wq1": np.transpose(L1_attn_Wq), "wk1": np.transpose(L1_attn_Wk), "wv1": np.transpose(L1_attn_Wv),
        "w_real": L1_ffn_w_freq_real, "w_imag": L1_ffn_w_freq_imag,
        "bias": np.reshape(L1_ffn_bias, (1, D)),
    }
    arrays.update(constants())
    nc = bacc.Bacc("TRN2", target_bir_lowering=False, num_devices=1)
    feed, io = {}, {}
    for name, a in arrays.items():
        a = np.ascontiguousarray(a)
        feed[f"in_{name}"] = a
        io[name] = nc.dram_tensor(f"in_{name}", a.shape, mybir.dt.from_np(a.dtype), kind="ExternalInput").ap()
    out = nc.dram_tensor("out", (B * S, D), F32, kind="ExternalOutput").ap()
    build(nc, io, out)
    result = run_bass_kernel_spmd(nc, [feed], core_ids=[0])
    return np.reshape(result.results[0]["out"], (B, S, D))
```
